# Optimizing a Trainium2 kernel written in Bass

```python
import numpy as np
import jax
import jax.numpy as jnp

def _softmax(x, axis=-1):
    return jax.nn.softmax(x, axis=axis)

def _gelu(x):
    return jax.nn.gelu(x, approximate=True)

def _silu(x):
    return jax.nn.silu(x)

def _sigmoid(x):
    return jax.nn.sigmoid(x)

def _layernorm(x, axis=-1, eps=1e-05):
    m = jnp.mean(x, axis=axis, keepdims=True)
    v = jnp.var(x, axis=axis, keepdims=True)
    return (x - m) / jnp.sqrt(v + eps)

def _scatter_add(tgt, idx, src, axis=0):
    return tgt.at[idx].add(src)

def _segment_sum(src, seg, n):
    return jax.ops.segment_sum(src, seg, n)
kernel_name = 'mk_gnn_ffn_d2_gnn_r8_a670ac'

def setup_inputs(seed: int=0):
    np.random.seed(seed)
    _w = jnp.asarray

    def _rec_inputs():
        import jax
        import jax.numpy as jnp
        _gk = jax.random.key(seed)
        x = -0.0002117 + 1 * jax.random.normal(jax.random.fold_in(_gk, 1), (1250, 512), jnp.float32)
        src = jax.random.randint(jax.random.fold_in(_gk, 2), (20000,), 0, 1250, jnp.int32)
        dst = jnp.minimum((1250 * jax.random.uniform(jax.random.fold_in(_gk, 3), (20000,)) ** 2.0).astype(jnp.int32), 9999)
        _o = jnp.argsort(dst, stable=True)
        src = src[_o]
        dst = dst[_o]
        return (x, src, dst)
    x, src, dst = _rec_inputs()

    def _L0_gnn_setup():
        import jax, jax.numpy as jnp
        import numpy as np
        BN_EPS = 1e-05
        key = jax.random.key(seed)
        ks = jax.random.split(key, 6)
        N, F, H, E = (6250, 512, 512, 20000)
        x = jax.random.normal(ks[0], (N, F), dtype=jnp.float32)
        edge_index = jax.random.randint(ks[1], (2, E), 0, N, dtype=jnp.int64)
        adj_norm_sp = jnp.zeros((1,), dtype=jnp.float32)
        W = jax.random.normal(ks[2], (H, F), dtype=jnp.float32) * (1.0 / np.sqrt(F))
        b = jax.random.normal(ks[3], (H,), dtype=jnp.float32) * 0.01
        gamma = jax.random.uniform(ks[4], (H,), dtype=jnp.float32)
        beta = jax.random.normal(ks[5], (H,), dtype=jnp.float32) * 0.01
        return {'x': x, 'edge_index': edge_index, 'adj_norm_sp': adj_norm_sp, 'W': W, 'b': b, 'gamma': gamma, 'beta': beta}
    _L0_gnn_all = _L0_gnn_setup()
    _L0_gnn_in = {k: v for k, v in _L0_gnn_all.items() if k in ('adj_norm_sp', 'W', 'b', 'gamma', 'beta')}
    del _L0_gnn_all

    def _L0_ffn_setup():
        import jax, jax.numpy as jnp
        import numpy as np
        B, S, D = (16, 1024, 512)
        H = 256
        E = 16
        TOP_K = 4
        key = jax.random.key(seed)
        ks = jax.random.split(key, 8)
        scale = 0.02
        x = jax.random.normal(ks[0], (B, S, D), dtype=jnp.float32)
        router_w = jax.random.normal(ks[1], (D, E), dtype=jnp.float32) * scale
        router_b = jax.random.normal(ks[2], (E,), dtype=jnp.float32) * scale
        w1 = jax.random.normal(ks[3], (E, D, H), dtype=jnp.float32) * scale
        b1 = jax.random.normal(ks[4], (E, H), dtype=jnp.float32) * scale
        w2 = jax.random.normal(ks[5], (E, H, D), dtype=jnp.float32) * scale
        b2 = jax.random.normal(ks[6], (E, D), dtype=jnp.float32) * scale
        return {'x': x, 'router_w': router_w, 'router_b': router_b, 'w1': w1, 'b1': b1, 'w2': w2, 'b2': b2}
    _L0_ffn_all = _L0_ffn_setup()
    _L0_ffn_in = {k: v for k, v in _L0_ffn_all.items() if k in ('router_w', 'router_b', 'w1', 'b1', 'w2', 'b2')}
    del _L0_ffn_all

    def _L1_gnn_setup():
        import jax, jax.numpy as jnp
        import numpy as np
        from math import sqrt
        N = 6250
        E = 100000
        D_EMB = 512
        DK = 64
        DV = 64
        HEADS = 8

        def _attention_message(Q, K, V, senders, receivers, n_nodes):
            scale = 1.0 / sqrt(Q.shape[-1])
            scores = jnp.einsum('ehd,ehd->eh', Q[receivers], K[senders]) * scale
            smax = jax.ops.segment_max(scores, receivers, num_segments=n_nodes)
            ex = jnp.exp(scores - smax[receivers])
            denom = jax.ops.segment_sum(ex, receivers, num_segments=n_nodes)
            att = ex / denom[receivers]
            out = jax.ops.segment_sum(att[:, :, None] * V[senders], receivers, num_segments=n_nodes)
            return (out, att)
        key = jax.random.key(seed)
        k1, k2, k3, k4 = jax.random.split(key, 4)
        x = jax.random.normal(k1, (N, D_EMB), dtype=jnp.float32)
        edge_index = jax.random.randint(k2, (2, E), 0, N, dtype=jnp.int64)
        out_qkv = (2 * DK + DV) * HEADS
        W_qkv = jax.random.normal(k3, (out_qkv, D_EMB), dtype=jnp.float32) / sqrt(D_EMB)
        b_qkv = jnp.zeros((out_qkv,), dtype=jnp.float32)
        W_ff = jax.random.normal(k4, (D_EMB, DV * HEADS), dtype=jnp.float32) / sqrt(DV * HEADS)
        b_ff = jnp.zeros((D_EMB,), dtype=jnp.float32)
        return {'x': x, 'edge_index': edge_index, 'W_qkv': W_qkv, 'b_qkv': b_qkv, 'W_ff': W_ff, 'b_ff': b_ff}
    _L1_gnn_all = _L1_gnn_setup()
    _L1_gnn_in = {k: v for k, v in _L1_gnn_all.items() if k in ('W_qkv', 'b_qkv', 'W_ff', 'b_ff')}
    del _L1_gnn_all

    def _L1_ffn_setup():
        import jax, jax.numpy as jnp
        import numpy as np
        B, T, C = (8, 1024, 512)
        H = 1024
        G, EG = (2, 4)
        E = G * EG
        K = 2
        LN_EPS = 1e-05

        def _swiglu(x):
            a, b = jnp.split(x, 2, axis=-1)
            return jax.nn.silu(a) * b
        key = jax.random.key(seed)
        ks = jax.random.split(key, 8)
        n = lambda k, shape, s: jax.random.normal(k, shape, dtype=jnp.float32) * s
        return {'x': n(ks[0], (B, T, C), 1.0), 'ln_scale': jnp.ones((C,), jnp.float32), 'ln_bias': jnp.zeros((C,), jnp.float32), 'shared_in_w': n(ks[1], (2 * H, C), 0.02), 'shared_out_w': n(ks[2], (C, H), 0.02), 'shared_out_b': jnp.zeros((C,), jnp.float32), 'expert_in_w': n(ks[3], (2 * H, C), 0.02), 'expert_out_weight': n(ks[4], (E, C, H), 0.02), 'expert_out_bias': jnp.zeros((E, C), jnp.float32), 'group_gate_w': n(ks[5], (G, C), 0.02), 'expert_gate_w': n(ks[6], (E, C), 0.02), 'group_bias': jnp.zeros((G,), jnp.float32), 'expert_bias': jnp.zeros((E,), jnp.float32)}
    _L1_ffn_all = _L1_ffn_setup()
    _L1_ffn_in = {k: v for k, v in _L1_ffn_all.items() if k in ('ln_scale', 'ln_bias', 'shared_in_w', 'shared_out_w', 'shared_out_b', 'expert_in_w', 'expert_out_weight', 'expert_out_bias', 'group_gate_w', 'expert_gate_w', 'group_bias', 'expert_bias')}
    del _L1_ffn_all
    return {'x': x, 'src': src, 'dst': dst, 'L0_gnn_adj_norm_sp': _L0_gnn_in['adj_norm_sp'], 'L0_gnn_W': _L0_gnn_in['W'], 'L0_gnn_b': _L0_gnn_in['b'], 'L0_gnn_gamma': _L0_gnn_in['gamma'], 'L0_gnn_beta': _L0_gnn_in['beta'], 'L0_ffn_router_w': _L0_ffn_in['router_w'], 'L0_ffn_router_b': _L0_ffn_in['router_b'], 'L0_ffn_w1': _L0_ffn_in['w1'], 'L0_ffn_b1': _L0_ffn_in['b1'], 'L0_ffn_w2': _L0_ffn_in['w2'], 'L0_ffn_b2': _L0_ffn_in['b2'], 'L1_gnn_W_qkv': _L1_gnn_in['W_qkv'], 'L1_gnn_b_qkv': _L1_gnn_in['b_qkv'], 'L1_gnn_W_ff': _L1_gnn_in['W_ff'], 'L1_gnn_b_ff': _L1_gnn_in['b_ff'], 'L1_ffn_ln_scale': _L1_ffn_in['ln_scale'], 'L1_ffn_ln_bias': _L1_ffn_in['ln_bias'], 'L1_ffn_shared_in_w': _L1_ffn_in['shared_in_w'], 'L1_ffn_shared_out_w': _L1_ffn_in['shared_out_w'], 'L1_ffn_shared_out_b': _L1_ffn_in['shared_out_b'], 'L1_ffn_expert_in_w': _L1_ffn_in['expert_in_w'], 'L1_ffn_expert_out_weight': _L1_ffn_in['expert_out_weight'], 'L1_ffn_expert_out_bias': _L1_ffn_in['expert_out_bias'], 'L1_ffn_group_gate_w': _L1_ffn_in['group_gate_w'], 'L1_ffn_expert_gate_w': _L1_ffn_in['expert_gate_w'], 'L1_ffn_group_bias': _L1_ffn_in['group_bias'], 'L1_ffn_expert_bias': _L1_ffn_in['expert_bias']}

def reference(x, src, dst, L0_gnn_adj_norm_sp, L0_gnn_W, L0_gnn_b, L0_gnn_gamma, L0_gnn_beta, L0_ffn_router_w, L0_ffn_router_b, L0_ffn_w1, L0_ffn_b1, L0_ffn_w2, L0_ffn_b2, L1_gnn_W_qkv, L1_gnn_b_qkv, L1_gnn_W_ff, L1_gnn_b_ff, L1_ffn_ln_scale, L1_ffn_ln_bias, L1_ffn_shared_in_w, L1_ffn_shared_out_w, L1_ffn_shared_out_b, L1_ffn_expert_in_w, L1_ffn_expert_out_weight, L1_ffn_expert_out_bias, L1_ffn_group_gate_w, L1_ffn_expert_gate_w, L1_ffn_group_bias, L1_ffn_expert_bias):
    import jax
    import jax.numpy as jnp

    def _L0_gnn_ref(x, edge_index, adj_norm_sp, W, b, gamma, beta):
        import jax, jax.numpy as jnp
        import numpy as np
        BN_EPS = 1e-05
        src = edge_index[0]
        dst = edge_index[1]
        agg = jax.ops.segment_sum(x[src], dst, num_segments=x.shape[0])
        h = x + agg
        z = h @ W.T + b
        mean = jnp.mean(z, axis=0)
        var = jnp.mean((z - mean) ** 2, axis=0)
        out = gamma * (z - mean) * jax.lax.rsqrt(var + BN_EPS) + beta
        return out

    def _L0_ffn_ref(x, router_w, router_b, w1, b1, w2, b2):
        import jax, jax.numpy as jnp
        import numpy as np
        B, S, D = (16, 1024, 512)
        H = 256
        E = 16
        TOP_K = 4
        x_flat = x.reshape(-1, D)
        logits = x_flat @ router_w + router_b
        top_vals, top_idx = jax.lax.top_k(logits, TOP_K)
        gates = jax.nn.softmax(top_vals, axis=-1)
        onehot = jax.nn.one_hot(top_idx, E, dtype=x.dtype)
        comb = jnp.einsum('tk,tke->te', gates, onehot)
        out = jnp.zeros_like(x_flat)
        for e in range(E):
            h = jax.nn.relu(x_flat @ w1[e] + b1[e])
            y = h @ w2[e] + b2[e]
            out = out + comb[:, e:e + 1] * y
        return out.reshape(x.shape)

    def _L1_gnn_ref(x, edge_index, W_qkv, b_qkv, W_ff, b_ff):
        import jax, jax.numpy as jnp
        import numpy as np
        from math import sqrt
        N = 6250
        E = 100000
        D_EMB = 512
        DK = 64
        DV = 64
        HEADS = 8

        def _attention_message(Q, K, V, senders, receivers, n_nodes):
            scale = 1.0 / sqrt(Q.shape[-1])
            scores = jnp.einsum('ehd,ehd->eh', Q[receivers], K[senders]) * scale
            smax = jax.ops.segment_max(scores, receivers, num_segments=n_nodes)
            ex = jnp.exp(scores - smax[receivers])
            denom = jax.ops.segment_sum(ex, receivers, num_segments=n_nodes)
            att = ex / denom[receivers]
            out = jax.ops.segment_sum(att[:, :, None] * V[senders], receivers, num_segments=n_nodes)
            return (out, att)
        n_nodes = x.shape[0]
        qkv = x @ W_qkv.T + b_qkv
        Q, K, V = jnp.split(qkv, [DK * HEADS, 2 * DK * HEADS], axis=-1)
        Q = Q.reshape(n_nodes, HEADS, DK)
        K = K.reshape(n_nodes, HEADS, DK)
        V = V.reshape(n_nodes, HEADS, DV)
        senders, receivers = (edge_index[0], edge_index[1])
        msg, _ = _attention_message(Q, K, V, senders, receivers, n_nodes)
        out = msg.reshape(n_nodes, HEADS * DV) @ W_ff.T + b_ff
        return out

    def _L1_ffn_ref(x, ln_scale, ln_bias, shared_in_w, shared_out_w, shared_out_b, expert_in_w, expert_out_weight, expert_out_bias, group_gate_w, expert_gate_w, group_bias, expert_bias):
        import jax, jax.numpy as jnp
        import numpy as np
        B, T, C = (8, 1024, 512)
        H = 1024
        G, EG = (2, 4)
        E = G * EG
        K = 2
        LN_EPS = 1e-05

        def _swiglu(x):
            a, b = jnp.split(x, 2, axis=-1)
            return jax.nn.silu(a) * b
        Bx, Tx, Cx = x.shape
        S = Bx * Tx
        flat = x.reshape(S, Cx)
        mu = flat.mean(-1, keepdims=True)
        var = ((flat - mu) ** 2).mean(-1, keepdims=True)
        flat = (flat - mu) * jax.lax.rsqrt(var + LN_EPS) * ln_scale + ln_bias
        h_shared = _swiglu(flat @ shared_in_w.T)
        out_shared = h_shared @ shared_out_w.T + shared_out_b
        g_logits = flat @ group_gate_w.T + group_bias
        g_idx = jnp.argmax(g_logits, axis=-1)
        e_logits = (flat @ expert_gate_w.T).reshape(S, G, EG)
        e_sel = jnp.take_along_axis(e_logits, g_idx[:, None, None], axis=1)[:, 0, :]
        e_sel = e_sel + expert_bias.reshape(G, EG)[g_idx]
        e_probs = jax.nn.softmax(e_sel, axis=-1)
        topv, topi = jax.lax.top_k(e_probs, K)
        topv = topv / (topv.sum(-1, keepdims=True) + 1e-08)
        disp = g_idx[:, None] * EG + topi
        h_expert = _swiglu(flat @ expert_in_w.T)
        rows = jnp.arange(S)[:, None]
        comb = jnp.zeros((S, E), flat.dtype).at[rows, disp].add(topv)
        cnt = jnp.zeros((S, E), flat.dtype).at[rows, disp].add(1.0)
        routed = cnt @ expert_out_bias
        for e in range(E):
            routed = routed + comb[:, e:e + 1] * (h_expert @ expert_out_weight[e].T)
        return (out_shared + routed).reshape(Bx, Tx, Cx)
    edge_index = jnp.stack([src, dst])
    x = x + _L0_gnn_ref(_layernorm(x, axis=-1), edge_index, L0_gnn_adj_norm_sp, L0_gnn_W, L0_gnn_b, L0_gnn_gamma, L0_gnn_beta)
    x = x + _L0_ffn_ref(_layernorm(x, axis=-1)[None], L0_ffn_router_w, L0_ffn_router_b, L0_ffn_w1, L0_ffn_b1, L0_ffn_w2, L0_ffn_b2)[0]
    x = x + _L1_gnn_ref(_layernorm(x, axis=-1), edge_index, L1_gnn_W_qkv, L1_gnn_b_qkv, L1_gnn_W_ff, L1_gnn_b_ff)
    x = x + _L1_ffn_ref(_layernorm(x, axis=-1)[None], L1_ffn_ln_scale, L1_ffn_ln_bias, L1_ffn_shared_in_w, L1_ffn_shared_out_w, L1_ffn_shared_out_b, L1_ffn_expert_in_w, L1_ffn_expert_out_weight, L1_ffn_expert_out_bias, L1_ffn_group_gate_w, L1_ffn_expert_gate_w, L1_ffn_group_bias, L1_ffn_expert_bias)[0]
    return x

_drawn_inputs = setup_inputs


def setup_inputs(seed=0):
    import zlib

    import numpy as np

    out = dict(_drawn_inputs(seed))
    spreads = {'L1_gnn_b_qkv': (0.0, 0.1),
     'L1_gnn_b_ff': (0.0, 0.1),
     'L1_ffn_ln_scale': (1.0, 0.2),
     'L1_ffn_ln_bias': (0.0, 0.1),
     'L1_ffn_shared_out_b': (0.0, 0.1),
     'L1_ffn_expert_out_bias': (0.0, 0.1),
     'L1_ffn_group_bias': (0.0, 0.1),
     'L1_ffn_expert_bias': (0.0, 0.1)}
    factors = {'L0_gnn_b': 8.0, 'L0_ffn_router_b': 4.845, 'L0_ffn_b1': 7.565, 'L0_ffn_b2': 3.114}
    for name, (base, spread) in spreads.items():
        noise = np.random.default_rng([zlib.crc32(name.encode()), seed]).standard_normal(out[name].shape)
        drawn = base * np.exp(spread * noise) if base else spread * noise
        out[name] = jnp.asarray(drawn.astype(out[name].dtype))
    for name, factor in factors.items():
        out[name] = (out[name] * factor).astype(out[name].dtype)
    return out
```

```python
import numpy as np
import concourse.bass as bass
from concourse import mybir
from contextlib import ExitStack

F32 = mybir.dt.float32
BF16 = mybir.dt.bfloat16
F16 = mybir.dt.float16
U16 = mybir.dt.uint16
I32 = mybir.dt.int32
ALU = mybir.AluOpType
ACT = mybir.ActivationFunctionType
AX = mybir.AxisListType

N = 1250
D = 512
E = 20000
TP = 125
NT = N // TP
ET = E // TP
DC = D // 128
SPANS = [(0, 500), (500, 500), (1000, 250)]
GROUPS = [(0, 4), (4, 4), (8, 2)]
EPS = 1e-5
NEG = -1.0e30

R1, H1 = 16, 256
TOP1 = 4
HEADS, DK = 8, 64
H2 = 1024
G2, EG2 = 2, 4
R2 = G2 * EG2
TOP2 = 2


class OnChip:
    pass


def blocks5(ap):
    return ap.rearrange("p (a b) -> p a b", b=256)[:, :, 0:250]


def five(ap):
    return ap.rearrange("p (a b) -> p a b", b=250)


def adjacency_stage(nc, k, d):
    ctx = ExitStack()
    sb = lambda n, s, t: ctx.enter_context(nc.sbuf_tensor(n, s, t))
    pb = lambda n, s, t: ctx.enter_context(nc.psum_tensor(n, s, t))
    sem = lambda n: ctx.enter_context(nc.semaphore(n))
    HALF = ET // 2
    with ctx:
        edges_i = sb("edges_i", [HALF, 2, 2, TP], I32)
        edges_f = sb("edges_f", [HALF, 2, 2, TP], F32)
        bounds_q = sb("bounds_q", [HALF, 2, 2], F32)
        spread = sb("spread", [HALF, 2, 2, HALF], F32)
        src_e = sb("src_e", [TP, ET], F32)
        dst_e = sb("dst_e", [TP, ET], F32)
        nodes_i = sb("nodes_i", [TP, N], I32)
        nodes = sb("nodes", [TP, N], F16)
        tile_up_i = sb("tile_up_i", [NT, ET], I32)
        tile_up = sb("tile_up", [NT, ET], F32)
        tile_down = sb("tile_down", [NT, ET], F32)
        first_i = sb("first_i", [NT, 1], I32)
        first = sb("first", [NT, 2], F32)
        ones_q = sb("ones_q", [HALF, NT], F32)
        before = sb("before", [NT, NT], F32)
        touch = sb("touch", [NT, 3, ET], F32)
        reach = sb("reach", [NT, 6], F32)
        table_i = sb("table_i", [NT, 3], I32)
        table = sb("table", [1, 3 * NT], I32)
        RING = 4
        hot_src = sb("hot_src", [TP, RING * N], BF16)
        hot_dst = sb("hot_dst", [TP, RING * TP], BF16)
        zeros = sb("zeros", [TP, 500], BF16)
        counts = [k.XN[:, :, :].rearrange("p t c -> p (t c)")[:, p * N:(p + 1) * N] for p in range(2)]
        pA = [pb(f"pA{p}", [128, 1536], F32) for p in range(2)]
        pT = [pb(f"pT{p}", [128, 512], F32) for p in range(2)]

        edges_in = sem("edges_in")
        table_in = sem("table_in")
        iota_done = sem("iota_done")
        consts_done = sem("consts_done")
        cast_done = sem("cast_done")
        ident_done = sem("ident_done")
        edges_turned = sem("edges_turned")
        edges_copied = sem("edges_copied")
        step = sem("step")
        spread_done = sem("spread_done")
        bounds_mm = sem("bounds_mm")
        reach_done = sem("reach_done")
        prefix_mm = sem("prefix_mm")
        table_done = sem("table_done")
        hot_ready = sem("hot_ready")
        hot_used = sem("hot_used")
        block_mm = sem("block_mm")
        counts_copied = sem("counts_copied")
        block_taken = sem("block_taken")
        turned = sem("turned")
        turned_copied = sem("turned_copied")

        with nc.Block() as block:
            @block.sync
            def _(sp):
                for j, e in enumerate((d["src"], d["dst"])):
                    sp.dma_start(edges_i[:, j, :, :], e.rearrange("(r q e) -> q r e", r=2, e=TP)).then_inc(edges_in, 16)
                sp.dma_start(k.X[:, :, :], d["x"].rearrange("(t p) c -> p t c", p=TP)).then_inc(k.x_in, 16)
                sp.dma_start(k.WT[:, :, :], d["gnn_w"].rearrange("(c p) f -> p c f", p=128)).then_inc(k.gnn_w_in, 16)
                for j, row in enumerate((d["gnn_b"], d["gnn_gamma"], d["gnn_beta"])):
                    sp.dma_start(k.ROWS[:, j, :], row.rearrange("(a n) -> a n", a=1).to_broadcast([TP, D])).then_inc(k.gnn_w_in, 16)
                sp.wait_ge(table_done, 1)
                for b in range(NT):
                    sp.dma_start(table[0:1, 3 * b:3 * b + 3], table_i[b:b + 1, :]).then_inc(table_in, 16)

            @block.gpsimd
            def _(pool):
                pool.iota(nodes_i[:, :], pattern=[[1, N]], base=0, channel_multiplier=0).then_inc(iota_done, 1)
                pool.iota(tile_up_i[:, :], pattern=[[1, ET]], base=1, channel_multiplier=0).then_inc(iota_done, 1)
                pool.iota(first_i[:, :], pattern=[[0, 1]], base=0, channel_multiplier=TP).then_inc(iota_done, 1)
                pool.memset(k.IDENT[:, :], 0.0).then_inc(consts_done, 1)
                pool.memset(before[:, :], 1.0).then_inc(consts_done, 1)
                pool.memset(ones_q[:, :], 1.0).then_inc(consts_done, 1)
                pool.memset(zeros[:, :], 0.0).then_inc(consts_done, 1)
                pool.memset(k.ONES[:, :], 1.0).then_inc(consts_done, 1)
                pool.memset(k.EPSC[:, :], EPS).then_inc(consts_done, 1)
                pool.wait_ge(consts_done, 6)
                pool.affine_select(out=k.IDENT[:, :], in_=k.IDENT[:, :], compare_op=ALU.not_equal, fill=1.0,
                                   base=0, pattern=[[-1, 128]], channel_multiplier=1).then_inc(ident_done, 1)
                pool.affine_select(out=before[:, :], in_=before[:, :], compare_op=ALU.is_gt, fill=0.0,
                                   base=0, pattern=[[1, NT]], channel_multiplier=-1).then_inc(ident_done, 1)

            @block.vector
            def _(dve):
                dve.wait_ge(edges_in, 32)
                nc.vector.tensor_copy(edges_f[:, :, :, :], edges_i[:, :, :, :]).then_inc(cast_done, 1)
                dve.wait_ge(iota_done, 3)
                nc.vector.tensor_copy(nodes[:, :], nodes_i[:, :]).then_inc(cast_done, 1)
                nc.vector.tensor_copy(tile_up[:, :], tile_up_i[:, :]).then_inc(step, 1)
                nc.vector.tensor_copy(first[:, 0:1], first_i[:, :]).then_inc(step, 1)
                dve.wait_ge(cast_done, 1)
                nc.vector.tensor_reduce(bounds_q[:, 0, :], edges_f[:, 1, :, :], AX.X, ALU.min).then_inc(step, 1)
                nc.vector.tensor_reduce(bounds_q[:, 1, :], edges_f[:, 1, :, :], AX.X, ALU.max).then_inc(step, 1)
                dve.wait_ge(step, 4)
                nc.vector.tensor_scalar(tile_down[:, :], tile_up[:, :], -1.0, float(ET + 1), ALU.mult, ALU.add).then_inc(step, 1)
                nc.vector.tensor_scalar(first[:, 1:2], first[:, 0:1], float(TP - 1), None, ALU.add).then_inc(step, 1)
                dve.wait_ge(ident_done, 1)
                for m in range(2):
                    for r in range(2):
                        nc.vector.tensor_scalar(spread[:, m, r, :], k.IDENT[0:HALF, 0:HALF], bounds_q[:, m, r:r + 1], None,
                                                ALU.mult).then_inc(spread_done, 1)
                dve.wait_ge(edges_turned, 1)
                nc.vector.tensor_copy(src_e[:, :], pT[0][0:TP, 0:ET]).then_inc(edges_copied, 1)
                nc.vector.tensor_copy(dst_e[:, :], pT[0][0:TP, 256:256 + ET]).then_inc(edges_copied, 1)
                dve.wait_ge(bounds_mm, 1)
                dve.wait_ge(step, 6)
                nc.vector.tensor_scalar(touch[:, 0, :], pT[1][0:NT, 0:ET], first[:, 1:2], None, ALU.is_le).then_inc(step, 1)
                nc.vector.tensor_scalar(touch[:, 1, :], pT[1][0:NT, 256:256 + ET], first[:, 0:1], None, ALU.is_ge).then_inc(step, 1)
                dve.wait_ge(step, 8)
                nc.vector.tensor_tensor(touch[:, 2, :], touch[:, 0, :], touch[:, 1, :], ALU.mult).then_inc(step, 1)
                dve.wait_ge(step, 9)
                nc.vector.tensor_tensor(touch[:, 0, :], touch[:, 2, :], tile_down[:, :], ALU.mult).then_inc(step, 1)
                nc.vector.tensor_tensor(touch[:, 1, :], touch[:, 2, :], tile_up[:, :], ALU.mult).then_inc(step, 1)
                dve.wait_ge(step, 11)
                nc.vector.tensor_reduce(reach[:, 0:2], touch[:, 0:2, :], AX.X, ALU.max).then_inc(step, 1)
                dve.wait_ge(step, 12)
                nc.vector.tensor_scalar(reach[:, 2:3], reach[:, 0:1], -1.0, float(ET), ALU.mult, ALU.add).then_inc(step, 1)
                dve.wait_ge(step, 13)
                nc.vector.tensor_scalar(reach[:, 2:3], reach[:, 2:3], float(ET - 1), None, ALU.min).then_inc(step, 1)
                dve.wait_ge(step, 14)
                nc.vector.tensor_tensor(reach[:, 3:4], reach[:, 1:2], reach[:, 2:3], ALU.subtract).then_inc(step, 1)
                dve.wait_ge(step, 15)
                nc.vector.tensor_scalar(reach[:, 3:4], reach[:, 3:4], 1.0, None, ALU.max).then_inc(reach_done, 1)
                dve.wait_ge(reach_done, 1)
                nc.vector.tensor_tensor(reach[:, 4:5], reach[:, 2:3], reach[:, 3:4], ALU.add).then_inc(step, 1)
                dve.wait_ge(prefix_mm, 1)
                nc.vector.tensor_tensor(reach[:, 5:6], pT[0][0:NT, 510:511], reach[:, 2:3], ALU.subtract).then_inc(step, 1)
                dve.wait_ge(step, 17)
                nc.vector.tensor_scalar(reach[:, 5:6], reach[:, 5:6], float(ET), None, ALU.add).then_inc(step, 1)
                nc.vector.tensor_copy(table_i[:, 0:1], reach[:, 2:3]).then_inc(step, 1)
                nc.vector.tensor_copy(table_i[:, 1:2], reach[:, 4:5]).then_inc(step, 1)
                dve.wait_ge(step, 20)
                nc.vector.tensor_copy(table_i[:, 2:3], reach[:, 5:6]).then_inc(table_done, 1)
                dve.wait_ge(edges_copied, 2)
                dve.wait_ge(cast_done, 2)
                dve.wait_ge(table_in, 16 * NT)
                dve.sem_inc(hot_ready, ET)
                with dve.Fori(0, NT) as b:
                    lo = dve.value_load(table[0:1, bass.ds(3 * b, 1)], min_val=0, max_val=ET - 1)
                    hi = dve.value_load(table[0:1, bass.ds(3 * b + 1, 1)], min_val=1, max_val=ET)
                    off = dve.value_load(table[0:1, bass.ds(3 * b + 2, 1)], min_val=1, max_val=NT * ET)
                    with dve.Fori(lo, hi) as t:
                        s = dve.snap((off + t) % RING)
                        dve.wait_ge(hot_used, off + t + 1)
                        nc.vector.tensor_scalar(hot_dst[:, bass.ds(s * TP, TP)], nodes[:, bass.ds(b * TP, TP)],
                                                dst_e[:, bass.ds(t, 1)], None, ALU.is_equal)
                        nc.vector.tensor_scalar(hot_src[:, bass.ds(s * N, N)], nodes[:, :],
                                                src_e[:, bass.ds(t, 1)], None, ALU.is_equal).then_inc(hot_ready, 1)
                dve.wait_ge(block_taken, NT + 2)
                nc.vector.tensor_scalar(k.M[:, :, :], k.A16[:, :, :], 0.0, NEG, ALU.is_equal, ALU.mult).then_inc(step, 1)
                dve.wait_ge(turned_copied, 3 * NT + 2)
                for t in range(NT):
                    nc.vector.tensor_tensor(k.AT[:, t, t * TP:(t + 1) * TP], k.AT[:, t, t * TP:(t + 1) * TP],
                                            k.IDENT[0:TP, 0:TP], ALU.add).then_inc(step, 1)

            @block.tensor
            def _(pe):
                pe.wait_ge(ident_done, 2)
                pe.wait_ge(cast_done, 1)
                for j in range(2):
                    for r in range(2):
                        last = nc.tensor.transpose(pT[0][0:TP, 256 * j + HALF * r:256 * j + HALF * (r + 1)],
                                                   edges_f[:, j, r, :], k.IDENT[0:HALF, 0:HALF])
                last.then_inc(edges_turned, 1)
                pe.wait_ge(spread_done, 4)
                for m in range(2):
                    last = nc.tensor.matmul(pT[1][0:NT, 256 * m:256 * m + ET], ones_q[:, :],
                                            spread[:, m, :, :].rearrange("p r q -> p (r q)"), start=True, stop=True)
                last.then_inc(bounds_mm, 1)
                pe.wait_ge(reach_done, 1)
                pe.wait_ge(edges_copied, 2)
                nc.tensor.matmul(pT[0][0:NT, 510:511], before[:, :], reach[:, 3:4], start=True, stop=True).then_inc(prefix_mm, 1)
                pe.wait_ge(table_in, 16 * NT)
                pe.sem_inc(hot_used, ET + RING)
                with pe.Fori(0, NT // 2) as u:
                    for p in range(2):
                        b = 2 * u + p
                        lo = pe.value_load(table[0:1, bass.ds(3 * b, 1)], min_val=0, max_val=ET - 1)
                        hi = pe.value_load(table[0:1, bass.ds(3 * b + 1, 1)], min_val=1, max_val=ET)
                        off = pe.value_load(table[0:1, bass.ds(3 * b + 2, 1)], min_val=1, max_val=NT * ET)
                        pe.wait_ge(block_taken, 2 * u + p + 1)
                        for c0, w in SPANS:
                            out = pA[p][0:TP, c0 * 256 // 250:c0 * 256 // 250 + w * 256 // 250]
                            nc.tensor.matmul(out.rearrange("p (a b) -> p a b", b=256)[:, :, 0:250], zeros[:, 0:TP],
                                             zeros[:, 0:w].rearrange("p (a b) -> p a b", b=250), start=True, stop=False,
                                             skip_group_check=True)
                        with pe.Fori(lo, hi) as t:
                            s = pe.snap((off + t) % RING)
                            pe.wait_ge(hot_ready, off + t + 1)
                            for c0, w in SPANS:
                                out = pA[p][0:TP, c0 * 256 // 250:c0 * 256 // 250 + w * 256 // 250]
                                last = nc.tensor.matmul(out.rearrange("p (a b) -> p a b", b=256)[:, :, 0:250],
                                                        hot_dst[:, bass.ds(s * TP, TP)],
                                                        hot_src[:, bass.ds(s * N + c0, w)].rearrange("p (a b) -> p a b", b=250),
                                                        start=False, stop=False, skip_group_check=True)
                            last.then_inc(hot_used, 1)
                        for c0, w in SPANS:
                            out = pA[p][0:TP, c0 * 256 // 250:c0 * 256 // 250 + w * 256 // 250]
                            last = nc.tensor.matmul(out.rearrange("p (a b) -> p a b", b=256)[:, :, 0:250], zeros[:, 0:TP],
                                                    zeros[:, 0:w].rearrange("p (a b) -> p a b", b=250), start=False, stop=True,
                                                    skip_group_check=True)
                        last.then_inc(block_mm, 1)
                        pe.wait_ge(counts_copied, 2 * u + p + 1)
                        for g, (t0, n) in enumerate(GROUPS):
                            q = (3 * p + g) % 2
                            pe.wait_ge(turned_copied, 6 * u + 3 * p + g + 1)
                            for t in range(n):
                                last = nc.tensor.transpose(pT[q][0:TP, t * TP:(t + 1) * TP],
                                                           counts[p][:, (t0 + t) * TP:(t0 + t + 1) * TP], k.IDENT[0:TP, 0:TP])
                            last.then_inc(turned, 1)

            @block.scalar
            def _(act):
                act.sem_inc(block_taken, 2)
                act.wait_ge(table_in, 16 * NT)
                act.sem_inc(turned_copied, 2)
                with act.Fori(0, NT // 2) as u:
                    for p in range(2):
                        b = 2 * u + p
                        act.wait_ge(block_mm, 2 * u + p + 1)
                        nc.scalar.activation(five(counts[p]), blocks5(pA[p][0:TP, 0:1280]), ACT.Copy).then_inc(counts_copied, 1)
                        nc.scalar.activation(k.A16[:, bass.ds(b, 1), :].rearrange("p o (a b) -> p (o a) b", b=250),
                                             blocks5(pA[p][0:TP, 0:1280]), ACT.Copy).then_inc(block_taken, 1)
                        for g, (t0, n) in enumerate(GROUPS):
                            q = (3 * p + g) % 2
                            act.wait_ge(turned, 6 * u + 3 * p + g + 1)
                            nc.scalar.activation(k.AT[:, t0:t0 + n, bass.ds(b * TP, TP)],
                                                 pT[q][0:TP, 0:n * TP].rearrange("p (t n) -> p t n", n=TP),
                                                 ACT.Copy).then_inc(turned_copied, 1)



def normalise_rows_vector(nc, k, dve, src, dst, s, done):
    for t in range(NT):
        nc.vector.bn_stats(k.STATS[:, t, :], src[:, t, :]).then_inc(s.stats, 1)
    for t in range(NT):
        dve.wait_ge(s.stats, t + 1)
        nc.vector.bn_aggr(k.MV[:, t, :], k.STATS[:, t, :]).then_inc(s.moments, 1)
    dve.wait_ge(s.std, 1)
    nc.vector.reciprocal(k.RSTD[:, :], k.STD[:, :]).then_inc(s.rstd, 1)
    dve.wait_ge(s.rstd, 1)
    for t in range(NT):
        nc.vector.tensor_scalar(dst[:, t, :], src[:, t, :], k.MV[:, t, 0:1], k.RSTD[:, t:t + 1],
                                ALU.subtract, ALU.mult).then_inc(done, 1)


def normalise_rows_scalar(nc, k, act, s):
    act.wait_ge(s.moments, NT)
    nc.scalar.activation(k.STD[:, :], k.MV[:, :, 1], ACT.Sqrt, bias=k.EPSC[0:TP, 0:1]).then_inc(s.std, 1)


def turn_rows_tensor(nc, k, pe, banks, rows_done, turned, taken):
    for t in range(NT):
        pe.wait_ge(rows_done, t + 1)
        if t >= len(banks):
            pe.wait_ge(taken, t - len(banks) + 1)
        for c in range(DC):
            last = nc.tensor.transpose(banks[t % len(banks)][:, c * TP:(c + 1) * TP],
                                       k.XN[:, t, c * 128:(c + 1) * 128], k.IDENT[0:TP, 0:TP])
        last.then_inc(turned, 1)


def turn_rows_scalar(nc, k, act, banks, turned, taken):
    for t in range(NT):
        act.wait_ge(turned, t + 1)
        nc.scalar.activation(k.XT[:, :, t * TP:(t + 1) * TP],
                             banks[t % len(banks)][:, 0:DC * TP].rearrange("p (c n) -> p c n", n=TP),
                             ACT.Copy).then_inc(taken, 1)


def norm_semaphores(sem, name):
    s = OnChip()
    s.stats, s.moments, s.std, s.rstd = sem(name + "_stats"), sem(name + "_moments"), sem(name + "_std"), sem(name + "_rstd")
    return s


def graph_stage(nc, k, d):
    ctx = ExitStack()
    pb = lambda n, s, t: ctx.enter_context(nc.psum_tensor(n, s, t))
    sem = lambda n: ctx.enter_context(nc.semaphore(n))
    with ctx:
        bank = [pb(f"gbank{i}", [128, 512], F32) for i in range(6)]
        column_mean = pb("column_mean", [128, 512], F32)
        column_var = pb("column_var", [128, 512], F32)
        SQ = ctx.enter_context(nc.sbuf_tensor("SQ", [TP, 2, D], F32))
        GAIN = ctx.enter_context(nc.sbuf_tensor("GAIN", [TP, D], F32))
        MEAN = ctx.enter_context(nc.sbuf_tensor("MEAN", [TP, D], F32))
        norm = norm_semaphores(sem, "g")
        rows_done, agg_mm, agg_taken = sem("g_rows_done"), sem("agg_mm"), sem("agg_taken")
        z_mm, z_done, mean_mm, mean_done = sem("z_mm"), sem("z_done"), sem("mean_mm"), sem("mean_done")
        centred, squared, var_mm = sem("centred"), sem("squared"), sem("var_mm")
        std_done, gain, beta_added, scaled, added = sem("std_done"), sem("gain"), sem("beta_added"), sem("scaled"), sem("added")
        Z = k.XN
        with nc.Block() as block:
            @block.vector
            def _(dve):
                dve.wait_ge(k.x_in, 16)
                normalise_rows_vector(nc, k, dve, k.X, k.XN, norm, rows_done)
                dve.wait_ge(k.gnn_w_in, 64)
                dve.wait_ge(agg_taken, 3 * DC)
                for t in range(NT):
                    dve.wait_ge(z_mm, t + 1)
                    nc.vector.tensor_tensor(Z[:, t, :], bank[t % 6][0:TP, :], k.ROWS[:, 0, :], ALU.add).then_inc(z_done, 1)
                dve.wait_ge(mean_mm, 1)
                nc.vector.tensor_scalar(MEAN[:, :], column_mean[0:TP, :], 1.0 / N, None, ALU.mult).then_inc(mean_done, 1)
                dve.wait_ge(z_done, NT)
                dve.wait_ge(mean_done, 1)
                for t in range(NT):
                    nc.vector.tensor_tensor(Z[:, t, :], Z[:, t, :], MEAN[:, :], ALU.subtract).then_inc(centred, 1)
                dve.wait_ge(std_done, 1)
                nc.vector.reciprocal(MEAN[:, :], GAIN[:, :]).then_inc(gain, 1)
                dve.wait_ge(gain, 1)
                nc.vector.tensor_tensor(MEAN[:, :], MEAN[:, :], k.ROWS[:, 1, :], ALU.mult).then_inc(gain, 1)
                dve.wait_ge(gain, 2)
                dve.wait_ge(centred, NT)
                dve.wait_ge(squared, NT)
                for t in range(NT):
                    nc.vector.tensor_tensor(Z[:, t, :], Z[:, t, :], MEAN[:, :], ALU.mult).then_inc(scaled, 1)
                dve.wait_ge(beta_added, NT)
                for t in range(NT):
                    dve.wait_ge(scaled, t + 1)
                    nc.vector.tensor_tensor(k.X[:, t, :], k.X[:, t, :], Z[:, t, :], ALU.add).then_inc(added, 1)

            @block.scalar
            def _(act):
                normalise_rows_scalar(nc, k, act, norm)
                g = 0
                for c in range(DC):
                    for c0, w in SPANS:
                        act.wait_ge(agg_mm, g + 1)
                        nc.scalar.activation(k.XT[:, c, c0:c0 + w], bank[g % 6][:, 0:w], ACT.Copy).then_inc(agg_taken, 1)
                        g += 1
                for t in range(NT):
                    act.wait_ge(centred, t + 1)
                    if t >= 2:
                        act.wait_ge(var_mm, t - 1)
                    nc.scalar.activation(SQ[:, t % 2, :], Z[:, t, :], ACT.Square).then_inc(squared, 1)
                act.wait_ge(var_mm, NT)
                nc.scalar.activation(GAIN[:, :], column_var[0:TP, :], ACT.Sqrt, bias=k.EPSC[0:TP, 0:1],
                                     scale=1.0 / N).then_inc(std_done, 1)

            @block.gpsimd
            def _(pool):
                pool.wait_ge(k.gnn_w_in, 64)
                pool.wait_ge(rows_done, NT)
                for t in range(NT):
                    pool.tensor_tensor(k.X[:, t, :], k.X[:, t, :], k.ROWS[:, 2, :], ALU.add).then_inc(beta_added, 1)

            @block.tensor
            def _(pe):
                pe.wait_ge(rows_done, NT)
                g = 0
                for c in range(DC):
                    for c0, w in SPANS:
                        if g >= 6:
                            pe.wait_ge(agg_taken, g - 5)
                        for s in range(NT):
                            last = nc.tensor.matmul(bank[g % 6][:, 0:w], k.XN[:, s, c * 128:(c + 1) * 128],
                                                    k.AT[:, s, c0:c0 + w], start=s == 0, stop=s == NT - 1)
                        last.then_inc(agg_mm, 1)
                        g += 1
                pe.wait_ge(agg_taken, 3 * DC)
                pe.wait_ge(k.gnn_w_in, 64)

                def add_mean(t):
                    pe.wait_ge(z_done, t + 1)
                    last = nc.tensor.matmul(column_mean[0:TP, :], k.ONES[0:TP, 0:TP], Z[:, t, :], start=t == 0, stop=t == NT - 1)
                    if t == NT - 1:
                        last.then_inc(mean_mm, 1)

                for t in range(NT):
                    if t >= 6:
                        pe.wait_ge(z_done, t - 5)
                    for c in range(DC):
                        last = nc.tensor.matmul(bank[t % 6][0:TP, :], k.XT[:, c, t * TP:(t + 1) * TP], k.WT[:, c, :],
                                                start=c == 0, stop=c == DC - 1)
                    last.then_inc(z_mm, 1)
                    if t >= 2:
                        add_mean(t - 2)
                add_mean(NT - 2)
                add_mean(NT - 1)
                for t in range(NT):
                    pe.wait_ge(squared, t + 1)
                    nc.tensor.matmul(column_var[0:TP, :], k.ONES[0:TP, 0:TP], SQ[:, t % 2, :], start=t == 0,
                                     stop=t == NT - 1).then_inc(var_mm, 1)


def mixture_stage(nc, k, d):
    ctx = ExitStack()
    sb = lambda n, s, t: ctx.enter_context(nc.sbuf_tensor(n, s, t))
    pb = lambda n, s, t: ctx.enter_context(nc.psum_tensor(n, s, t))
    sem = lambda n: ctx.enter_context(nc.semaphore(n))
    HC = H1 // 128
    with ctx:
        W1 = [sb(f"W1_{p}", [128, DC, H1], F32) for p in range(2)]
        W2 = [sb(f"W2_{p}", [128, HC, D], F32) for p in range(2)]
        HID = [sb(f"HID_{p}", [128, HC, N], F32) for p in range(2)]
        B1 = [sb(f"B1_{p}", [128, HC], F32) for p in range(2)]
        B2 = sb("B2", [R1, D], F32)
        RW = sb("RW", [128, DC, R1], F32)
        RB = sb("RB", [TP, R1], F32)
        LG = sb("LG", [TP, NT, R1], F32)
        GATE = sb("GATE", [TP, NT, R1], F32)
        GT = sb("GT", [R1, N], F32)
        COL = sb("COL", [TP, 4, NT], F32)
        BEAT = sb("BEAT", [TP, R1 * R1 * 2, ], F32)
        LOWER = sb("LOWER", [TP, R1, R1], F32)
        RANK = sb("RANK", [TP, NT, R1], F32)
        hbank = [pb(f"hbank{i}", [128, 512], F32) for i in range(4)]
        ybank = [pb(f"ybank{i}", [128, 512], F32) for i in range(4)]
        norm = norm_semaphores(sem, "m")
        rows_done, turned, taken = sem("m_rows_done"), sem("m_turned"), sem("m_taken")
        w_ready = [sem(f"w_ready{p}") for p in range(2)]
        small_in, lower_done, logit_mm = sem("small_in"), sem("lower_done"), sem("logit_mm")
        vstep, exped, gates = sem("m_vstep"), sem("exped"), sem("gates")
        gates_turned, gates_copied, bias_mm, bias_added = sem("gates_turned"), sem("gates_copied"), sem("bias_mm"), sem("bias_added")
        hid_mm, hid_done, y_mm, y_added = sem("hid_mm"), sem("hid_done"), sem("y_mm"), sem("y_added")
        w1v = d["w1"].rearrange("e (c p) h -> e p c h", p=128)
        w2v = d["w2"].rearrange("e (c p) f -> e p c f", p=128)

        with nc.Block() as block:
            @block.sync
            def _(sp):
                sp.dma_start(RW[:, :, :], d["router_w"].rearrange("(c p) e -> p c e", p=128)).then_inc(small_in, 16)
                sp.dma_start(RB[:, :], d["router_b"].rearrange("(a n) -> a n", a=1).to_broadcast([TP, R1])).then_inc(small_in, 16)
                sp.dma_start(B2[:, :], d["b2"]).then_inc(small_in, 16)
                with sp.Fori(0, R1 // 2) as u:
                    for p in range(2):
                        sp.wait_ge(y_mm, 2 * NT * u + NT * (p + 1))
                        sp.dma_start(B1[p][:, :], d["b1"][bass.ds(2 * u + p, 1)].rearrange("o (p c) -> p (o c)", p=128)).then_inc(w_ready[p], 16)
                        sp.dma_start(W1[p][:, :, :], w1v[bass.ds(2 * u + p, 1)].rearrange("o p c h -> p (o c) h")).then_inc(w_ready[p], 16)
                        sp.dma_start(W2[p][:, :, :], w2v[bass.ds(2 * u + p, 1)].rearrange("o p c f -> p (o c) f")).then_inc(w_ready[p], 16)

            @block.gpsimd
            def _(pool):
                pool.memset(LOWER[:, :, :], 1.0).then_inc(lower_done, 1)
                pool.wait_ge(lower_done, 1)
                pool.affine_select(out=LOWER[:, :, :], in_=LOWER[:, :, :], compare_op=ALU.is_gt, fill=0.0, base=0,
                                   pattern=[[1, R1], [-1, R1]], channel_multiplier=0).then_inc(lower_done, 1)

            @block.vector
            def _(dve):
                normalise_rows_vector(nc, k, dve, k.X, k.XN, norm, rows_done)
                dve.wait_ge(small_in, 48)
                dve.wait_ge(logit_mm, 1)
                nc.vector.tensor_tensor(LG[:, :, :], hbank[0][0:TP, 0:NT * R1].rearrange("p (t e) -> p t e", e=R1),
                                        RB[:, :].unsqueeze(1).to_broadcast([TP, NT, R1]), ALU.add).then_inc(vstep, 1)
                dve.wait_ge(vstep, 1)
                nc.vector.tensor_reduce(COL[:, 0, :], LG[:, :, :], AX.X, ALU.max).then_inc(vstep, 1)
                dve.wait_ge(lower_done, 2)
                n = 2
                for t in range(NT):
                    mine = LG[:, t, :].unsqueeze(2).to_broadcast([TP, R1, R1])
                    other = LG[:, t, :].unsqueeze(1).to_broadcast([TP, R1, R1])
                    beat = BEAT[:, 0:R1 * R1].rearrange("p (i j) -> p i j", j=R1)
                    same = BEAT[:, R1 * R1:2 * R1 * R1].rearrange("p (i j) -> p i j", j=R1)
                    if t:
                        dve.wait_ge(vstep, n)
                    nc.vector.tensor_tensor(beat, other, mine, ALU.is_gt).then_inc(vstep, 1)
                    nc.vector.tensor_tensor(same, other, mine, ALU.is_equal).then_inc(vstep, 1)
                    dve.wait_ge(vstep, n + 2)
                    nc.vector.tensor_tensor(same, same, LOWER[:, :, :], ALU.mult).then_inc(vstep, 1)
                    dve.wait_ge(vstep, n + 3)
                    nc.vector.tensor_tensor(beat, beat, same, ALU.add).then_inc(vstep, 1)
                    dve.wait_ge(vstep, n + 4)
                    nc.vector.tensor_reduce(RANK[:, t, :], beat, AX.X, ALU.add).then_inc(vstep, 1)
                    n += 5
                nc.vector.tensor_tensor(LG[:, :, :], LG[:, :, :], COL[:, 0, :].unsqueeze(2).to_broadcast([TP, NT, R1]),
                                        ALU.subtract).then_inc(vstep, 1)
                n += 1
                dve.wait_ge(vstep, n)
                nc.vector.tensor_scalar(RANK[:, :, :], RANK[:, :, :], TOP1 - 0.5, None, ALU.is_lt).then_inc(vstep, 1)
                n += 1
                dve.wait_ge(exped, 1)
                dve.wait_ge(vstep, n)
                nc.vector.tensor_tensor(GATE[:, :, :], GATE[:, :, :], RANK[:, :, :], ALU.mult).then_inc(vstep, 1)
                dve.wait_ge(vstep, n + 1)
                nc.vector.tensor_reduce(COL[:, 1, :], GATE[:, :, :], AX.X, ALU.add).then_inc(vstep, 1)
                dve.wait_ge(vstep, n + 2)
                nc.vector.reciprocal(COL[:, 2, :], COL[:, 1, :]).then_inc(vstep, 1)
                dve.wait_ge(vstep, n + 3)
                nc.vector.tensor_tensor(GATE[:, :, :], GATE[:, :, :], COL[:, 2, :].unsqueeze(2).to_broadcast([TP, NT, R1]),
                                        ALU.mult).then_inc(gates, 1)
                for t in range(NT):
                    dve.wait_ge(bias_mm, t + 1)
                    nc.vector.tensor_tensor(k.X[:, t, :], k.X[:, t, :], ybank[t % 4][0:TP, :], ALU.add).then_inc(bias_added, 1)
                dve.wait_ge(bias_added, NT)
                dve.wait_ge(gates, 1)
                dve.sem_inc(y_added, 4)
                with dve.Fori(0, R1 // 2) as u:
                    for m in range(2 * NT):
                        p, t = divmod(m, NT)
                        dve.wait_ge(y_mm, 2 * NT * (u + 1) + m + 1)
                        dve.wait_ge(y_added, 2 * NT * u + m + 4)
                        nc.vector.scalar_tensor_tensor(out=k.X[:, t, :], in0=ybank[m % 4][0:TP, :],
                                                       scalar=GATE[:, t, bass.ds(2 * u + p, 1)], in1=k.X[:, t, :],
                                                       op0=ALU.mult, op1=ALU.add).then_inc(y_added, 1)

            @block.scalar
            def _(act):
                normalise_rows_scalar(nc, k, act, norm)
                turn_rows_scalar(nc, k, act, ybank, turned, taken)
                act.wait_ge(vstep, 2 + 5 * NT + 1)
                nc.scalar.activation(GATE[:, :, :], LG[:, :, :], ACT.Exp).then_inc(exped, 1)
                for g, (t0, n) in enumerate(GROUPS):
                    act.wait_ge(gates_turned, g + 1)
                    nc.scalar.activation(GT[:, t0 * TP:(t0 + n) * TP], hbank[1 + g][0:R1, 0:n * TP], ACT.Copy).then_inc(gates_copied, 1)
                act.sem_inc(hid_done, 4)
                with act.Fori(0, R1 // 2) as u:
                    m = 0
                    for p in range(2):
                        act.wait_ge(w_ready[p], 48 * u + 48)
                        act.wait_ge(y_mm, 2 * NT * u + NT * (p + 1))
                        for c0, w in SPANS:
                            for h in range(HC):
                                act.wait_ge(hid_mm, 12 * u + m + 1)
                                nc.scalar.activation(HID[p][:, h, c0:c0 + w], hbank[m % 4][:, 0:w], ACT.Relu,
                                                     bias=B1[p][:, h:h + 1]).then_inc(hid_done, 1)
                                m += 1

            @block.tensor
            def _(pe):
                pe.sem_inc(y_mm, 2 * NT)
                turn_rows_tensor(nc, k, pe, ybank, rows_done, turned, taken)
                pe.wait_ge(taken, NT)
                pe.wait_ge(small_in, 48)
                for t in range(NT):
                    for c in range(DC):
                        last = nc.tensor.matmul(hbank[0][0:TP, t * R1:(t + 1) * R1], k.XT[:, c, t * TP:(t + 1) * TP], RW[:, c, :],
                                                start=c == 0, stop=c == DC - 1)
                last.then_inc(logit_mm, 1)
                pe.wait_ge(gates, 1)
                for g, (t0, n) in enumerate(GROUPS):
                    for t in range(n):
                        last = nc.tensor.transpose(hbank[1 + g][0:R1, t * TP:(t + 1) * TP], GATE[:, t0 + t, :], k.IDENT[0:TP, 0:TP])
                    last.then_inc(gates_turned, 1)
                pe.wait_ge(gates_copied, 3)
                for t in range(NT):
                    if t >= 4:
                        pe.wait_ge(bias_added, t - 3)
                    nc.tensor.matmul(ybank[t % 4][0:TP, :], GT[:, t * TP:(t + 1) * TP], B2[:, :], start=True, stop=True).then_inc(bias_mm, 1)
                pe.wait_ge(bias_added, NT)
                with pe.Fori(0, R1 // 2) as u:
                    m = 0
                    for p in range(2):
                        pe.wait_ge(w_ready[p], 48 * u + 48)
                        for c0, w in SPANS:
                            for h in range(HC):
                                pe.wait_ge(hid_done, 12 * u + m + 1)
                                for c in range(DC):
                                    last = nc.tensor.matmul(hbank[m % 4][:, 0:w], W1[p][:, c, h * 128:(h + 1) * 128],
                                                            k.XT[:, c, c0:c0 + w], start=c == 0, stop=c == DC - 1)
                                last.then_inc(hid_mm, 1)
                                m += 1
                        for t in range(NT):
                            y = NT * p + t
                            pe.wait_ge(hid_done, 12 * u + 6 * p + 2 * (t // 4) + 2 + 4)
                            pe.wait_ge(y_added, 2 * NT * u + y + 1)
                            for h in range(HC):
                                last = nc.tensor.matmul(ybank[y % 4][0:TP, :], HID[p][:, h, t * TP:(t + 1) * TP], W2[p][:, h, :],
                                                        start=h == 0, stop=h == HC - 1)
                            last.then_inc(y_mm, 1)


def attention_stage(nc, k, d):
    ctx = ExitStack()
    sb = lambda n, s, t: ctx.enter_context(nc.sbuf_tensor(n, s, t))
    pb = lambda n, s, t: ctx.enter_context(nc.psum_tensor(n, s, t))
    sem = lambda n: ctx.enter_context(nc.semaphore(n))
    PAIRS = HEADS // 2
    UNITS = 2 * NT
    SCALE = 1.0 / float(np.sqrt(DK))
    with ctx:
        WQKV = sb("WQKV", [128, 3, DC, 128], F32)
        WFF = sb("WFF", [128, D], F32)
        BQK = sb("BQK", [128, 2], F32)
        BV = sb("BV", [TP, 128], F32)
        BFF = sb("BFF", [TP, D], F32)
        QT = sb("QT", [128, N], F32)
        KT = sb("KT", [128, N], F32)
        V = sb("V", [TP, NT, 128], F32)
        MASKED = [sb(f"MASKED{p}", [TP, N], F32) for p in range(2)]
        PROB = [sb(f"PROB{p}", [TP, N], F32) for p in range(3)]
        PROBT = [sb(f"PROBT{p}", [TP, NT, TP], F32) for p in range(2)]
        MSG = sb("MSG", [TP, NT, 2, DK], F32)
        MSGT = sb("MSGT", [128, N], F32)
        TOP = sb("TOP", [TP, UNITS], F32)
        SHIFT = sb("SHIFT", [TP, UNITS], F32)
        DEN = sb("DEN", [TP, 2, NT], F32)
        score = pb("score", [128, 1536], F32)
        turn = pb("turn", [128, 3, 512], F32)
        out_bank = [pb(f"out_bank{p}", [128, 512], F32) for p in range(2)]
        norm = norm_semaphores(sem, "a")
        rows_done, turned, taken = sem("a_rows_done"), sem("a_turned"), sem("a_taken")
        wqkv_in, wff_in, bff_in, bff_added = sem("wqkv_in"), sem("wff_in"), sem("bff_in"), sem("bff_added")
        proj_mm, qk_done, v_done = sem("proj_mm"), sem("qk_done"), sem("v_done")
        scores_seen = sem("scores_seen")
        score_mm, masked, shift_done, exp_done, weighted = sem("score_mm"), sem("masked"), sem("shift_done"), sem("exp_done"), sem("weighted")
        prob_turned, prob_copied, msg_mm, msg_copied = sem("prob_turned"), sem("prob_copied"), sem("msg_mm"), sem("msg_copied")
        den_done, msg_done, msg_turned, msgt_copied = sem("den_done"), sem("msg_done"), sem("msg_turned"), sem("msgt_copied")
        ff_mm, ff_added = sem("ff_mm"), sem("ff_added")
        bank = lambda i: score[:, 512 * i:512 * (i + 1)] if i < 3 else turn[:, i - 3, :]
        turn_banks = [bank(i) for i in range(6)]

        with nc.Block() as block:
            @block.sync
            def _(sp):
                sp.dma_start(BFF[:, :], d["ff_b"].rearrange("(a n) -> a n", a=1).to_broadcast([TP, D])).then_inc(bff_in, 16)
                with sp.Fori(0, PAIRS) as i:
                    sp.wait_ge(proj_mm, 9 * i + 9)
                    for j in range(3):
                        sp.dma_start(WQKV[:, j, :, :], d["qkv_w"].rearrange("(c p) f -> p c f", p=128)[:, :, bass.ds(128 * i + D * j, 128)]).then_inc(wqkv_in, 16)
                    sp.wait_ge(ff_mm, NT * i + NT)
                    sp.dma_start(BQK[:, :], d["qk_b"][bass.ds(i, 1)].rearrange("o (p j) -> p (o j)", p=128)).then_inc(wff_in, 16)
                    sp.dma_start(BV[:, :], d["v_b"][bass.ds(i, 1)].to_broadcast([TP, 128])).then_inc(wff_in, 16)
                    sp.dma_start(WFF[:, :], d["ff_w"][bass.ds(128 * i, 128), :]).then_inc(wff_in, 16)

            @block.gpsimd
            def _(pool):
                pool.wait_ge(bff_in, 16)
                pool.wait_ge(rows_done, NT)
                for t in range(NT):
                    pool.tensor_tensor(k.X[:, t, :], k.X[:, t, :], BFF[:, :], ALU.add).then_inc(bff_added, 1)

            @block.vector
            def _(dve):
                normalise_rows_vector(nc, k, dve, k.X, k.XN, norm, rows_done)
                dve.wait_ge(bff_added, NT)
                dve.sem_inc(ff_added, 3)
                with dve.Fori(0, PAIRS) as i:
                    dve.wait_ge(wff_in, 48 * i + 48)
                    for g, (t0, n) in enumerate(GROUPS):
                        dve.wait_ge(proj_mm, 9 * i + 9 + 6 + g + 1)
                        nc.vector.tensor_tensor(V[:, t0:t0 + n, :], bank(g)[0:TP, 0:128 * n].rearrange("p (t c) -> p t c", c=128),
                                                BV[:, :].unsqueeze(1).to_broadcast([TP, n, 128]), ALU.add).then_inc(v_done, 1)
                    for s in range(UNITS + 4):
                        if s < UNITS:
                            u, t = s, s % NT
                            dve.wait_ge(score_mm, UNITS * i + u + 1)
                            if u >= 2:
                                dve.wait_ge(exp_done, UNITS * i + u - 1)
                            dve.sem_inc(scores_seen, 1)
                            nc.vector.tensor_tensor_reduce(out=five(MASKED[u % 2][:, :]), in0=blocks5(score[0:TP, 0:1280]),
                                                           in1=five(k.M[:, t, :]), scale=1.0, scalar=3.0 * NEG, op0=ALU.add, op1=ALU.max,
                                                           accum_out=TOP[:, u:u + 1]).then_inc(masked, 1)
                            dve.wait_ge(masked, UNITS * i + u + 1)
                            nc.vector.tensor_scalar(SHIFT[:, u:u + 1], TOP[:, u:u + 1], -SCALE, None, ALU.mult).then_inc(shift_done, 1)
                        if 1 <= s <= UNITS:
                            u = s - 1
                            h, t = divmod(u, NT)
                            dve.wait_ge(exp_done, UNITS * i + u + 1)
                            nc.vector.tensor_tensor_reduce(out=PROB[u % 3][:, :], in0=PROB[u % 3][:, :], in1=k.A16[:, t, :], scale=1.0,
                                                           scalar=0.0, op0=ALU.mult, op1=ALU.add,
                                                           accum_out=DEN[:, h, t:t + 1]).then_inc(weighted, 1)
                        if s >= 4:
                            u = s - 4
                            h, t = divmod(u, NT)
                            dve.wait_ge(msg_mm, UNITS * i + u + 1)
                            nc.vector.tensor_copy(MSG[:, t, h, :], out_bank[u % 2][0:TP, 0:DK]).then_inc(msg_copied, 1)
                    dve.wait_ge(weighted, UNITS * i + UNITS)
                    nc.vector.tensor_scalar(DEN[:, :, :], DEN[:, :, :], 1e-30, None, ALU.max).then_inc(den_done, 1)
                    dve.wait_ge(den_done, 2 * i + 1)
                    nc.vector.reciprocal(DEN[:, :, :], DEN[:, :, :]).then_inc(den_done, 1)
                    dve.wait_ge(den_done, 2 * i + 2)
                    dve.wait_ge(msg_copied, UNITS * i + UNITS)
                    for h in range(2):
                        nc.vector.tensor_tensor(MSG[:, :, h, :], MSG[:, :, h, :], DEN[:, h, :].unsqueeze(2).to_broadcast([TP, NT, DK]),
                                                ALU.mult).then_inc(msg_done, 1)
                    for t in range(NT):
                        dve.wait_ge(ff_mm, NT * i + NT + t + 1)
                        nc.vector.tensor_tensor(k.X[:, t, :], k.X[:, t, :], bank(t % 3)[0:TP, :], ALU.add).then_inc(ff_added, 1)
                    dve.wait_ge(ff_added, NT * i + NT + 3)

            @block.scalar
            def _(act):
                normalise_rows_scalar(nc, k, act, norm)
                turn_rows_scalar(nc, k, act, turn_banks, turned, taken)
                with act.Fori(0, PAIRS) as i:
                    act.wait_ge(wff_in, 48 * i + 48)
                    for j, T in enumerate((QT, KT)):
                        for g, (c0, w) in enumerate(SPANS):
                            act.wait_ge(proj_mm, 9 * i + 9 + 3 * j + g + 1)
                            nc.scalar.activation(T[:, c0:c0 + w], bank(3 * j + g)[:, 0:w], ACT.Identity, bias=BQK[:, j:j + 1]).then_inc(qk_done, 1)
                    for s in range(UNITS + 2):
                        if s < UNITS:
                            u = s
                            act.wait_ge(shift_done, UNITS * i + u + 1)
                            if u >= 3:
                                act.wait_ge(prob_turned, 3 * (UNITS * i + u - 2))
                            nc.scalar.activation(PROB[u % 3][:, :], MASKED[u % 2][:, :], ACT.Exp, bias=SHIFT[:, u:u + 1],
                                                 scale=SCALE).then_inc(exp_done, 1)
                        if s >= 2:
                            u = s - 2
                            if u >= 2:
                                act.wait_ge(msg_mm, UNITS * i + u - 1)
                            for g, (t0, n) in enumerate(GROUPS):
                                act.wait_ge(prob_turned, 3 * (UNITS * i + u) + g + 1)
                                nc.scalar.activation(PROBT[u % 2][:, t0:t0 + n, :], turn[0:TP, g, 0:n * TP].rearrange("p (t n) -> p t n", n=TP),
                                                     ACT.Copy).then_inc(prob_copied, 1)
                    for g, (t0, n) in enumerate(GROUPS):
                        act.wait_ge(msg_turned, 3 * i + g + 1)
                        nc.scalar.activation(MSGT[:, t0 * TP:(t0 + n) * TP], turn[:, g, 0:n * TP], ACT.Copy).then_inc(msgt_copied, 1)

            @block.tensor
            def _(pe):
                turn_rows_tensor(nc, k, pe, turn_banks, rows_done, turned, taken)
                pe.wait_ge(taken, NT)
                pe.sem_inc(proj_mm, 9)
                pe.sem_inc(ff_mm, NT)
                with pe.Fori(0, PAIRS) as i:
                    pe.wait_ge(wqkv_in, 48 * i + 48)
                    pe.wait_ge(ff_added, NT * i + 3)
                    for j in range(2):
                        for g, (c0, w) in enumerate(SPANS):
                            for c in range(DC):
                                last = nc.tensor.matmul(bank(3 * j + g)[:, 0:w], WQKV[:, j, c, :], k.XT[:, c, c0:c0 + w],
                                                        start=c == 0, stop=c == DC - 1)
                            last.then_inc(proj_mm, 1)
                    for g, (t0, n) in enumerate(GROUPS):
                        pe.wait_ge(qk_done, 6 * i + g + 1)
                        for t in range(n):
                            for c in range(DC):
                                last = nc.tensor.matmul(bank(g)[0:TP, 128 * t:128 * (t + 1)], k.XT[:, c, (t0 + t) * TP:(t0 + t + 1) * TP],
                                                        WQKV[:, 2, c, :], start=c == 0, stop=c == DC - 1)
                        last.then_inc(proj_mm, 1)
                    for s in range(UNITS + 3):
                        if s < UNITS:
                            u = s
                            h, t = divmod(u, NT)
                            if u == 0:
                                pe.wait_ge(qk_done, 6 * i + 6)
                                pe.wait_ge(v_done, 3 * i + 3)
                            else:
                                pe.wait_ge(masked, UNITS * i + u)
                            for c0, w in SPANS:
                                col = c0 * 256 // 250
                                last = nc.tensor.matmul(blocks5(score[0:TP, col:col + w * 256 // 250]),
                                                        QT[h * DK:(h + 1) * DK, t * TP:(t + 1) * TP],
                                                        five(KT[h * DK:(h + 1) * DK, c0:c0 + w]), start=True, stop=True)
                            last.then_inc(score_mm, 1)
                        if 2 <= s < UNITS + 2:
                            u = s - 2
                            pe.wait_ge(weighted, UNITS * i + u + 1)
                            for g, (t0, n) in enumerate(GROUPS):
                                if u:
                                    pe.wait_ge(prob_copied, 3 * (UNITS * i + u - 1) + g + 1)
                                for t in range(n):
                                    last = nc.tensor.transpose(turn[0:TP, g, t * TP:(t + 1) * TP],
                                                               PROB[u % 3][:, (t0 + t) * TP:(t0 + t + 1) * TP], k.IDENT[0:TP, 0:TP])
                                last.then_inc(prob_turned, 1)
                        if s >= 3:
                            u = s - 3
                            h, t = divmod(u, NT)
                            pe.wait_ge(prob_copied, 3 * (UNITS * i + u) + 3)
                            if u >= 2:
                                pe.wait_ge(msg_copied, UNITS * i + u - 1)
                            for q in range(NT):
                                last = nc.tensor.matmul(out_bank[u % 2][0:TP, 0:DK], PROBT[u % 2][:, q, :],
                                                        V[:, q, h * DK:(h + 1) * DK], start=q == 0, stop=q == NT - 1)
                            last.then_inc(msg_mm, 1)
                    pe.wait_ge(msg_done, 2 * i + 2)
                    for g, (t0, n) in enumerate(GROUPS):
                        for t in range(n):
                            last = nc.tensor.transpose(turn[:, g, t * TP:(t + 1) * TP],
                                                       MSG[:, t0 + t, :, :].rearrange("p h c -> p (h c)"), k.IDENT[0:TP, 0:TP])
                        last.then_inc(msg_turned, 1)
                    pe.wait_ge(wff_in, 48 * i + 48)
                    for t in range(NT):
                        if t % 4 == 0:
                            pe.wait_ge(msgt_copied, 3 * i + t // 4 + 1)
                        if t >= 3:
                            pe.wait_ge(ff_added, NT * i + t - 2 + 3)
                        nc.tensor.matmul(bank(t % 3)[0:TP, :], MSGT[:, t * TP:(t + 1) * TP], WFF[:, :], start=True, stop=True).then_inc(ff_mm, 1)
                pe.wait_ge(ff_added, NT * PAIRS + 3)


def feedforward_stage(nc, k, d):
    ctx = ExitStack()
    sb = lambda n, s, t: ctx.enter_context(nc.sbuf_tensor(n, s, t))
    pb = lambda n, s, t: ctx.enter_context(nc.psum_tensor(n, s, t))
    sem = lambda n: ctx.enter_context(nc.semaphore(n))
    HC = H2 // 128
    GE = G2 + R2
    with ctx:
        WIN = [sb(f"WIN{p}", [128, 2, DC, 128], F32) for p in range(2)]
        WOUT = [sb(f"WOUT{p}", [128, HC, D], F32) for p in range(2)]
        HID = sb("HID2", [128, HC, N], F32)
        SILU = [sb(f"SILU{p}", [128, 500], F32) for p in range(2)]
        ROW = sb("ROW2", [TP, 3, D], F32)
        GW = sb("GW", [128, DC, GE], F32)
        GB = sb("GB", [TP, GE], F32)
        EB = sb("EB", [R2, D], F32)
        LG = sb("LG2", [TP, NT, GE], F32)
        BEST = sb("BEST", [TP, 3, NT], F32)
        P4 = sb("P4", [TP, 4, NT, EG2], F32)
        COL = sb("COL2", [TP, 3, NT], F32)
        RANK = sb("RANK2", [TP, NT, EG2], F32)
        BEAT = sb("BEAT2", [TP, 2, NT, EG2 * EG2], F32)
        LOWER = sb("LOWER2", [TP, EG2, EG2], F32)
        GATE = sb("GATE2", [TP, NT, R2], F32)
        CNT = sb("CNT", [TP, NT, R2], F32)
        CT = sb("CT", [R2, N], F32)
        bank = [pb(f"fbank{i}", [128, 512], F32) for i in range(8)]
        norm, norm2 = norm_semaphores(sem, "f"), norm_semaphores(sem, "f2")
        rows1, rows2, scaled_rows, rows_done = sem("f_rows1"), sem("f_rows2"), sem("f_scaled"), sem("f_rows_done")
        turned, taken = sem("f_turned"), sem("f_taken")
        small_in, lower_done, lower_half, logit_mm = sem("f_small_in"), sem("f_lower"), sem("f_lower_half"), sem("f_logit_mm")
        win_in = [sem(f"win_in{p}") for p in range(2)]
        wout_in = [sem(f"wout_in{p}") for p in range(2)]
        vs, exped, gates, shared_bias = sem("f_vs"), sem("f_exped"), sem("f_gates"), sem("shared_bias")
        cnt_turned, cnt_copied, cb_mm, cb_added = sem("cnt_turned"), sem("cnt_copied"), sem("cb_mm"), sem("cb_added")
        in_mm, silu_done, hid_done, y_mm, y_added = sem("in_mm"), sem("silu_done"), sem("f_hid_done"), sem("f_y_mm"), sem("f_y_added")
        stored = sem("stored")
        winv = d["in_w"].rearrange("w (c p) (s j q) -> w j p s c q", p=128, s=2, q=128)
        woutv = d["out_w"].rearrange("e (j p) f -> e p j f", p=128)

        with nc.Block() as block:
            @block.sync
            def _(sp):
                for j, row in enumerate((d["ln_scale"], d["ln_bias"], d["shared_out_b"])):
                    sp.dma_start(ROW[:, j, :], row.rearrange("(a n) -> a n", a=1).to_broadcast([TP, D])).then_inc(small_in, 16)
                sp.dma_start(GW[:, :, :], d["gate_w"].rearrange("(c p) e -> p c e", p=128)).then_inc(small_in, 16)
                sp.dma_start(GB[:, :], d["gate_b"].rearrange("(a n) -> a n", a=1).to_broadcast([TP, GE])).then_inc(small_in, 16)
                sp.dma_start(EB[:, :], d["expert_out_b"]).then_inc(small_in, 16)
                sp.dma_start(WOUT[0][:, :, :], woutv[0]).then_inc(wout_in[0], 16)
                for part in range(2):
                    for j in range(HC):
                        n, p = HC * part + j, j % 2
                        if n >= 2:
                            sp.wait_ge(in_mm, 6 * (n - 1))
                        for s in range(2):
                            sp.dma_start(WIN[p][:, s, :, :], winv[part, j, :, s]).then_inc(win_in[p], 16)
                with sp.Fori(0, R2 // 2) as u:
                    for p in range(2):
                        sp.wait_ge(y_mm, NT * (2 * u + p + 1))
                        sp.dma_start(WOUT[1 - p][:, :, :], woutv[bass.ds(2 * u + p + 1, 1)].rearrange("o p j f -> p (o j) f")).then_inc(wout_in[1 - p], 16)
                for t in range(NT):
                    sp.wait_ge(y_added, NT * R2 + t + 1 + 4)
                    sp.dma_start(d["out"][t * TP:(t + 1) * TP, :], k.X[:, t, :]).then_inc(stored, 16)
                sp.wait_ge(stored, 16 * NT)

            @block.gpsimd
            def _(pool):
                pool.memset(LOWER[:, :, :], 1.0).then_inc(lower_done, 1)
                pool.wait_ge(lower_done, 1)
                pool.affine_select(out=LOWER[:, :, :], in_=LOWER[:, :, :], compare_op=ALU.is_gt, fill=0.0, base=0,
                                   pattern=[[1, EG2], [-1, EG2]], channel_multiplier=0).then_inc(lower_done, 1)
                pool.wait_ge(small_in, 96)
                pool.wait_ge(rows1, NT)
                for t in range(NT):
                    pool.tensor_tensor(k.X[:, t, :], k.X[:, t, :], ROW[:, 2, :], ALU.add).then_inc(shared_bias, 1)

            @block.vector
            def _(dve):
                normalise_rows_vector(nc, k, dve, k.X, k.XN, norm, rows1)
                dve.wait_ge(rows1, NT)
                normalise_rows_vector(nc, k, dve, k.XN, k.XN, norm2, rows2)
                dve.wait_ge(small_in, 96)
                for t in range(NT):
                    dve.wait_ge(rows2, t + 1)
                    nc.vector.tensor_tensor(k.XN[:, t, :], k.XN[:, t, :], ROW[:, 0, :], ALU.mult).then_inc(scaled_rows, 1)
                for t in range(NT):
                    dve.wait_ge(scaled_rows, t + 1)
                    nc.vector.tensor_tensor(k.XN[:, t, :], k.XN[:, t, :], ROW[:, 1, :], ALU.add).then_inc(rows_done, 1)
                n = [0]

                def chain(instruction):
                    n[0] += 1
                    instruction.then_inc(vs, 1)
                    dve.wait_ge(vs, n[0])

                dve.wait_ge(logit_mm, 1)
                chain(nc.vector.tensor_tensor(LG[:, :, :], bank[6][0:TP, 0:NT * GE].rearrange("p (t e) -> p t e", e=GE),
                                              GB[:, :].unsqueeze(1).to_broadcast([TP, NT, GE]), ALU.add))
                chain(nc.vector.tensor_tensor(BEST[:, 1, :], LG[:, :, 1], LG[:, :, 0], ALU.is_gt))
                chain(nc.vector.tensor_scalar(BEST[:, 0, :], BEST[:, 1, :], -1.0, 1.0, ALU.mult, ALU.add))
                for g in range(2):
                    chain(nc.vector.tensor_tensor(P4[:, g, :, :], LG[:, :, G2 + EG2 * g:G2 + EG2 * (g + 1)],
                                                  BEST[:, g, :].unsqueeze(2).to_broadcast([TP, NT, EG2]), ALU.mult))
                chain(nc.vector.tensor_tensor(P4[:, 2, :, :], P4[:, 0, :, :], P4[:, 1, :, :], ALU.add))
                chain(nc.vector.tensor_reduce(COL[:, 0, :], P4[:, 2, :, :], AX.X, ALU.max))
                chain(nc.vector.tensor_tensor(P4[:, 0, :, :], P4[:, 2, :, :], COL[:, 0, :].unsqueeze(2).to_broadcast([TP, NT, EG2]), ALU.subtract))
                dve.wait_ge(exped, 1)
                chain(nc.vector.tensor_reduce(COL[:, 0, :], P4[:, 1, :, :], AX.X, ALU.add))
                chain(nc.vector.reciprocal(COL[:, 1, :], COL[:, 0, :]))
                chain(nc.vector.tensor_tensor(P4[:, 2, :, :], P4[:, 1, :, :], COL[:, 1, :].unsqueeze(2).to_broadcast([TP, NT, EG2]), ALU.mult))
                dve.wait_ge(lower_done, 2)
                for t in range(NT):
                    mine = P4[:, 2, t, :].unsqueeze(2).to_broadcast([TP, EG2, EG2])
                    other = P4[:, 2, t, :].unsqueeze(1).to_broadcast([TP, EG2, EG2])
                    beat = BEAT[:, 0, t, :].rearrange("p (i j) -> p i j", j=EG2)
                    same = BEAT[:, 1, t, :].rearrange("p (i j) -> p i j", j=EG2)
                    nc.vector.tensor_tensor(beat, other, mine, ALU.is_gt).then_inc(lower_half, 1)
                    nc.vector.tensor_tensor(same, other, mine, ALU.is_equal).then_inc(lower_half, 1)
                dve.wait_ge(lower_half, 2 * NT)
                chain(nc.vector.tensor_tensor(BEAT[:, 1, :, :], BEAT[:, 1, :, :],
                                              LOWER[:, :, :].rearrange("p i j -> p (i j)").unsqueeze(1).to_broadcast([TP, NT, EG2 * EG2]), ALU.mult))
                chain(nc.vector.tensor_tensor(BEAT[:, 0, :, :], BEAT[:, 0, :, :], BEAT[:, 1, :, :], ALU.add))
                chain(nc.vector.tensor_reduce(RANK[:, :, :], BEAT[:, 0, :, :].rearrange("p t (i j) -> p t i j", j=EG2), AX.X, ALU.add))
                chain(nc.vector.tensor_scalar(RANK[:, :, :], RANK[:, :, :], TOP2 - 0.5, None, ALU.is_lt))
                chain(nc.vector.tensor_tensor(P4[:, 0, :, :], P4[:, 2, :, :], RANK[:, :, :], ALU.mult))
                chain(nc.vector.tensor_reduce(COL[:, 0, :], P4[:, 0, :, :], AX.X, ALU.add))
                chain(nc.vector.tensor_scalar(COL[:, 1, :], COL[:, 0, :], 1e-8, None, ALU.add))
                chain(nc.vector.reciprocal(COL[:, 2, :], COL[:, 1, :]))
                chain(nc.vector.tensor_tensor(P4[:, 3, :, :], P4[:, 0, :, :], COL[:, 2, :].unsqueeze(2).to_broadcast([TP, NT, EG2]), ALU.mult))
                for g in range(2):
                    best = BEST[:, g, :].unsqueeze(2).to_broadcast([TP, NT, EG2])
                    nc.vector.tensor_tensor(GATE[:, :, EG2 * g:EG2 * (g + 1)], P4[:, 3, :, :], best, ALU.mult).then_inc(gates, 1)
                    nc.vector.tensor_tensor(CNT[:, :, EG2 * g:EG2 * (g + 1)], RANK[:, :, :], best, ALU.mult).then_inc(gates, 1)
                dve.wait_ge(shared_bias, NT)
                for t in range(NT):
                    dve.wait_ge(cb_mm, t + 1)
                    nc.vector.tensor_tensor(k.X[:, t, :], k.X[:, t, :], bank[4 + t % 4][0:TP, :], ALU.add).then_inc(cb_added, 1)
                dve.wait_ge(cb_added, NT)
                dve.wait_ge(gates, 4)
                dve.sem_inc(y_added, 4)

                def hidden(part):
                    m = 3 * HC * part
                    for j in range(HC):
                        for c0, w in SPANS:
                            dve.wait_ge(silu_done, m + 1)
                            nc.vector.tensor_tensor(HID[:, j, c0:c0 + w], SILU[m % 2][:, 0:w], bank[2 * (m % 2) + 1][:, 0:w], ALU.mult).then_inc(hid_done, 1)
                            m += 1

                hidden(0)
                for t in range(NT):
                    dve.wait_ge(y_mm, NT + t + 1)
                    nc.vector.tensor_tensor(k.X[:, t, :], k.X[:, t, :], bank[4 + t % 4][0:TP, :], ALU.add).then_inc(y_added, 1)
                dve.wait_ge(y_added, NT + 4)
                hidden(1)
                with dve.Fori(0, R2 // 2) as u:
                    for m in range(2 * NT):
                        p, t = divmod(m, NT)
                        dve.wait_ge(y_mm, 2 * NT * (u + 1) + m + 1)
                        dve.wait_ge(y_added, NT + 2 * NT * u + m + 4)
                        nc.vector.scalar_tensor_tensor(out=k.X[:, t, :], in0=bank[4 + (m + 2) % 4][0:TP, :],
                                                       scalar=GATE[:, t, bass.ds(2 * u + p, 1)], in1=k.X[:, t, :],
                                                       op0=ALU.mult, op1=ALU.add).then_inc(y_added, 1)

            @block.scalar
            def _(act):
                normalise_rows_scalar(nc, k, act, norm)
                normalise_rows_scalar(nc, k, act, norm2)
                turn_rows_scalar(nc, k, act, bank[4:8], turned, taken)
                act.wait_ge(vs, 8)
                nc.scalar.activation(P4[:, 1, :, :], P4[:, 0, :, :], ACT.Exp).then_inc(exped, 1)
                for g, (t0, n) in enumerate(GROUPS):
                    act.wait_ge(cnt_turned, g + 1)
                    nc.scalar.activation(CT[:, t0 * TP:(t0 + n) * TP], bank[1 + g][0:R2, 0:n * TP], ACT.Copy).then_inc(cnt_copied, 1)
                for m in range(2 * 3 * HC):
                    w = SPANS[m % 3][1]
                    act.wait_ge(in_mm, 2 * m + 2)
                    if m >= 2:
                        act.wait_ge(hid_done, m - 1)
                    nc.scalar.activation(SILU[m % 2][:, 0:w], bank[2 * (m % 2)][:, 0:w], ACT.Silu).then_inc(silu_done, 1)

            @block.tensor
            def _(pe):
                pe.sem_inc(y_mm, NT)
                turn_rows_tensor(nc, k, pe, bank[4:8], rows_done, turned, taken)
                pe.wait_ge(taken, NT)
                pe.wait_ge(small_in, 96)
                for t in range(NT):
                    for c in range(DC):
                        last = nc.tensor.matmul(bank[6][0:TP, t * GE:(t + 1) * GE], k.XT[:, c, t * TP:(t + 1) * TP], GW[:, c, :],
                                                start=c == 0, stop=c == DC - 1)
                last.then_inc(logit_mm, 1)
                pe.wait_ge(gates, 4)
                for g, (t0, n) in enumerate(GROUPS):
                    for t in range(n):
                        last = nc.tensor.transpose(bank[1 + g][0:R2, t * TP:(t + 1) * TP], CNT[:, t0 + t, :], k.IDENT[0:TP, 0:TP])
                    last.then_inc(cnt_turned, 1)
                pe.wait_ge(cnt_copied, 3)
                for t in range(NT):
                    if t >= 4:
                        pe.wait_ge(cb_added, t - 3)
                    nc.tensor.matmul(bank[4 + t % 4][0:TP, :], CT[:, t * TP:(t + 1) * TP], EB[:, :], start=True, stop=True).then_inc(cb_mm, 1)
                pe.wait_ge(cb_added, NT)

                def hidden(part):
                    m = 3 * HC * part
                    for j in range(HC):
                        n = HC * part + j
                        pe.wait_ge(win_in[j % 2], 32 * (n // 2 + 1))
                        for c0, w in SPANS:
                            if m >= 2:
                                pe.wait_ge(hid_done, m - 1)
                            for s in range(2):
                                for c in range(DC):
                                    last = nc.tensor.matmul(bank[2 * (m % 2) + s][:, 0:w], WIN[j % 2][:, s, c, :], k.XT[:, c, c0:c0 + w],
                                                            start=c == 0, stop=c == DC - 1)
                                last.then_inc(in_mm, 1)
                            m += 1

                hidden(0)
                pe.wait_ge(wout_in[0], 16)
                pe.wait_ge(hid_done, 3 * HC)
                for t in range(NT):
                    if t >= 4:
                        pe.wait_ge(y_added, t - 3 + 4)
                    for j in range(HC):
                        last = nc.tensor.matmul(bank[4 + t % 4][0:TP, :], HID[:, j, t * TP:(t + 1) * TP], WOUT[0][:, j, :],
                                                start=j == 0, stop=j == HC - 1)
                    last.then_inc(y_mm, 1)
                hidden(1)
                pe.wait_ge(hid_done, 2 * 3 * HC)
                with pe.Fori(0, R2 // 2) as u:
                    for m in range(2 * NT):
                        p, t = divmod(m, NT)
                        if t == 0:
                            pe.wait_ge(wout_in[1 - p], 16 * u + 16 + (16 if p == 1 else 0))
                        pe.wait_ge(y_added, NT + 2 * NT * u + m + 1)
                        for j in range(HC):
                            last = nc.tensor.matmul(bank[4 + (m + 2) % 4][0:TP, :], HID[:, j, t * TP:(t + 1) * TP], WOUT[1 - p][:, j, :],
                                                    start=j == 0, stop=j == HC - 1)
                        last.then_inc(y_mm, 1)


def finish_stage(nc, k, d):
    with nc.semaphore("stored") as stored, nc.Block() as block:
        @block.sync
        def _(sp):
            sp.dma_start(d["out"].rearrange("(t p) c -> p t c", p=TP), k.X[:, :, :]).then_inc(stored, 16)
            sp.wait_ge(stored, 16)


def program(nc, d):
    with ExitStack() as ctx:
        sb = lambda n, s, t: ctx.enter_context(nc.sbuf_tensor(n, s, t))
        k = OnChip()
        k.X = sb("X", [TP, NT, D], F32)
        k.XN = sb("XN", [TP, NT, D], F32)
        k.XT = sb("XT", [128, DC, N], F32)
        k.IDENT = sb("IDENT", [128, 128], F32)
        k.ONES = sb("ONES", [128, 128], F32)
        k.EPSC = sb("EPSC", [128, 1], F32)
        k.STATS = sb("STATS", [TP, NT, 6], F32)
        k.MV = sb("MV", [TP, NT, 2], F32)
        k.STD = sb("STD", [TP, NT], F32)
        k.RSTD = sb("RSTD", [TP, NT], F32)
        k.x_in = ctx.enter_context(nc.semaphore("x_in"))
        k.gnn_w_in = ctx.enter_context(nc.semaphore("gnn_w_in"))
        stop = d.get("stop", 4)
        with ExitStack() as graph:
            k.A16 = graph.enter_context(nc.sbuf_tensor("A16", [TP, NT, N], U16))
            k.M = graph.enter_context(nc.sbuf_tensor("M", [TP, NT, N], BF16))
            with ExitStack() as gnn:
                k.AT = gnn.enter_context(nc.sbuf_tensor("AT", [TP, NT, N], F32))
                k.WT = gnn.enter_context(nc.sbuf_tensor("WT", [128, DC, D], F32))
                k.ROWS = gnn.enter_context(nc.sbuf_tensor("ROWS", [TP, 3, D], F32))
                adjacency_stage(nc, k, d)
                graph_stage(nc, k, d)
            if stop == 1:
                return finish_stage(nc, k, d)
            mixture_stage(nc, k, d)
            if stop == 2:
                return finish_stage(nc, k, d)
            attention_stage(nc, k, d)
            if stop == 3:
                return finish_stage(nc, k, d)
        feedforward_stage(nc, k, d)


def layout(nc, inputs):
    arrays = {
        "x": inputs["x"], "src": inputs["src"], "dst": inputs["dst"],
        "gnn_w": inputs["L0_gnn_W"].T, "gnn_b": inputs["L0_gnn_b"],
        "gnn_gamma": inputs["L0_gnn_gamma"], "gnn_beta": inputs["L0_gnn_beta"],
        "router_w": inputs["L0_ffn_router_w"], "router_b": inputs["L0_ffn_router_b"],
        "w1": inputs["L0_ffn_w1"], "b1": inputs["L0_ffn_b1"].reshape(R1, H1 // 128, 128).transpose(0, 2, 1).reshape(R1, H1),
        "w2": inputs["L0_ffn_w2"], "b2": inputs["L0_ffn_b2"],
    }
    bqkv = inputs["L1_gnn_b_qkv"].reshape(3, HEADS // 2, 128)
    arrays |= {
        "qkv_w": inputs["L1_gnn_W_qkv"].T, "ff_w": inputs["L1_gnn_W_ff"].T, "ff_b": inputs["L1_gnn_b_ff"],
        "qk_b": bqkv[0:2].transpose(1, 2, 0).reshape(HEADS // 2, 256), "v_b": bqkv[2],
    }
    rows = lambda w: w.T[None]
    arrays |= {
        "in_w": np.concatenate([rows(inputs["L1_ffn_shared_in_w"]), rows(inputs["L1_ffn_expert_in_w"])]),
        "out_w": np.concatenate([rows(inputs["L1_ffn_shared_out_w"]), inputs["L1_ffn_expert_out_weight"].transpose(0, 2, 1)]),
        "gate_w": np.concatenate([inputs["L1_ffn_group_gate_w"], inputs["L1_ffn_expert_gate_w"]]).T,
        "gate_b": np.concatenate([inputs["L1_ffn_group_bias"], inputs["L1_ffn_expert_bias"]]),
        "shared_out_b": inputs["L1_ffn_shared_out_b"], "expert_out_b": inputs["L1_ffn_expert_out_bias"],
        "ln_scale": inputs["L1_ffn_ln_scale"], "ln_bias": inputs["L1_ffn_ln_bias"],
    }
    d = {}
    for name, a in arrays.items():
        arrays[name] = a = np.ascontiguousarray(a)
        d[name] = nc.dram_tensor(name, a.shape, mybir.dt.from_np(a.dtype), kind="ExternalInput").ap()
    d["out"] = nc.dram_tensor("out", (N, D), F32, kind="ExternalOutput").ap()
    return arrays, d


def kernel(**inputs):
    import numpy as _np
    import concourse.bacc as _bacc
    from concourse.bass_utils import run_bass_kernel_spmd as _run

    nc = _bacc.Bacc("TRN2", target_bir_lowering=False, num_devices=1)
    arrays, d = layout(nc, {name: _np.asarray(a) for name, a in inputs.items()})
    program(nc, d)
    r = _run(nc, [arrays], core_ids=[0])
    return r.results[0]["out"]
```

```python
import numpy as np
import concourse.bass as bass
from concourse import mybir
from contextlib import ExitStack

F32 = mybir.dt.float32
BF16 = mybir.dt.bfloat16
F16 = mybir.dt.float16
U16 = mybir.dt.uint16
I32 = mybir.dt.int32
ALU = mybir.AluOpType
ACT = mybir.ActivationFunctionType
AX = mybir.AxisListType

N = 1250
D = 512
E = 20000
TP = 125
NT = N // TP
ET = E // TP
DC = D // 128
SPANS = [(0, 500), (500, 500), (1000, 250)]
GROUPS = [(0, 4), (4, 4), (8, 2)]
EPS = 1e-5
NEG = -1.0e30

R1, H1 = 16, 256
TOP1 = 4
HEADS, DK = 8, 64
H2 = 1024
G2, EG2 = 2, 4
R2 = G2 * EG2
TOP2 = 2


class OnChip:
    pass


def blocks5(ap):
    return ap.rearrange("p (a b) -> p a b", b=256)[:, :, 0:250]


def five(ap):
    return ap.rearrange("p (a b) -> p a b", b=250)


def adjacency_stage(nc, k, d):
    ctx = ExitStack()
    sb = lambda n, s, t: ctx.enter_context(nc.sbuf_tensor(n, s, t))
    pb = lambda n, s, t: ctx.enter_context(nc.psum_tensor(n, s, t))
    sem = lambda n: nc.alloc_semaphore(name=n)
    HALF = ET // 2
    with ctx:
        edges_i = sb("edges_i", [HALF, 2, 2, TP], I32)
        edges_f = sb("edges_f", [HALF, 2, 2, TP], F32)
        bounds_q = sb("bounds_q", [HALF, 2, 2], F32)
        spread = sb("spread", [HALF, 2, 2, HALF], F32)
        src_e = sb("src_e", [TP, ET], F32)
        dst_e = sb("dst_e", [TP, ET], F32)
        nodes_i = sb("nodes_i", [TP, N], I32)
        nodes = sb("nodes", [TP, N], F16)
        tile_up_i = sb("tile_up_i", [NT, ET], I32)
        tile_up = sb("tile_up", [NT, ET], F32)
        tile_down = sb("tile_down", [NT, ET], F32)
        first_i = sb("first_i", [NT, 1], I32)
        first = sb("first", [NT, 2], F32)
        ones_q = sb("ones_q", [HALF, NT], F32)
        before = sb("before", [NT, NT], F32)
        touch = sb("touch", [NT, 3, ET], F32)
        reach = sb("reach", [NT, 6], F32)
        table_i = sb("table_i", [NT, 3], I32)
        table = sb("table", [1, 3 * NT], I32)
        RING = 4
        hot_src = sb("hot_src", [TP, RING * N], BF16)
        hot_dst = sb("hot_dst", [TP, RING * TP], BF16)
        zeros = sb("zeros", [TP, 500], BF16)
        counts = [k.XN[:, :, :].rearrange("p t c -> p (t c)")[:, p * N:(p + 1) * N] for p in range(2)]
        pA = [pb(f"pA{p}", [128, 1536], F32) for p in range(2)]
        pT = [pb(f"pT{p}", [128, 512], F32) for p in range(2)]

        edges_in = sem("edges_in")
        table_in = sem("table_in")
        iota_done = sem("iota_done")
        consts_done = sem("consts_done")
        cast_done = sem("cast_done")
        ident_done = sem("ident_done")
        edges_turned = sem("edges_turned")
        edges_copied = sem("edges_copied")
        step = sem("step")
        spread_done = sem("spread_done")
        bounds_mm = sem("bounds_mm")
        reach_done = sem("reach_done")
        prefix_mm = sem("prefix_mm")
        table_done = sem("table_done")
        hot_ready = sem("hot_ready")
        hot_used = sem("hot_used")
        block_mm = sem("block_mm")
        counts_copied = sem("counts_copied")
        block_taken = sem("block_taken")
        turned = sem("turned")
        turned_copied = sem("turned_copied")

        with nc.Block() as block:
            @block.sync
            def _(sp):
                for j, e in enumerate((d["src"], d["dst"])):
                    sp.dma_start(edges_i[:, j, :, :], e.rearrange("(r q e) -> q r e", r=2, e=TP)).then_inc(edges_in, 16)
                sp.dma_start(k.X[:, :, :], d["x"].rearrange("(t p) c -> p t c", p=TP)).then_inc(k.x_in, 16)
                sp.dma_start(k.WT[:, :, :], d["gnn_w"].rearrange("(c p) f -> p c f", p=128)).then_inc(k.gnn_w_in, 16)
                for j, row in enumerate((d["gnn_b"], d["gnn_gamma"], d["gnn_beta"])):
                    sp.dma_start(k.ROWS[:, j, :], row.rearrange("(a n) -> a n", a=1).to_broadcast([TP, D])).then_inc(k.gnn_w_in, 16)
                sp.wait_ge(table_done, 1)
                for b in range(NT):
                    sp.dma_start(table[0:1, 3 * b:3 * b + 3], table_i[b:b + 1, :]).then_inc(table_in, 16)

            @block.gpsimd
            def _(pool):
                pool.iota(nodes_i[:, :], pattern=[[1, N]], base=0, channel_multiplier=0).then_inc(iota_done, 1)
                pool.iota(tile_up_i[:, :], pattern=[[1, ET]], base=1, channel_multiplier=0).then_inc(iota_done, 1)
                pool.iota(first_i[:, :], pattern=[[0, 1]], base=0, channel_multiplier=TP).then_inc(iota_done, 1)
                pool.memset(k.IDENT[:, :], 0.0).then_inc(consts_done, 1)
                pool.memset(before[:, :], 1.0).then_inc(consts_done, 1)
                pool.memset(ones_q[:, :], 1.0).then_inc(consts_done, 1)
                pool.memset(zeros[:, :], 0.0).then_inc(consts_done, 1)
                pool.memset(k.ONES[:, :], 1.0).then_inc(consts_done, 1)
                pool.memset(k.EPSC[:, :], EPS).then_inc(consts_done, 1)
                pool.wait_ge(consts_done, 6)
                pool.affine_select(out=k.IDENT[:, :], in_=k.IDENT[:, :], compare_op=ALU.not_equal, fill=1.0,
                                   base=0, pattern=[[-1, 128]], channel_multiplier=1).then_inc(ident_done, 1)
                pool.affine_select(out=before[:, :], in_=before[:, :], compare_op=ALU.is_gt, fill=0.0,
                                   base=0, pattern=[[1, NT]], channel_multiplier=-1).then_inc(ident_done, 1)

            @block.vector
            def _(dve):
                dve.wait_ge(edges_in, 32)
                nc.vector.tensor_copy(edges_f[:, :, :, :], edges_i[:, :, :, :]).then_inc(cast_done, 1)
                dve.wait_ge(iota_done, 3)
                nc.vector.tensor_copy(nodes[:, :], nodes_i[:, :]).then_inc(cast_done, 1)
                nc.vector.tensor_copy(tile_up[:, :], tile_up_i[:, :]).then_inc(step, 1)
                nc.vector.tensor_copy(first[:, 0:1], first_i[:, :]).then_inc(step, 1)
                dve.wait_ge(cast_done, 1)
                nc.vector.tensor_reduce(bounds_q[:, 0, :], edges_f[:, 1, :, :], AX.X, ALU.min).then_inc(step, 1)
                nc.vector.tensor_reduce(bounds_q[:, 1, :], edges_f[:, 1, :, :], AX.X, ALU.max).then_inc(step, 1)
                dve.wait_ge(step, 4)
                nc.vector.tensor_scalar(tile_down[:, :], tile_up[:, :], -1.0, float(ET + 1), ALU.mult, ALU.add).then_inc(step, 1)
                nc.vector.tensor_scalar(first[:, 1:2], first[:, 0:1], float(TP - 1), None, ALU.add).then_inc(step, 1)
                dve.wait_ge(ident_done, 1)
                for m in range(2):
                    for r in range(2):
                        nc.vector.tensor_scalar(spread[:, m, r, :], k.IDENT[0:HALF, 0:HALF], bounds_q[:, m, r:r + 1], None,
                                                ALU.mult).then_inc(spread_done, 1)
                dve.wait_ge(edges_turned, 1)
                nc.vector.tensor_copy(src_e[:, :], pT[0][0:TP, 0:ET]).then_inc(edges_copied, 1)
                nc.vector.tensor_copy(dst_e[:, :], pT[0][0:TP, 256:256 + ET]).then_inc(edges_copied, 1)
                dve.wait_ge(bounds_mm, 1)
                dve.wait_ge(step, 6)
                nc.vector.tensor_scalar(touch[:, 0, :], pT[1][0:NT, 0:ET], first[:, 1:2], None, ALU.is_le).then_inc(step, 1)
                nc.vector.tensor_scalar(touch[:, 1, :], pT[1][0:NT, 256:256 + ET], first[:, 0:1], None, ALU.is_ge).then_inc(step, 1)
                dve.wait_ge(step, 8)
                nc.vector.tensor_tensor(touch[:, 2, :], touch[:, 0, :], touch[:, 1, :], ALU.mult).then_inc(step, 1)
                dve.wait_ge(step, 9)
                nc.vector.tensor_tensor(touch[:, 0, :], touch[:, 2, :], tile_down[:, :], ALU.mult).then_inc(step, 1)
                nc.vector.tensor_tensor(touch[:, 1, :], touch[:, 2, :], tile_up[:, :], ALU.mult).then_inc(step, 1)
                dve.wait_ge(step, 11)
                nc.vector.tensor_reduce(reach[:, 0:2], touch[:, 0:2, :], AX.X, ALU.max).then_inc(step, 1)
                dve.wait_ge(step, 12)
                nc.vector.tensor_scalar(reach[:, 2:3], reach[:, 0:1], -1.0, float(ET), ALU.mult, ALU.add).then_inc(step, 1)
                dve.wait_ge(step, 13)
                nc.vector.tensor_scalar(reach[:, 2:3], reach[:, 2:3], float(ET - 1), None, ALU.min).then_inc(step, 1)
                dve.wait_ge(step, 14)
                nc.vector.tensor_tensor(reach[:, 3:4], reach[:, 1:2], reach[:, 2:3], ALU.subtract).then_inc(step, 1)
                dve.wait_ge(step, 15)
                nc.vector.tensor_scalar(reach[:, 3:4], reach[:, 3:4], 1.0, None, ALU.max).then_inc(reach_done, 1)
                dve.wait_ge(reach_done, 1)
                nc.vector.tensor_tensor(reach[:, 4:5], reach[:, 2:3], reach[:, 3:4], ALU.add).then_inc(step, 1)
                dve.wait_ge(prefix_mm, 1)
                nc.vector.tensor_tensor(reach[:, 5:6], pT[0][0:NT, 510:511], reach[:, 2:3], ALU.subtract).then_inc(step, 1)
                dve.wait_ge(step, 17)
                nc.vector.tensor_scalar(reach[:, 5:6], reach[:, 5:6], float(ET), None, ALU.add).then_inc(step, 1)
                nc.vector.tensor_copy(table_i[:, 0:1], reach[:, 2:3]).then_inc(step, 1)
                nc.vector.tensor_copy(table_i[:, 1:2], reach[:, 4:5]).then_inc(step, 1)
                dve.wait_ge(step, 20)
                nc.vector.tensor_copy(table_i[:, 2:3], reach[:, 5:6]).then_inc(table_done, 1)
                dve.wait_ge(edges_copied, 2)
                dve.wait_ge(cast_done, 2)
                dve.wait_ge(table_in, 16 * NT)
                dve.sem_inc(hot_ready, ET)
                with dve.Fori(0, NT) as b:
                    lo = dve.value_load(table[0:1, bass.ds(3 * b, 1)], min_val=0, max_val=ET - 1)
                    hi = dve.value_load(table[0:1, bass.ds(3 * b + 1, 1)], min_val=1, max_val=ET)
                    off = dve.value_load(table[0:1, bass.ds(3 * b + 2, 1)], min_val=1, max_val=NT * ET)
                    with dve.Fori(lo, hi) as t:
                        s = dve.snap((off + t) % RING)
                        dve.wait_ge(hot_used, off + t + 1)
                        nc.vector.tensor_scalar(hot_dst[:, bass.ds(s * TP, TP)], nodes[:, bass.ds(b * TP, TP)],
                                                dst_e[:, bass.ds(t, 1)], None, ALU.is_equal)
                        nc.vector.tensor_scalar(hot_src[:, bass.ds(s * N, N)], nodes[:, :],
                                                src_e[:, bass.ds(t, 1)], None, ALU.is_equal).then_inc(hot_ready, 1)
                dve.wait_ge(block_taken, NT + 2)
                nc.vector.tensor_scalar(k.M[:, :, :], k.A16[:, :, :], 0.0, NEG, ALU.is_equal, ALU.mult).then_inc(step, 1)
                dve.wait_ge(turned_copied, 3 * NT + 2)
                for t in range(NT):
                    nc.vector.tensor_tensor(k.AT[:, t, t * TP:(t + 1) * TP], k.AT[:, t, t * TP:(t + 1) * TP],
                                            k.IDENT[0:TP, 0:TP], ALU.add).then_inc(step, 1)

            @block.tensor
            def _(pe):
                pe.wait_ge(ident_done, 2)
                pe.wait_ge(cast_done, 1)
                for j in range(2):
                    for r in range(2):
                        last = nc.tensor.transpose(pT[0][0:TP, 256 * j + HALF * r:256 * j + HALF * (r + 1)],
                                                   edges_f[:, j, r, :], k.IDENT[0:HALF, 0:HALF])
                last.then_inc(edges_turned, 1)
                pe.wait_ge(spread_done, 4)
                for m in range(2):
                    last = nc.tensor.matmul(pT[1][0:NT, 256 * m:256 * m + ET], ones_q[:, :],
                                            spread[:, m, :, :].rearrange("p r q -> p (r q)"), start=True, stop=True)
                last.then_inc(bounds_mm, 1)
                pe.wait_ge(reach_done, 1)
                pe.wait_ge(edges_copied, 2)
                nc.tensor.matmul(pT[0][0:NT, 510:511], before[:, :], reach[:, 3:4], start=True, stop=True).then_inc(prefix_mm, 1)
                pe.wait_ge(table_in, 16 * NT)
                pe.sem_inc(hot_used, ET + RING)
                with pe.Fori(0, NT // 2) as u:
                    for p in range(2):
                        b = 2 * u + p
                        lo = pe.value_load(table[0:1, bass.ds(3 * b, 1)], min_val=0, max_val=ET - 1)
                        hi = pe.value_load(table[0:1, bass.ds(3 * b + 1, 1)], min_val=1, max_val=ET)
                        off = pe.value_load(table[0:1, bass.ds(3 * b + 2, 1)], min_val=1, max_val=NT * ET)
                        pe.wait_ge(block_taken, 2 * u + p + 1)
                        for c0, w in SPANS:
                            out = pA[p][0:TP, c0 * 256 // 250:c0 * 256 // 250 + w * 256 // 250]
                            nc.tensor.matmul(out.rearrange("p (a b) -> p a b", b=256)[:, :, 0:250], zeros[:, 0:TP],
                                             zeros[:, 0:w].rearrange("p (a b) -> p a b", b=250), start=True, stop=False,
                                             skip_group_check=True)
                        with pe.Fori(lo, hi) as t:
                            s = pe.snap((off + t) % RING)
                            pe.wait_ge(hot_ready, off + t + 1)
                            for c0, w in SPANS:
                                out = pA[p][0:TP, c0 * 256 // 250:c0 * 256 // 250 + w * 256 // 250]
                                last = nc.tensor.matmul(out.rearrange("p (a b) -> p a b", b=256)[:, :, 0:250],
                                                        hot_dst[:, bass.ds(s * TP, TP)],
                                                        hot_src[:, bass.ds(s * N + c0, w)].rearrange("p (a b) -> p a b", b=250),
                                                        start=False, stop=False, skip_group_check=True)
                            last.then_inc(hot_used, 1)
                        for c0, w in SPANS:
                            out = pA[p][0:TP, c0 * 256 // 250:c0 * 256 // 250 + w * 256 // 250]
                            last = nc.tensor.matmul(out.rearrange("p (a b) -> p a b", b=256)[:, :, 0:250], zeros[:, 0:TP],
                                                    zeros[:, 0:w].rearrange("p (a b) -> p a b", b=250), start=False, stop=True,
                                                    skip_group_check=True)
                        last.then_inc(block_mm, 1)
                        pe.wait_ge(counts_copied, 2 * u + p + 1)
                        for g, (t0, n) in enumerate(GROUPS):
                            q = (3 * p + g) % 2
                            pe.wait_ge(turned_copied, 6 * u + 3 * p + g + 1)
                            for t in range(n):
                                last = nc.tensor.transpose(pT[q][0:TP, t * TP:(t + 1) * TP],
                                                           counts[p][:, (t0 + t) * TP:(t0 + t + 1) * TP], k.IDENT[0:TP, 0:TP])
                            last.then_inc(turned, 1)

            @block.scalar
            def _(act):
                act.sem_inc(block_taken, 2)
                act.wait_ge(table_in, 16 * NT)
                act.sem_inc(turned_copied, 2)
                with act.Fori(0, NT // 2) as u:
                    for p in range(2):
                        b = 2 * u + p
                        act.wait_ge(block_mm, 2 * u + p + 1)
                        nc.scalar.activation(five(counts[p]), blocks5(pA[p][0:TP, 0:1280]), ACT.Copy).then_inc(counts_copied, 1)
                        nc.scalar.activation(k.A16[:, bass.ds(b, 1), :].rearrange("p o (a b) -> p (o a) b", b=250),
                                             blocks5(pA[p][0:TP, 0:1280]), ACT.Copy).then_inc(block_taken, 1)
                        for g, (t0, n) in enumerate(GROUPS):
                            q = (3 * p + g) % 2
                            act.wait_ge(turned, 6 * u + 3 * p + g + 1)
                            nc.scalar.activation(k.AT[:, t0:t0 + n, bass.ds(b * TP, TP)],
                                                 pT[q][0:TP, 0:n * TP].rearrange("p (t n) -> p t n", n=TP),
                                                 ACT.Copy).then_inc(turned_copied, 1)



def normalise_rows_vector(nc, k, dve, src, dst, s, done):
    for t in range(NT):
        nc.vector.bn_stats(k.STATS[:, t, :], src[:, t, :]).then_inc(s.stats, 1)
    for t in range(NT):
        dve.wait_ge(s.stats, t + 1)
        nc.vector.bn_aggr(k.MV[:, t, :], k.STATS[:, t, :]).then_inc(s.moments, 1)
    dve.wait_ge(s.std, 1)
    nc.vector.reciprocal(k.RSTD[:, :], k.STD[:, :]).then_inc(s.rstd, 1)
    dve.wait_ge(s.rstd, 1)
    for t in range(NT):
        nc.vector.tensor_scalar(dst[:, t, :], src[:, t, :], k.MV[:, t, 0:1], k.RSTD[:, t:t + 1],
                                ALU.subtract, ALU.mult).then_inc(done, 1)


def normalise_rows_scalar(nc, k, act, s):
    act.wait_ge(s.moments, NT)
    nc.scalar.activation(k.STD[:, :], k.MV[:, :, 1], ACT.Sqrt, bias=k.EPSC[0:TP, 0:1]).then_inc(s.std, 1)


def turn_rows_tensor(nc, k, pe, banks, rows_done, turned, taken):
    for t in range(NT):
        pe.wait_ge(rows_done, t + 1)
        if t >= len(banks):
            pe.wait_ge(taken, t - len(banks) + 1)
        for c in range(DC):
            last = nc.tensor.transpose(banks[t % len(banks)][:, c * TP:(c + 1) * TP],
                                       k.XN[:, t, c * 128:(c + 1) * 128], k.IDENT[0:TP, 0:TP])
        last.then_inc(turned, 1)


def turn_rows_scalar(nc, k, act, banks, turned, taken):
    for t in range(NT):
        act.wait_ge(turned, t + 1)
        nc.scalar.activation(k.XT[:, :, t * TP:(t + 1) * TP],
                             banks[t % len(banks)][:, 0:DC * TP].rearrange("p (c n) -> p c n", n=TP),
                             ACT.Copy).then_inc(taken, 1)


def norm_semaphores(sem, name):
    s = OnChip()
    s.stats, s.moments, s.std, s.rstd = sem(name + "_stats"), sem(name + "_moments"), sem(name + "_std"), sem(name + "_rstd")
    return s


def graph_stage(nc, k, d):
    ctx = ExitStack()
    pb = lambda n, s, t: ctx.enter_context(nc.psum_tensor(n, s, t))
    sem = lambda n: nc.alloc_semaphore(name=n)
    with ctx:
        bank = [pb(f"gbank{i}", [128, 512], F32) for i in range(6)]
        column_mean = pb("column_mean", [128, 512], F32)
        column_var = pb("column_var", [128, 512], F32)
        SQ = ctx.enter_context(nc.sbuf_tensor("SQ", [TP, 2, D], F32))
        GAIN = ctx.enter_context(nc.sbuf_tensor("GAIN", [TP, D], F32))
        MEAN = ctx.enter_context(nc.sbuf_tensor("MEAN", [TP, D], F32))
        norm = norm_semaphores(sem, "g")
        rows_done, agg_mm, agg_taken = sem("g_rows_done"), sem("agg_mm"), sem("agg_taken")
        z_mm, z_done, mean_mm, mean_done = sem("z_mm"), sem("z_done"), sem("mean_mm"), sem("mean_done")
        centred, squared, var_mm = sem("centred"), sem("squared"), sem("var_mm")
        std_done, gain, beta_added, scaled, added = sem("std_done"), sem("gain"), sem("beta_added"), sem("scaled"), sem("added")
        Z = k.XN
        with nc.Block() as block:
            @block.vector
            def _(dve):
                dve.wait_ge(k.x_in, 16)
                normalise_rows_vector(nc, k, dve, k.X, k.XN, norm, rows_done)
                dve.wait_ge(k.gnn_w_in, 64)
                dve.wait_ge(agg_taken, 3 * DC)
                for t in range(NT):
                    dve.wait_ge(z_mm, t + 1)
                    nc.vector.tensor_tensor(Z[:, t, :], bank[t % 6][0:TP, :], k.ROWS[:, 0, :], ALU.add).then_inc(z_done, 1)
                dve.wait_ge(mean_mm, 1)
                nc.vector.tensor_scalar(MEAN[:, :], column_mean[0:TP, :], 1.0 / N, None, ALU.mult).then_inc(mean_done, 1)
                dve.wait_ge(z_done, NT)
                dve.wait_ge(mean_done, 1)
                for t in range(NT):
                    nc.vector.tensor_tensor(Z[:, t, :], Z[:, t, :], MEAN[:, :], ALU.subtract).then_inc(centred, 1)
                dve.wait_ge(std_done, 1)
                nc.vector.reciprocal(MEAN[:, :], GAIN[:, :]).then_inc(gain, 1)
                dve.wait_ge(gain, 1)
                nc.vector.tensor_tensor(MEAN[:, :], MEAN[:, :], k.ROWS[:, 1, :], ALU.mult).then_inc(gain, 1)
                dve.wait_ge(gain, 2)
                dve.wait_ge(centred, NT)
                dve.wait_ge(squared, NT)
                for t in range(NT):
                    nc.vector.tensor_tensor(Z[:, t, :], Z[:, t, :], MEAN[:, :], ALU.mult).then_inc(scaled, 1)
                dve.wait_ge(beta_added, NT)
                for t in range(NT):
                    dve.wait_ge(scaled, t + 1)
                    nc.vector.tensor_tensor(k.X[:, t, :], k.X[:, t, :], Z[:, t, :], ALU.add).then_inc(added, 1)

            @block.scalar
            def _(act):
                normalise_rows_scalar(nc, k, act, norm)
                g = 0
                for c in range(DC):
                    for c0, w in SPANS:
                        act.wait_ge(agg_mm, g + 1)
                        nc.scalar.activation(k.XT[:, c, c0:c0 + w], bank[g % 6][:, 0:w], ACT.Copy).then_inc(agg_taken, 1)
                        g += 1
                for t in range(NT):
                    act.wait_ge(centred, t + 1)
                    if t >= 2:
                        act.wait_ge(var_mm, t - 1)
                    nc.scalar.activation(SQ[:, t % 2, :], Z[:, t, :], ACT.Square).then_inc(squared, 1)
                act.wait_ge(var_mm, NT)
                nc.scalar.activation(GAIN[:, :], column_var[0:TP, :], ACT.Sqrt, bias=k.EPSC[0:TP, 0:1],
                                     scale=1.0 / N).then_inc(std_done, 1)

            @block.gpsimd
            def _(pool):
                pool.wait_ge(k.gnn_w_in, 64)
                pool.wait_ge(rows_done, NT)
                for t in range(NT):
                    pool.tensor_tensor(k.X[:, t, :], k.X[:, t, :], k.ROWS[:, 2, :], ALU.add).then_inc(beta_added, 1)

            @block.tensor
            def _(pe):
                pe.wait_ge(rows_done, NT)
                g = 0
                for c in range(DC):
                    for c0, w in SPANS:
                        if g >= 6:
                            pe.wait_ge(agg_taken, g - 5)
                        for s in range(NT):
                            last = nc.tensor.matmul(bank[g % 6][:, 0:w], k.XN[:, s, c * 128:(c + 1) * 128],
                                                    k.AT[:, s, c0:c0 + w], start=s == 0, stop=s == NT - 1)
                        last.then_inc(agg_mm, 1)
                        g += 1
                pe.wait_ge(agg_taken, 3 * DC)
                pe.wait_ge(k.gnn_w_in, 64)

                def add_mean(t):
                    pe.wait_ge(z_done, t + 1)
                    last = nc.tensor.matmul(column_mean[0:TP, :], k.ONES[0:TP, 0:TP], Z[:, t, :], start=t == 0, stop=t == NT - 1)
                    if t == NT - 1:
                        last.then_inc(mean_mm, 1)

                for t in range(NT):
                    if t >= 6:
                        pe.wait_ge(z_done, t - 5)
                    for c in range(DC):
                        last = nc.tensor.matmul(bank[t % 6][0:TP, :], k.XT[:, c, t * TP:(t + 1) * TP], k.WT[:, c, :],
                                                start=c == 0, stop=c == DC - 1)
                    last.then_inc(z_mm, 1)
                    if t >= 2:
                        add_mean(t - 2)
                add_mean(NT - 2)
                add_mean(NT - 1)
                for t in range(NT):
                    pe.wait_ge(squared, t + 1)
                    nc.tensor.matmul(column_var[0:TP, :], k.ONES[0:TP, 0:TP], SQ[:, t % 2, :], start=t == 0,
                                     stop=t == NT - 1).then_inc(var_mm, 1)


GROUP = 256


def groups_max(experts, top):
    return N * top // GROUP + experts


class Dispatch:

    def __init__(self, nc, k, ctx, name, experts, top):
        sb = lambda n, s, t: ctx.enter_context(nc.sbuf_tensor(name + n, s, t))
        sem = lambda n: nc.alloc_semaphore(name=name + n)
        self.R, self.K = experts, top
        self.LOWER = sb("LOWER", [TP, experts, experts], F32)
        self.EARLIER = sb("EARLIER", [TP, TP], F32)
        self.RANK = sb("RANK", [TP, NT, experts], F32)
        self.SEL = sb("SEL", [TP, NT, experts], F32)
        self.GATE = sb("GATE", [TP, NT, experts], F32)
        self.SLOT = sb("SLOT", [TP, NT, experts], F32)
        self.PICK = sb("PICK", [TP, top, NT, experts], F32)
        self.WORK = sb("WORK", [TP, top, NT, experts], F32)
        self.PAIR = sb("PAIR", [TP, experts, experts], F32)
        self.OVER = sb("OVER", [TP, experts, 4], F32)
        self.TOTAL = sb("TOTAL", [TP, experts], F32)
        self.TAB = sb("TAB", [TP, 3, experts], F32)
        self.TABI = sb("TABI", [1, 3, experts], I32)
        self.AT = sb("AT", [TP, top, NT], F32)
        self.INDEX = sb("INDEX", [TP, top, NT], I32)
        self.WEIGHT = sb("WEIGHT", [TP, top, NT], F32)
        self.lower_done, self.selected, self.counted = sem("lower_done"), sem("selected"), sem("counted")
        self.step, self.table_done, self.index_done = sem("step"), sem("table_done"), sem("index_done")

    def gpsimd(self, nc, pool):
        pool.memset(self.LOWER[:, :, :], 1.0).then_inc(self.lower_done, 1)
        pool.memset(self.EARLIER[:, :], 1.0).then_inc(self.lower_done, 1)
        pool.wait_ge(self.lower_done, 2)
        pool.affine_select(out=self.LOWER[:, :, :], in_=self.LOWER[:, :, :], compare_op=ALU.is_gt, fill=0.0, base=0,
                           pattern=[[1, self.R], [-1, self.R]], channel_multiplier=0).then_inc(self.lower_done, 1)
        pool.affine_select(out=self.EARLIER[:, :], in_=self.EARLIER[:, :], compare_op=ALU.is_gt, fill=0.0, base=0,
                           pattern=[[1, TP]], channel_multiplier=-1).then_inc(self.lower_done, 1)

    def tensor(self, nc, pe, k, places, totals):
        R = self.R
        pe.wait_ge(self.lower_done, 4)
        pe.wait_ge(self.selected, 1)
        flat = self.SEL[:, :, :].rearrange("p t e -> p (t e)")
        nc.tensor.matmul(places[0:TP, 0:NT * R], self.EARLIER[:, :], flat, start=True, stop=False)
        for s in range(1, NT):
            nc.tensor.matmul(places[0:TP, s * R:NT * R], k.ONES[0:TP, 0:TP], flat[:, 0:(NT - s) * R], start=False, stop=s == NT - 1)
        for t in range(NT):
            last = nc.tensor.matmul(totals[0:TP, 0:R], k.ONES[0:TP, 0:TP], self.SEL[:, t, :], start=t == 0, stop=t == NT - 1)
        last.then_inc(self.counted, 1)

    def vector(self, nc, dve, places, totals):
        R, K = self.R, self.K
        n = [0]

        def chain(instruction):
            n[0] += 1
            instruction.then_inc(self.step, 1)
            dve.wait_ge(self.step, n[0])

        for r in range(K):
            chain(nc.vector.tensor_scalar(self.PICK[:, r, :, :], self.RANK[:, :, :], float(r), None, ALU.is_equal))
        dve.wait_ge(self.lower_done, 4)
        dve.wait_ge(self.counted, 1)
        chain(nc.vector.tensor_copy(self.TOTAL[:, :], totals[0:TP, 0:R]))
        over_totals = self.TOTAL[:, :].unsqueeze(1).to_broadcast([TP, R, R])
        chain(nc.vector.tensor_tensor(self.PAIR[:, :, :], over_totals, self.LOWER[:, :, :], ALU.mult))
        chain(nc.vector.tensor_reduce(self.TAB[:, 0, :], self.PAIR[:, :, :], AX.X, ALU.add))
        for j in range(4):
            chain(nc.vector.tensor_scalar(self.OVER[:, :, j], self.TOTAL[:, :], GROUP * (j + 1) + 0.5, None, ALU.is_gt))
        chain(nc.vector.tensor_reduce(self.TAB[:, 1, :], self.OVER[:, :, :], AX.X, ALU.add))
        chain(nc.vector.tensor_scalar(self.TAB[:, 1, :], self.TAB[:, 1, :], 1.0, None, ALU.add))
        chain(nc.vector.tensor_tensor(self.PAIR[:, :, :], self.TAB[:, 1, :].unsqueeze(1).to_broadcast([TP, R, R]), self.LOWER[:, :, :], ALU.mult))
        chain(nc.vector.tensor_reduce(self.TAB[:, 2, :], self.PAIR[:, :, :], AX.X, ALU.add))
        nc.vector.tensor_copy(self.TABI[:, :, :], self.TAB[0:1, :, :]).then_inc(self.table_done, 1)
        chain(nc.vector.tensor_tensor(self.SLOT[:, :, :], places[0:TP, 0:NT * R].rearrange("p (t e) -> p t e", e=R),
                                      self.TAB[:, 0, :].unsqueeze(1).to_broadcast([TP, NT, R]), ALU.add))
        work = self.WORK[:, :, :, :].rearrange("p k t e -> p k (t e)")
        pick = self.PICK[:, :, :, :].rearrange("p k t e -> p k (t e)")
        slot = self.SLOT[:, :, :].rearrange("p t e -> p (t e)").unsqueeze(1).to_broadcast([TP, K, NT * R])
        chain(nc.vector.tensor_tensor(work, pick, slot, ALU.mult))
        chain(nc.vector.tensor_reduce(self.AT[:, :, :], self.WORK[:, :, :, :], AX.X, ALU.add))
        nc.vector.tensor_copy(self.INDEX[:, :, :], self.AT[:, :, :]).then_inc(self.index_done, 1)
        gate = self.GATE[:, :, :].rearrange("p t e -> p (t e)").unsqueeze(1).to_broadcast([TP, K, NT * R])
        chain(nc.vector.tensor_tensor(work, pick, gate, ALU.mult))
        chain(nc.vector.tensor_reduce(self.WEIGHT[:, :, :], self.WORK[:, :, :, :], AX.X, ALU.add))

    def row(self, engine, e):
        return engine.value_load(self.TABI[0:1, 0, bass.ds(e, 1)], min_val=0, max_val=N * self.K)

    def groups(self, engine, e):
        return engine.value_load(self.TABI[0:1, 1, bass.ds(e, 1)], min_val=1, max_val=(N + GROUP - 1) // GROUP)

    def base(self, engine, e):
        return engine.value_load(self.TABI[0:1, 2, bass.ds(e, 1)], min_val=0, max_val=groups_max(self.R, self.K) - 1)


def mixture_stage(nc, k, d):
    ctx = ExitStack()
    sb = lambda n, s, t: ctx.enter_context(nc.sbuf_tensor(n, s, t))
    pb = lambda n, s, t: ctx.enter_context(nc.psum_tensor(n, s, t))
    sem = lambda n: nc.alloc_semaphore(name=n)
    HC = H1 // 128
    SB = GROUP // 128
    BACK = 8
    rows_in = nc.dram_tensor("m_rows_in", (N * TOP1 + 5 * GROUP, D), F32, kind="Internal").ap()
    rows_out = nc.dram_tensor("m_rows_out", (N * TOP1 + 5 * GROUP, D), F32, kind="Internal").ap()
    with ctx:
        W1 = [sb(f"W1_{p}", [128, DC, H1], F32) for p in range(2)]
        W2 = [sb(f"W2_{p}", [128, HC, D], F32) for p in range(2)]
        B1 = [sb(f"B1_{p}", [128, HC], F32) for p in range(2)]
        SLOTS = sb("SLOTS", [128, SB, D], F32)
        SLOTST = sb("SLOTST", [128, DC, GROUP], F32)
        HID = sb("HID", [128, HC, GROUP], F32)
        OUT = sb("OUT", [128, SB, D], F32)
        RES = sb("RES", [TP, BACK, D], F32)
        ZERO = sb("ZERO", [128, D], F32)
        B2 = sb("B2", [R1, D], F32)
        RW = sb("RW", [128, DC, R1], F32)
        RB = sb("RB", [TP, R1], F32)
        LG = sb("LG", [TP, NT, R1], F32)
        GT = sb("GT", [R1, N], F32)
        COL = sb("COL", [TP, 3, NT], F32)
        BEAT = sb("BEAT", [TP, 2, NT, R1 * R1], F32)
        D1 = Dispatch(nc, k, ctx, "m_", R1, TOP1)
        bank = [pb(f"mbank{i}", [128, 512], F32) for i in range(8)]
        ybank, tbank, hbank = bank[0:4], bank[4:6], bank[6:8]
        norm = norm_semaphores(sem, "m")
        rows_done, turned, taken = sem("m_rows_done"), sem("m_turned"), sem("m_taken")
        w_ready = [sem(f"w_ready{p}") for p in range(2)]
        small_in, logit_mm, zero_done, pad_in = sem("small_in"), sem("logit_mm"), sem("zero_done"), sem("pad_in")
        vstep, shifted, exped, gates = sem("m_vstep"), sem("shifted"), sem("exped"), sem("gates")
        gates_turned, gates_copied, bias_mm, bias_added = sem("gates_turned"), sem("gates_copied"), sem("bias_mm"), sem("bias_added")
        sent, slots_in = sem("m_sent"), sem("slots_in")
        slots_turned, slots_copied, hid_mm, hid_done = sem("slots_turned"), sem("slots_copied"), sem("hid_mm"), sem("hid_done")
        y_mm, y_copied, out_stored, pool_passed = sem("y_mm"), sem("y_copied"), sem("out_stored"), sem("m_pool_passed")
        passed = sem("m_passed")
        back_in = [sem(f"back_in{i}") for i in range(BACK)]
        back_added = sem("back_added")
        w1v = d["w1"].rearrange("e (c p) h -> e p c h", p=128)
        w2v = d["w2"].rearrange("e (c p) f -> e p c f", p=128)

        with nc.Block() as block:
            @block.sync
            def _(sp):
                sp.dma_start(RW[:, :, :], d["router_w"].rearrange("(c p) e -> p c e", p=128)).then_inc(small_in, 16)
                sp.dma_start(RB[:, :], d["router_b"].rearrange("(a n) -> a n", a=1).to_broadcast([TP, R1])).then_inc(small_in, 16)
                sp.dma_start(B2[:, :], d["b2"]).then_inc(small_in, 16)
                sp.wait_ge(zero_done, 1)
                for s in range(SB):
                    sp.dma_start(rows_in[N * TOP1 + 128 * s:N * TOP1 + 128 * (s + 1), :], ZERO[:, :]).then_inc(pad_in, 16)
                sp.wait_ge(pad_in, 16 * SB)

                sp.wait_ge(D1.table_done, 1)
                sp.wait_ge(sent, 16 * TOP1 * NT)
                with sp.Fori(0, R1) as e:
                    row, groups, base = D1.row(sp, e), D1.groups(sp, e), D1.base(sp, e)
                    with sp.Fori(0, groups) as j:
                        sp.wait_ge(slots_turned, base + j + 1)
                        sp.dma_start(SLOTS[:, :, :], rows_in[bass.ds(row + GROUP * j, GROUP), :].rearrange("(s p) c -> p s c", p=128)).then_inc(slots_in, 16)
                last_base, last_groups = D1.base(sp, R1 - 1), D1.groups(sp, R1 - 1)
                sp.wait_ge(slots_turned, last_base + last_groups + 1)
                sp.dma_start(SLOTS[:, :, :], rows_in[0:GROUP, :].rearrange("(s p) c -> p s c", p=128)).then_inc(slots_in, 16)
                sp.wait_ge(slots_turned, last_base + last_groups + 2)
                sp.sem_inc(passed, 1)

            @block.gpsimd
            def _(pool):
                pool.memset(ZERO[:, :], 0.0).then_inc(zero_done, 1)

                def load_weights(e, p):
                    pool.dma_start(B1[p][:, :], d["b1"][bass.ds(e, 1)].rearrange("o (p c) -> p (o c)", p=128)).then_inc(w_ready[p], 16)
                    pool.dma_start(W1[p][:, :, :], w1v[bass.ds(e, 1)].rearrange("o p c h -> p (o c) h")).then_inc(w_ready[p], 16)
                    pool.dma_start(W2[p][:, :, :], w2v[bass.ds(e, 1)].rearrange("o p c f -> p (o c) f")).then_inc(w_ready[p], 16)

                load_weights(0, 0)
                load_weights(1, 1)
                D1.gpsimd(nc, pool)
                pool.wait_ge(rows_done, NT)
                pool.wait_ge(D1.index_done, 1)
                for t in range(NT):
                    for r in range(TOP1):
                        pool.indirect_dma_start(rows_in[0:N * TOP1, :], bass.IndirectOffsetOnAxis(D1.INDEX[:, r, t:t + 1], 0),
                                                k.XN[:, t, :], None).then_inc(sent, 16)
                with pool.Fori(1, R1 // 2) as u:
                    for p in range(2):
                        done = D1.base(pool, 2 * u + p - 1)
                        pool.wait_ge(y_mm, SB * done + SB)
                        pool.sem_inc(pool_passed, 1)
                        load_weights(2 * u + p, p)
                last_base, last_groups = D1.base(pool, R1 - 1), D1.groups(pool, R1 - 1)
                pool.wait_ge(out_stored, 16 * (last_base + last_groups) + 16)
                pool.sem_inc(pool_passed, 1)
                for n in range(NT * TOP1):
                    t, r = divmod(n, TOP1)
                    if n >= BACK:
                        pool.wait_ge(back_added, n - BACK + 1)
                    pool.indirect_dma_start(RES[:, n % BACK, :], None, rows_out[0:N * TOP1, :],
                                            bass.IndirectOffsetOnAxis(D1.INDEX[:, r, t:t + 1], 0)).then_inc(back_in[n % BACK], 16)

            @block.vector
            def _(dve):
                normalise_rows_vector(nc, k, dve, k.X, k.XN, norm, rows_done)
                dve.wait_ge(small_in, 48)
                dve.wait_ge(logit_mm, 1)
                nc.vector.tensor_tensor(LG[:, :, :], hbank[0][0:TP, 0:NT * R1].rearrange("p (t e) -> p t e", e=R1),
                                        RB[:, :].unsqueeze(1).to_broadcast([TP, NT, R1]), ALU.add).then_inc(vstep, 1)
                dve.wait_ge(vstep, 1)
                mine = LG[:, :, :].unsqueeze(3).to_broadcast([TP, NT, R1, R1])
                other = LG[:, :, :].unsqueeze(2).to_broadcast([TP, NT, R1, R1])
                beat = BEAT[:, 0, :, :].rearrange("p t (i j) -> p t i j", j=R1)
                same = BEAT[:, 1, :, :].rearrange("p t (i j) -> p t i j", j=R1)
                nc.vector.tensor_tensor(same, other, mine, ALU.is_equal).then_inc(vstep, 1)
                nc.vector.tensor_tensor(beat, other, mine, ALU.is_gt).then_inc(vstep, 1)
                dve.wait_ge(D1.lower_done, 4)
                dve.wait_ge(vstep, 3)
                nc.vector.tensor_tensor(BEAT[:, 1, :, :], BEAT[:, 1, :, :], D1.LOWER[:, :, :].rearrange("p i j -> p (i j)").unsqueeze(1)
                                        .to_broadcast([TP, NT, R1 * R1]), ALU.mult).then_inc(vstep, 1)
                dve.wait_ge(vstep, 4)
                nc.vector.tensor_tensor(BEAT[:, 0, :, :], BEAT[:, 0, :, :], BEAT[:, 1, :, :], ALU.add).then_inc(vstep, 1)
                dve.wait_ge(vstep, 5)
                nc.vector.tensor_reduce(D1.RANK[:, :, :], beat, AX.X, ALU.add).then_inc(vstep, 1)
                dve.wait_ge(vstep, 6)
                nc.vector.tensor_scalar(D1.SEL[:, :, :], D1.RANK[:, :, :], TOP1 - 0.5, None, ALU.is_lt).then_inc(D1.selected, 1)
                nc.vector.tensor_reduce(COL[:, 0, :], LG[:, :, :], AX.X, ALU.max).then_inc(vstep, 1)
                dve.wait_ge(vstep, 7)
                nc.vector.tensor_tensor(LG[:, :, :], LG[:, :, :], COL[:, 0, :].unsqueeze(2).to_broadcast([TP, NT, R1]),
                                        ALU.subtract).then_inc(shifted, 1)
                dve.wait_ge(exped, 1)
                dve.wait_ge(D1.selected, 1)
                nc.vector.tensor_tensor(D1.GATE[:, :, :], D1.GATE[:, :, :], D1.SEL[:, :, :], ALU.mult).then_inc(vstep, 1)
                dve.wait_ge(vstep, 8)
                nc.vector.tensor_reduce(COL[:, 1, :], D1.GATE[:, :, :], AX.X, ALU.add).then_inc(vstep, 1)
                dve.wait_ge(vstep, 9)
                nc.vector.reciprocal(COL[:, 2, :], COL[:, 1, :]).then_inc(vstep, 1)
                dve.wait_ge(vstep, 10)
                nc.vector.tensor_tensor(D1.GATE[:, :, :], D1.GATE[:, :, :], COL[:, 2, :].unsqueeze(2).to_broadcast([TP, NT, R1]),
                                        ALU.mult).then_inc(gates, 1)
                dve.wait_ge(gates, 1)
                D1.vector(nc, dve, tbank[0], tbank[1])
                for t in range(NT):
                    dve.wait_ge(bias_mm, t + 1)
                    nc.vector.tensor_tensor(k.X[:, t, :], k.X[:, t, :], ybank[t % 4][0:TP, :], ALU.add).then_inc(bias_added, 1)
                dve.wait_ge(bias_added, NT)
                dve.sem_inc(y_copied, SB)
                with dve.Fori(0, R1) as e:
                    groups, base = D1.groups(dve, e), D1.base(dve, e)
                    with dve.Fori(base, base + groups) as g:
                        dve.wait_ge(out_stored, 16 * g + 16)
                        for s in range(SB):
                            dve.wait_ge(y_mm, SB * g + SB + s + 1)
                            nc.vector.tensor_copy(OUT[:, s, :], ybank[s][:, :]).then_inc(y_copied, 1)
                for n in range(NT * TOP1):
                    t, r = divmod(n, TOP1)
                    dve.wait_ge(back_in[n % BACK], 16 * (n // BACK + 1))
                    if n:
                        dve.wait_ge(back_added, n)
                    nc.vector.scalar_tensor_tensor(out=k.X[:, t, :], in0=RES[:, n % BACK, :], scalar=D1.WEIGHT[:, r, t:t + 1],
                                                   in1=k.X[:, t, :], op0=ALU.mult, op1=ALU.add).then_inc(back_added, 1)

            @block.scalar
            def _(act):
                normalise_rows_scalar(nc, k, act, norm)
                turn_rows_scalar(nc, k, act, ybank, turned, taken)
                act.wait_ge(shifted, 1)
                nc.scalar.activation(D1.GATE[:, :, :], LG[:, :, :], ACT.Exp).then_inc(exped, 1)
                for g, (t0, n) in enumerate(GROUPS):
                    act.wait_ge(gates_turned, g + 1)
                    nc.scalar.activation(GT[:, t0 * TP:(t0 + n) * TP], (hbank + ybank[3:4])[g][0:R1, 0:n * TP], ACT.Copy).then_inc(gates_copied, 1)
                act.wait_ge(D1.table_done, 1)

                def copy_slots(g):
                    act.wait_ge(slots_turned, g + 2)
                    for s in range(SB):
                        nc.scalar.activation(SLOTST[:, :, s * 128:(s + 1) * 128], tbank[s][:, :].rearrange("p (c n) -> p c n", n=128),
                                             ACT.Copy).then_inc(slots_copied, 1)

                act.sem_inc(out_stored, 16)
                copy_slots(0)
                with act.Fori(0, R1 // 2) as u:
                    for p in range(2):
                        row, groups, base = D1.row(act, 2 * u + p), D1.groups(act, 2 * u + p), D1.base(act, 2 * u + p)
                        act.wait_ge(w_ready[p], 48 * u + 48)
                        with act.Fori(0, groups) as j:
                            g = base + j
                            for h in range(HC):
                                act.wait_ge(hid_mm, HC * g + h + 1)
                                nc.scalar.activation(HID[:, h, :], hbank[h][:, 0:GROUP], ACT.Relu, bias=B1[p][:, h:h + 1]).then_inc(hid_done, 1)
                            copy_slots(g + 1)
                            act.wait_ge(y_copied, SB * g + 2 * SB)
                            act.dma_start(rows_out[bass.ds(row + GROUP * j, GROUP), :].rearrange("(s p) c -> p s c", p=128), OUT[:, :, :]).then_inc(out_stored, 16)

            @block.tensor
            def _(pe):
                turn_rows_tensor(nc, k, pe, ybank, rows_done, turned, taken)
                pe.wait_ge(taken, NT)
                pe.wait_ge(small_in, 48)
                for t in range(NT):
                    for c in range(DC):
                        last = nc.tensor.matmul(hbank[0][0:TP, t * R1:(t + 1) * R1], k.XT[:, c, t * TP:(t + 1) * TP], RW[:, c, :],
                                                start=c == 0, stop=c == DC - 1)
                last.then_inc(logit_mm, 1)
                D1.tensor(nc, pe, k, tbank[0], tbank[1])
                pe.wait_ge(gates, 1)
                for g, (t0, n) in enumerate(GROUPS):
                    for t in range(n):
                        last = nc.tensor.transpose((hbank + ybank[3:4])[g][0:R1, t * TP:(t + 1) * TP], D1.GATE[:, t0 + t, :], k.IDENT[0:TP, 0:TP])
                    last.then_inc(gates_turned, 1)
                pe.wait_ge(gates_copied, 3)
                for t in range(NT):
                    if t >= 4:
                        pe.wait_ge(bias_added, t - 3)
                    nc.tensor.matmul(ybank[t % 4][0:TP, :], GT[:, t * TP:(t + 1) * TP], B2[:, :], start=True, stop=True).then_inc(bias_mm, 1)
                pe.wait_ge(bias_added, NT)
                pe.wait_ge(D1.table_done, 1)
                pe.sem_inc(slots_turned, 1)
                pe.sem_inc(y_mm, SB)

                def turn_slots(g):
                    pe.wait_ge(slots_in, 16 * g + 16)
                    for s in range(SB):
                        for c in range(DC):
                            last = nc.tensor.transpose(tbank[s][:, c * 128:(c + 1) * 128], SLOTS[:, s, c * 128:(c + 1) * 128], k.IDENT[:, :])
                    last.then_inc(slots_turned, 1)

                turn_slots(0)
                with pe.Fori(0, R1 // 2) as u:
                    for p in range(2):
                        groups, base = D1.groups(pe, 2 * u + p), D1.base(pe, 2 * u + p)
                        with pe.Fori(base, base + groups) as g:
                            pe.wait_ge(w_ready[p], 48 * u + 48)
                            pe.wait_ge(slots_copied, SB * g + SB)
                            for h in range(HC):
                                for c in range(DC):
                                    last = nc.tensor.matmul(hbank[h][:, 0:GROUP], W1[p][:, c, h * 128:(h + 1) * 128], SLOTST[:, c, :],
                                                            start=c == 0, stop=c == DC - 1)
                                last.then_inc(hid_mm, 1)
                            turn_slots(g + 1)
                            pe.wait_ge(hid_done, HC * g + HC)
                            for s in range(SB):
                                pe.wait_ge(y_copied, SB * g + s + 1)
                                for h in range(HC):
                                    last = nc.tensor.matmul(ybank[s][:, :], HID[:, h, s * 128:(s + 1) * 128], W2[p][:, h, :],
                                                            start=h == 0, stop=h == HC - 1)
                                last.then_inc(y_mm, 1)


def attention_stage(nc, k, d):
    ctx = ExitStack()
    sb = lambda n, s, t: ctx.enter_context(nc.sbuf_tensor(n, s, t))
    pb = lambda n, s, t: ctx.enter_context(nc.psum_tensor(n, s, t))
    sem = lambda n: nc.alloc_semaphore(name=n)
    PAIRS = HEADS // 2
    UNITS = 2 * NT
    SCALE = 1.0 / float(np.sqrt(DK))
    with ctx:
        WQKV = sb("WQKV", [128, 3, DC, 128], F32)
        WFF = sb("WFF", [128, D], F32)
        BQK = sb("BQK", [128, 2], F32)
        BV = sb("BV", [TP, 128], F32)
        BFF = sb("BFF", [TP, D], F32)
        QT = sb("QT", [128, N], F32)
        KT = sb("KT", [128, N], F32)
        V = sb("V", [TP, NT, 128], F32)
        MASKED = [sb(f"MASKED{p}", [TP, N], F32) for p in range(2)]
        PROB = [sb(f"PROB{p}", [TP, N], F32) for p in range(3)]
        PROBT = [sb(f"PROBT{p}", [TP, NT, TP], F32) for p in range(2)]
        MSG = sb("MSG", [TP, NT, 2, DK], F32)
        MSGT = sb("MSGT", [128, N], F32)
        TOP = sb("TOP", [TP, UNITS], F32)
        SHIFT = sb("SHIFT", [TP, UNITS], F32)
        DEN = sb("DEN", [TP, 2, NT], F32)
        score = pb("score", [128, 1536], F32)
        turn = pb("turn", [128, 3, 512], F32)
        out_bank = [pb(f"out_bank{p}", [128, 512], F32) for p in range(2)]
        norm = norm_semaphores(sem, "a")
        rows_done, turned, taken = sem("a_rows_done"), sem("a_turned"), sem("a_taken")
        wqkv_in, wff_in, bff_in, bff_added = sem("wqkv_in"), sem("wff_in"), sem("bff_in"), sem("bff_added")
        proj_mm, qk_done, v_done = sem("proj_mm"), sem("qk_done"), sem("v_done")
        scores_seen = sem("scores_seen")
        score_mm, masked, shift_done, exp_done, weighted = sem("score_mm"), sem("masked"), sem("shift_done"), sem("exp_done"), sem("weighted")
        prob_turned, prob_copied, msg_mm, msg_copied = sem("prob_turned"), sem("prob_copied"), sem("msg_mm"), sem("msg_copied")
        den_done, msg_done, msg_turned, msgt_copied = sem("den_done"), sem("msg_done"), sem("msg_turned"), sem("msgt_copied")
        ff_mm, ff_added = sem("ff_mm"), sem("ff_added")
        bank = lambda i: score[:, 512 * i:512 * (i + 1)] if i < 3 else turn[:, i - 3, :]
        turn_banks = [bank(i) for i in range(6)]

        with nc.Block() as block:
            @block.sync
            def _(sp):
                sp.dma_start(BFF[:, :], d["ff_b"].rearrange("(a n) -> a n", a=1).to_broadcast([TP, D])).then_inc(bff_in, 16)
                with sp.Fori(0, PAIRS) as i:
                    sp.wait_ge(proj_mm, 9 * i + 9)
                    for j in range(3):
                        sp.dma_start(WQKV[:, j, :, :], d["qkv_w"].rearrange("(c p) f -> p c f", p=128)[:, :, bass.ds(128 * i + D * j, 128)]).then_inc(wqkv_in, 16)
                    sp.wait_ge(ff_mm, NT * i + NT)
                    sp.dma_start(BQK[:, :], d["qk_b"][bass.ds(i, 1)].rearrange("o (p j) -> p (o j)", p=128)).then_inc(wff_in, 16)
                    sp.dma_start(BV[:, :], d["v_b"][bass.ds(i, 1)].to_broadcast([TP, 128])).then_inc(wff_in, 16)
                    sp.dma_start(WFF[:, :], d["ff_w"][bass.ds(128 * i, 128), :]).then_inc(wff_in, 16)

            @block.gpsimd
            def _(pool):
                pool.wait_ge(bff_in, 16)
                pool.wait_ge(rows_done, NT)
                for t in range(NT):
                    pool.tensor_tensor(k.X[:, t, :], k.X[:, t, :], BFF[:, :], ALU.add).then_inc(bff_added, 1)

            @block.vector
            def _(dve):
                normalise_rows_vector(nc, k, dve, k.X, k.XN, norm, rows_done)
                dve.wait_ge(bff_added, NT)
                dve.sem_inc(ff_added, 3)
                with dve.Fori(0, PAIRS) as i:
                    dve.wait_ge(wff_in, 48 * i + 48)
                    for g, (t0, n) in enumerate(GROUPS):
                        dve.wait_ge(proj_mm, 9 * i + 9 + 6 + g + 1)
                        nc.vector.tensor_tensor(V[:, t0:t0 + n, :], bank(g)[0:TP, 0:128 * n].rearrange("p (t c) -> p t c", c=128),
                                                BV[:, :].unsqueeze(1).to_broadcast([TP, n, 128]), ALU.add).then_inc(v_done, 1)
                    for s in range(UNITS + 4):
                        if s < UNITS:
                            u, t = s, s % NT
                            dve.wait_ge(score_mm, UNITS * i + u + 1)
                            if u >= 2:
                                dve.wait_ge(exp_done, UNITS * i + u - 1)
                            dve.sem_inc(scores_seen, 1)
                            nc.vector.tensor_tensor_reduce(out=five(MASKED[u % 2][:, :]), in0=blocks5(score[0:TP, 0:1280]),
                                                           in1=five(k.M[:, t, :]), scale=1.0, scalar=3.0 * NEG, op0=ALU.add, op1=ALU.max,
                                                           accum_out=TOP[:, u:u + 1]).then_inc(masked, 1)
                            dve.wait_ge(masked, UNITS * i + u + 1)
                            nc.vector.tensor_scalar(SHIFT[:, u:u + 1], TOP[:, u:u + 1], -SCALE, None, ALU.mult).then_inc(shift_done, 1)
                        if 1 <= s <= UNITS:
                            u = s - 1
                            h, t = divmod(u, NT)
                            dve.wait_ge(exp_done, UNITS * i + u + 1)
                            nc.vector.tensor_tensor_reduce(out=PROB[u % 3][:, :], in0=PROB[u % 3][:, :], in1=k.A16[:, t, :], scale=1.0,
                                                           scalar=0.0, op0=ALU.mult, op1=ALU.add,
                                                           accum_out=DEN[:, h, t:t + 1]).then_inc(weighted, 1)
                        if s >= 4:
                            u = s - 4
                            h, t = divmod(u, NT)
                            dve.wait_ge(msg_mm, UNITS * i + u + 1)
                            nc.vector.tensor_copy(MSG[:, t, h, :], out_bank[u % 2][0:TP, 0:DK]).then_inc(msg_copied, 1)
                    dve.wait_ge(weighted, UNITS * i + UNITS)
                    nc.vector.tensor_scalar(DEN[:, :, :], DEN[:, :, :], 1e-30, None, ALU.max).then_inc(den_done, 1)
                    dve.wait_ge(den_done, 2 * i + 1)
                    nc.vector.reciprocal(DEN[:, :, :], DEN[:, :, :]).then_inc(den_done, 1)
                    dve.wait_ge(den_done, 2 * i + 2)
                    dve.wait_ge(msg_copied, UNITS * i + UNITS)
                    for h in range(2):
                        nc.vector.tensor_tensor(MSG[:, :, h, :], MSG[:, :, h, :], DEN[:, h, :].unsqueeze(2).to_broadcast([TP, NT, DK]),
                                                ALU.mult).then_inc(msg_done, 1)
                    for t in range(NT):
                        dve.wait_ge(ff_mm, NT * i + NT + t + 1)
                        nc.vector.tensor_tensor(k.X[:, t, :], k.X[:, t, :], bank(t % 3)[0:TP, :], ALU.add).then_inc(ff_added, 1)
                    dve.wait_ge(ff_added, NT * i + NT + 3)

            @block.scalar
            def _(act):
                normalise_rows_scalar(nc, k, act, norm)
                turn_rows_scalar(nc, k, act, turn_banks, turned, taken)
                with act.Fori(0, PAIRS) as i:
                    act.wait_ge(wff_in, 48 * i + 48)
                    for j, T in enumerate((QT, KT)):
                        for g, (c0, w) in enumerate(SPANS):
                            act.wait_ge(proj_mm, 9 * i + 9 + 3 * j + g + 1)
                            nc.scalar.activation(T[:, c0:c0 + w], bank(3 * j + g)[:, 0:w], ACT.Identity, bias=BQK[:, j:j + 1]).then_inc(qk_done, 1)
                    for s in range(UNITS + 2):
                        if s < UNITS:
                            u = s
                            act.wait_ge(shift_done, UNITS * i + u + 1)
                            if u >= 3:
                                act.wait_ge(prob_turned, 3 * (UNITS * i + u - 2))
                            nc.scalar.activation(PROB[u % 3][:, :], MASKED[u % 2][:, :], ACT.Exp, bias=SHIFT[:, u:u + 1],
                                                 scale=SCALE).then_inc(exp_done, 1)
                        if s >= 2:
                            u = s - 2
                            if u >= 2:
                                act.wait_ge(msg_mm, UNITS * i + u - 1)
                            for g, (t0, n) in enumerate(GROUPS):
                                act.wait_ge(prob_turned, 3 * (UNITS * i + u) + g + 1)
                                nc.scalar.activation(PROBT[u % 2][:, t0:t0 + n, :], turn[0:TP, g, 0:n * TP].rearrange("p (t n) -> p t n", n=TP),
                                                     ACT.Copy).then_inc(prob_copied, 1)
                    for g, (t0, n) in enumerate(GROUPS):
                        act.wait_ge(msg_turned, 3 * i + g + 1)
                        nc.scalar.activation(MSGT[:, t0 * TP:(t0 + n) * TP], turn[:, g, 0:n * TP], ACT.Copy).then_inc(msgt_copied, 1)

            @block.tensor
            def _(pe):
                turn_rows_tensor(nc, k, pe, turn_banks, rows_done, turned, taken)
                pe.wait_ge(taken, NT)
                pe.sem_inc(proj_mm, 9)
                pe.sem_inc(ff_mm, NT)
                with pe.Fori(0, PAIRS) as i:
                    pe.wait_ge(wqkv_in, 48 * i + 48)
                    pe.wait_ge(ff_added, NT * i + 3)
                    for j in range(2):
                        for g, (c0, w) in enumerate(SPANS):
                            for c in range(DC):
                                last = nc.tensor.matmul(bank(3 * j + g)[:, 0:w], WQKV[:, j, c, :], k.XT[:, c, c0:c0 + w],
                                                        start=c == 0, stop=c == DC - 1)
                            last.then_inc(proj_mm, 1)
                    for g, (t0, n) in enumerate(GROUPS):
                        pe.wait_ge(qk_done, 6 * i + g + 1)
                        for t in range(n):
                            for c in range(DC):
                                last = nc.tensor.matmul(bank(g)[0:TP, 128 * t:128 * (t + 1)], k.XT[:, c, (t0 + t) * TP:(t0 + t + 1) * TP],
                                                        WQKV[:, 2, c, :], start=c == 0, stop=c == DC - 1)
                        last.then_inc(proj_mm, 1)
                    for s in range(UNITS + 3):
                        if s < UNITS:
                            u = s
                            h, t = divmod(u, NT)
                            if u == 0:
                                pe.wait_ge(qk_done, 6 * i + 6)
                                pe.wait_ge(v_done, 3 * i + 3)
                            else:
                                pe.wait_ge(masked, UNITS * i + u)
                            for c0, w in SPANS:
                                col = c0 * 256 // 250
                                last = nc.tensor.matmul(blocks5(score[0:TP, col:col + w * 256 // 250]),
                                                        QT[h * DK:(h + 1) * DK, t * TP:(t + 1) * TP],
                                                        five(KT[h * DK:(h + 1) * DK, c0:c0 + w]), start=True, stop=True)
                            last.then_inc(score_mm, 1)
                        if 2 <= s < UNITS + 2:
                            u = s - 2
                            pe.wait_ge(weighted, UNITS * i + u + 1)
                            for g, (t0, n) in enumerate(GROUPS):
                                if u:
                                    pe.wait_ge(prob_copied, 3 * (UNITS * i + u - 1) + g + 1)
                                for t in range(n):
                                    last = nc.tensor.transpose(turn[0:TP, g, t * TP:(t + 1) * TP],
                                                               PROB[u % 3][:, (t0 + t) * TP:(t0 + t + 1) * TP], k.IDENT[0:TP, 0:TP])
                                last.then_inc(prob_turned, 1)
                        if s >= 3:
                            u = s - 3
                            h, t = divmod(u, NT)
                            pe.wait_ge(prob_copied, 3 * (UNITS * i + u) + 3)
                            if u >= 2:
                                pe.wait_ge(msg_copied, UNITS * i + u - 1)
                            for q in range(NT):
                                last = nc.tensor.matmul(out_bank[u % 2][0:TP, 0:DK], PROBT[u % 2][:, q, :],
                                                        V[:, q, h * DK:(h + 1) * DK], start=q == 0, stop=q == NT - 1)
                            last.then_inc(msg_mm, 1)
                    pe.wait_ge(msg_done, 2 * i + 2)
                    for g, (t0, n) in enumerate(GROUPS):
                        for t in range(n):
                            last = nc.tensor.transpose(turn[:, g, t * TP:(t + 1) * TP],
                                                       MSG[:, t0 + t, :, :].rearrange("p h c -> p (h c)"), k.IDENT[0:TP, 0:TP])
                        last.then_inc(msg_turned, 1)
                    pe.wait_ge(wff_in, 48 * i + 48)
                    for t in range(NT):
                        if t % 4 == 0:
                            pe.wait_ge(msgt_copied, 3 * i + t // 4 + 1)
                        if t >= 3:
                            pe.wait_ge(ff_added, NT * i + t - 2 + 3)
                        nc.tensor.matmul(bank(t % 3)[0:TP, :], MSGT[:, t * TP:(t + 1) * TP], WFF[:, :], start=True, stop=True).then_inc(ff_mm, 1)
                pe.wait_ge(ff_added, NT * PAIRS + 3)


def feedforward_stage(nc, k, d):
    ctx = ExitStack()
    sb = lambda n, s, t: ctx.enter_context(nc.sbuf_tensor(n, s, t))
    pb = lambda n, s, t: ctx.enter_context(nc.psum_tensor(n, s, t))
    sem = lambda n: nc.alloc_semaphore(name=n)
    HC = H2 // 128
    HALF = H2 // 512
    GE = G2 + R2
    SB = GROUP // 128
    BACK = 8
    RING = 3
    rows_in = nc.dram_tensor("f_rows_in", (N * TOP2 + 5 * GROUP, H2), F32, kind="Internal").ap()
    rows_out = nc.dram_tensor("f_rows_out", (N * TOP2 + 5 * GROUP, D), F32, kind="Internal").ap()
    with ctx:
        WIN = [sb(f"WIN{p}", [128, 2, DC, 128], F32) for p in range(2)]
        WOUT = [sb(f"WOUT{p}", [128, HC, D], F32) for p in range(2)]
        HID = sb("HID2", [128, HC, N], F32)
        HIDN = sb("HIDN", [TP, RING, H2], F32)
        SILU = [sb(f"SILU{p}", [128, 512], F32) for p in range(2)]
        LATE = sb("LATE", [128, 9216], F32)
        WEX = LATE[:, 0:2 * H2 * DC].rearrange("p (c f) -> p c f", c=DC)
        SLOTS = LATE[:, 0:SB * H2].rearrange("p (s f) -> p s f", s=SB)
        SLOTST = LATE[:, 2048:2048 + HC * GROUP].rearrange("p (c n) -> p c n", c=HC)
        OUT = LATE[:, 4096:4096 + SB * D].rearrange("p (s f) -> p s f", s=SB)
        RES = LATE[0:TP, 5120:5120 + BACK * D].rearrange("p (b f) -> p b f", b=BACK)
        ROW = sb("ROW2", [TP, 3, D], F32)
        GW = sb("GW", [128, DC, GE], F32)
        GB = sb("GB", [TP, GE], F32)
        EB = sb("EB", [R2, D], F32)
        LG = sb("LG2", [TP, NT, GE], F32)
        BEST = sb("BEST", [TP, 2, NT], F32)
        P4 = sb("P4", [TP, 4, NT, EG2], F32)
        COL = sb("COL2", [TP, 3, NT], F32)
        RANK = sb("RANK2", [TP, NT, EG2], F32)
        BEAT = sb("BEAT2", [TP, 2, NT, EG2 * EG2], F32)
        LOWER = sb("LOWER2", [TP, EG2, EG2], F32)
        CT = k.XN[0:R2, :, :].rearrange("p t c -> p (t c)")[:, 0:N]
        D2 = Dispatch(nc, k, ctx, "f_", R2, TOP2)
        bank = [pb(f"fbank{i}", [128, 512], F32) for i in range(8)]
        norm, norm2 = norm_semaphores(sem, "f"), norm_semaphores(sem, "f2")
        rows1, rows2, scaled_rows, rows_done = sem("f_rows1"), sem("f_rows2"), sem("f_scaled"), sem("f_rows_done")
        turned, taken = sem("f_turned"), sem("f_taken")
        small_in, lower_done, compared, logit_mm, zero_done, pad_in = sem("f_small_in"), sem("f_lower"), sem("f_compared"), sem("f_logit_mm"), sem("f_zero"), sem("f_pad_in")
        win_in = [sem(f"win_in{p}") for p in range(2)]
        wout_in = [sem(f"wout_in{p}") for p in range(2)]
        wex_in = sem("wex_in")
        vs, exped, shared_bias = sem("f_vs"), sem("f_exped"), sem("shared_bias")
        cnt_turned, cnt_copied, cb_mm, cb_added = sem("cnt_turned"), sem("cnt_copied"), sem("cb_mm"), sem("cb_added")
        ex_mm, ex_silu, ex_done = sem("ex_mm"), sem("ex_silu"), sem("ex_done")
        sent = [sem(f"f_sent{i}") for i in range(RING)]
        in_mm, silu_done, hid_done, shared_mm, shared_added = sem("in_mm"), sem("silu_done"), sem("f_hid_done"), sem("shared_mm"), sem("shared_added")
        slots_in = [sem(f"f_slots_in{s}") for s in range(SB)]
        slots_turned, slots_copied = [sem(f"f_slots_turned{s}") for s in range(SB)], [sem(f"f_slots_copied{s}") for s in range(SB)]
        y_mm, y_copied, out_stored, passed = sem("f_y_mm"), sem("f_y_copied"), sem("f_out_stored"), sem("f_passed")
        back_in = [sem(f"f_back_in{i}") for i in range(BACK)]
        back_added, stored = sem("f_back_added"), sem("stored")
        winv = d["in_w"].rearrange("w (c p) (s j q) -> w j p s c q", p=128, s=2, q=128)
        woutv = d["out_w"].rearrange("e (j p) f -> e p j f", p=128)

        with nc.Block() as block:
            @block.sync
            def _(sp):
                for j, row in enumerate((d["ln_scale"], d["ln_bias"], d["shared_out_b"])):
                    sp.dma_start(ROW[:, j, :], row.rearrange("(a n) -> a n", a=1).to_broadcast([TP, D])).then_inc(small_in, 16)
                sp.dma_start(GW[:, :, :], d["gate_w"].rearrange("(c p) e -> p c e", p=128)).then_inc(small_in, 16)
                sp.dma_start(GB[:, :], d["gate_b"].rearrange("(a n) -> a n", a=1).to_broadcast([TP, GE])).then_inc(small_in, 16)
                sp.dma_start(EB[:, :], d["expert_out_b"]).then_inc(small_in, 16)
                for c in range(DC):
                    sp.dma_start(WEX[:, c, :], d["in_w"][1, 128 * c:128 * (c + 1), :]).then_inc(wex_in, 16)
                sp.wait_ge(zero_done, 1)
                for s in range(SB):
                    sp.dma_start(rows_in[N * TOP2 + 128 * s:N * TOP2 + 128 * (s + 1), :], HID[:, 0, 0:H2]).then_inc(pad_in, 16)
                for j in range(HC):
                    if j >= 2:
                        sp.wait_ge(in_mm, 6 * (j - 1))
                    for s in range(2):
                        sp.dma_start(WIN[j % 2][:, s, :, :], winv[0, j, :, s]).then_inc(win_in[j % 2], 16)
                sp.wait_ge(pad_in, 16 * SB)
                sp.wait_ge(D2.table_done, 1)
                for i in range(RING):
                    sp.wait_ge(sent[i], 16 * TOP2 * len(range(i, NT, RING)))
                sp.wait_ge(ex_mm, 2 * HALF * NT)
                with sp.Fori(0, R2) as e:
                    row, groups, base = D2.row(sp, e), D2.groups(sp, e), D2.base(sp, e)
                    with sp.Fori(0, groups) as j:
                        for s in range(SB):
                            sp.wait_ge(slots_turned[s], base + j + 1)
                            sp.dma_start(SLOTS[:, s, :], rows_in[bass.ds(row + GROUP * j + 128 * s, 128), :]).then_inc(slots_in[s], 16)
                last_base, last_groups = D2.base(sp, R2 - 1), D2.groups(sp, R2 - 1)
                for s in range(SB):
                    sp.wait_ge(slots_turned[s], last_base + last_groups + 1)
                    sp.dma_start(SLOTS[:, s, :], rows_in[0:128, :]).then_inc(slots_in[s], 16)
                sp.wait_ge(slots_turned[SB - 1], last_base + last_groups + 2)
                sp.sem_inc(passed, 1)
                for t in range(NT):
                    sp.wait_ge(back_added, TOP2 * (t + 1))
                    sp.dma_start(d["out"][t * TP:(t + 1) * TP, :], k.X[:, t, :]).then_inc(stored, 16)
                sp.wait_ge(stored, 16 * NT)

            @block.gpsimd
            def _(pool):
                pool.memset(HID[:, 0, 0:H2], 0.0).then_inc(zero_done, 1)
                pool.memset(LOWER[:, :, :], 1.0).then_inc(lower_done, 1)
                pool.wait_ge(lower_done, 1)
                pool.affine_select(out=LOWER[:, :, :], in_=LOWER[:, :, :], compare_op=ALU.is_gt, fill=0.0, base=0,
                                   pattern=[[1, EG2], [-1, EG2]], channel_multiplier=0).then_inc(lower_done, 1)
                D2.gpsimd(nc, pool)
                pool.dma_start(WOUT[0][:, :, :], woutv[0]).then_inc(wout_in[0], 16)
                pool.dma_start(WOUT[1][:, :, :], woutv[1]).then_inc(wout_in[1], 16)
                pool.wait_ge(small_in, 96)
                pool.wait_ge(rows1, NT)
                for t in range(NT):
                    pool.tensor_tensor(k.X[:, t, :], k.X[:, t, :], ROW[:, 2, :], ALU.add).then_inc(shared_bias, 1)
                pool.wait_ge(D2.index_done, 1)
                for t in range(NT):
                    pool.wait_ge(ex_done, HALF * (t + 1))
                    for r in range(TOP2):
                        pool.indirect_dma_start(rows_in[0:N * TOP2, :], bass.IndirectOffsetOnAxis(D2.INDEX[:, r, t:t + 1], 0),
                                                HIDN[:, t % RING, :], None).then_inc(sent[t % RING], 16)
                pool.wait_ge(shared_mm, NT)
                pool.dma_start(WOUT[0][:, :, :], woutv[2]).then_inc(wout_in[0], 16)
                with pool.Fori(1, R2 // 2) as u:
                    for p in range(2):
                        done = D2.base(pool, 2 * u + p - 1)
                        pool.wait_ge(y_mm, SB * done + SB)
                        pool.sem_inc(passed, 1)
                        pool.dma_start(WOUT[1 - p][:, :, :], woutv[bass.ds(2 * u + p + 1, 1)].rearrange("o p j f -> p (o j) f")).then_inc(wout_in[1 - p], 16)
                last_base, last_groups = D2.base(pool, R2 - 1), D2.groups(pool, R2 - 1)
                pool.wait_ge(out_stored, 16 * (last_base + last_groups) + 16)
                pool.sem_inc(passed, 1)
                for n in range(NT * TOP2):
                    t, r = divmod(n, TOP2)
                    if n >= BACK:
                        pool.wait_ge(back_added, n - BACK + 1)
                    pool.indirect_dma_start(RES[:, n % BACK, :], None, rows_out[0:N * TOP2, :],
                                            bass.IndirectOffsetOnAxis(D2.INDEX[:, r, t:t + 1], 0)).then_inc(back_in[n % BACK], 16)

            @block.vector
            def _(dve):
                normalise_rows_vector(nc, k, dve, k.X, k.XN, norm, rows1)
                dve.wait_ge(rows1, NT)
                normalise_rows_vector(nc, k, dve, k.XN, k.XN, norm2, rows2)
                dve.wait_ge(small_in, 96)
                for t in range(NT):
                    dve.wait_ge(rows2, t + 1)
                    nc.vector.tensor_tensor(k.XN[:, t, :], k.XN[:, t, :], ROW[:, 0, :], ALU.mult).then_inc(scaled_rows, 1)
                for t in range(NT):
                    dve.wait_ge(scaled_rows, t + 1)
                    nc.vector.tensor_tensor(k.XN[:, t, :], k.XN[:, t, :], ROW[:, 1, :], ALU.add).then_inc(rows_done, 1)
                n = [0]

                def chain(instruction):
                    n[0] += 1
                    instruction.then_inc(vs, 1)
                    dve.wait_ge(vs, n[0])

                dve.wait_ge(logit_mm, 1)
                chain(nc.vector.tensor_tensor(LG[:, :, :], bank[6][0:TP, 0:NT * GE].rearrange("p (t e) -> p t e", e=GE),
                                              GB[:, :].unsqueeze(1).to_broadcast([TP, NT, GE]), ALU.add))
                chain(nc.vector.tensor_tensor(BEST[:, 1, :], LG[:, :, 1], LG[:, :, 0], ALU.is_gt))
                chain(nc.vector.tensor_scalar(BEST[:, 0, :], BEST[:, 1, :], -1.0, 1.0, ALU.mult, ALU.add))
                for g in range(2):
                    chain(nc.vector.tensor_tensor(P4[:, g, :, :], LG[:, :, G2 + EG2 * g:G2 + EG2 * (g + 1)],
                                                  BEST[:, g, :].unsqueeze(2).to_broadcast([TP, NT, EG2]), ALU.mult))
                chain(nc.vector.tensor_tensor(P4[:, 2, :, :], P4[:, 0, :, :], P4[:, 1, :, :], ALU.add))
                chain(nc.vector.tensor_reduce(COL[:, 0, :], P4[:, 2, :, :], AX.X, ALU.max))
                chain(nc.vector.tensor_tensor(P4[:, 0, :, :], P4[:, 2, :, :], COL[:, 0, :].unsqueeze(2).to_broadcast([TP, NT, EG2]), ALU.subtract))
                dve.wait_ge(exped, 1)
                chain(nc.vector.tensor_reduce(COL[:, 0, :], P4[:, 1, :, :], AX.X, ALU.add))
                chain(nc.vector.reciprocal(COL[:, 1, :], COL[:, 0, :]))
                chain(nc.vector.tensor_tensor(P4[:, 2, :, :], P4[:, 1, :, :], COL[:, 1, :].unsqueeze(2).to_broadcast([TP, NT, EG2]), ALU.mult))
                dve.wait_ge(lower_done, 2)
                mine = P4[:, 2, :, :].unsqueeze(3).to_broadcast([TP, NT, EG2, EG2])
                other = P4[:, 2, :, :].unsqueeze(2).to_broadcast([TP, NT, EG2, EG2])
                nc.vector.tensor_tensor(BEAT[:, 0, :, :].rearrange("p t (i j) -> p t i j", j=EG2), other, mine, ALU.is_gt).then_inc(compared, 1)
                nc.vector.tensor_tensor(BEAT[:, 1, :, :].rearrange("p t (i j) -> p t i j", j=EG2), other, mine, ALU.is_equal).then_inc(compared, 1)
                dve.wait_ge(compared, 2)
                chain(nc.vector.tensor_tensor(BEAT[:, 1, :, :], BEAT[:, 1, :, :],
                                              LOWER[:, :, :].rearrange("p i j -> p (i j)").unsqueeze(1).to_broadcast([TP, NT, EG2 * EG2]), ALU.mult))
                chain(nc.vector.tensor_tensor(BEAT[:, 0, :, :], BEAT[:, 0, :, :], BEAT[:, 1, :, :], ALU.add))
                chain(nc.vector.tensor_reduce(RANK[:, :, :], BEAT[:, 0, :, :].rearrange("p t (i j) -> p t i j", j=EG2), AX.X, ALU.add))
                chain(nc.vector.tensor_scalar(COL[:, 0:2, :], BEST[:, :, :], float(-EG2), float(EG2), ALU.mult, ALU.add))
                for g in range(2):
                    chain(nc.vector.tensor_tensor(D2.RANK[:, :, EG2 * g:EG2 * (g + 1)], RANK[:, :, :],
                                                  COL[:, g, :].unsqueeze(2).to_broadcast([TP, NT, EG2]), ALU.add))
                nc.vector.tensor_scalar(D2.SEL[:, :, :], D2.RANK[:, :, :], TOP2 - 0.5, None, ALU.is_lt).then_inc(D2.selected, 1)
                chain(nc.vector.tensor_scalar(RANK[:, :, :], RANK[:, :, :], TOP2 - 0.5, None, ALU.is_lt))
                chain(nc.vector.tensor_tensor(P4[:, 0, :, :], P4[:, 2, :, :], RANK[:, :, :], ALU.mult))
                chain(nc.vector.tensor_reduce(COL[:, 0, :], P4[:, 0, :, :], AX.X, ALU.add))
                chain(nc.vector.tensor_scalar(COL[:, 1, :], COL[:, 0, :], 1e-8, None, ALU.add))
                chain(nc.vector.reciprocal(COL[:, 2, :], COL[:, 1, :]))
                chain(nc.vector.tensor_tensor(P4[:, 3, :, :], P4[:, 0, :, :], COL[:, 2, :].unsqueeze(2).to_broadcast([TP, NT, EG2]), ALU.mult))
                for g in range(2):
                    chain(nc.vector.tensor_tensor(D2.GATE[:, :, EG2 * g:EG2 * (g + 1)], P4[:, 3, :, :],
                                                  BEST[:, g, :].unsqueeze(2).to_broadcast([TP, NT, EG2]), ALU.mult))

                def expert_rows(t):
                    if t >= RING:
                        dve.wait_ge(sent[t % RING], 16 * TOP2 * (t // RING))
                    for h in range(HALF):
                        m = HALF * t + h
                        dve.wait_ge(ex_silu, m + 1)
                        dve.wait_ge(ex_mm, 2 * m + 2)
                        nc.vector.tensor_tensor(HIDN[:, t % RING, 512 * h:512 * (h + 1)], SILU[m % 2][0:TP, :], bank[2 * (m % 3) + 1][0:TP, :],
                                                ALU.mult).then_inc(ex_done, 1)

                expert_rows(0)
                D2.vector(nc, dve, bank[6], bank[7])
                for t in range(1, NT):
                    expert_rows(t)
                m = 0
                for j in range(HC):
                    for c0, w in SPANS:
                        dve.wait_ge(silu_done, m + 1)
                        dve.wait_ge(in_mm, 2 * m + 2)
                        nc.vector.tensor_tensor(HID[:, j, c0:c0 + w], SILU[m % 2][:, 0:w], bank[2 * (m % 2) + 1][:, 0:w], ALU.mult).then_inc(hid_done, 1)
                        m += 1
                dve.wait_ge(shared_bias, NT)
                for t in range(NT):
                    dve.wait_ge(shared_mm, t + 1)
                    nc.vector.tensor_tensor(k.X[:, t, :], k.X[:, t, :], bank[4 + t % 4][0:TP, :], ALU.add).then_inc(shared_added, 1)
                dve.sem_inc(y_copied, SB)
                with dve.Fori(0, R2) as e:
                    groups, base = D2.groups(dve, e), D2.base(dve, e)
                    with dve.Fori(base, base + groups) as g:
                        dve.wait_ge(out_stored, 16 * g + 16)
                        for s in range(SB):
                            dve.wait_ge(y_mm, SB * g + SB + s + 1)
                            nc.vector.tensor_copy(OUT[:, s, :], bank[4 + s][:, :]).then_inc(y_copied, 1)
                dve.wait_ge(shared_added, NT)
                for n in range(NT * TOP2):
                    t, r = divmod(n, TOP2)
                    dve.wait_ge(back_in[n % BACK], 16 * (n // BACK + 1))
                    if n:
                        dve.wait_ge(back_added, n)
                    nc.vector.scalar_tensor_tensor(out=k.X[:, t, :], in0=RES[:, n % BACK, :], scalar=D2.WEIGHT[:, r, t:t + 1],
                                                   in1=k.X[:, t, :], op0=ALU.mult, op1=ALU.add).then_inc(back_added, 1)

            @block.scalar
            def _(act):
                normalise_rows_scalar(nc, k, act, norm)
                normalise_rows_scalar(nc, k, act, norm2)
                turn_rows_scalar(nc, k, act, bank[0:4], turned, taken)
                act.wait_ge(vs, 8)
                nc.scalar.activation(P4[:, 1, :, :], P4[:, 0, :, :], ACT.Exp).then_inc(exped, 1)
                for m in range(HALF * NT):
                    act.wait_ge(ex_mm, 2 * m + 1)
                    if m >= 2:
                        act.wait_ge(ex_done, m - 1)
                    nc.scalar.activation(SILU[m % 2][0:TP, :], bank[2 * (m % 3)][0:TP, :], ACT.Silu).then_inc(ex_silu, 1)
                for m in range(3 * HC):
                    w = SPANS[m % 3][1]
                    act.wait_ge(in_mm, 2 * m + 1)
                    if m >= 2:
                        act.wait_ge(hid_done, m - 1)
                    else:
                        act.wait_ge(ex_done, HALF * NT)
                    nc.scalar.activation(SILU[m % 2][:, 0:w], bank[2 * (m % 2)][:, 0:w], ACT.Silu).then_inc(silu_done, 1)
                for g, (t0, n) in enumerate(GROUPS):
                    act.wait_ge(cnt_turned, g + 1)
                    nc.scalar.activation(CT[:, t0 * TP:(t0 + n) * TP], bank[g][0:R2, 0:n * TP], ACT.Copy).then_inc(cnt_copied, 1)

                def copy_slots(g, s):
                    act.wait_ge(slots_turned[s], g + 2)
                    for q in range(2):
                        last = nc.scalar.activation(SLOTST[:, 4 * q:4 * q + 4, s * 128:(s + 1) * 128],
                                                    bank[2 * s + q][:, :].rearrange("p (c n) -> p c n", n=128), ACT.Copy)
                    last.then_inc(slots_copied[s], 1)

                act.sem_inc(out_stored, 16)
                for s in range(SB):
                    copy_slots(0, s)
                with act.Fori(0, R2) as e:
                    row, groups, base = D2.row(act, e), D2.groups(act, e), D2.base(act, e)
                    with act.Fori(0, groups) as j:
                        g = base + j
                        for s in range(SB):
                            copy_slots(g + 1, s)
                        act.wait_ge(y_copied, SB * g + 2 * SB)
                        act.dma_start(rows_out[bass.ds(row + GROUP * j, GROUP), :].rearrange("(s p) c -> p s c", p=128), OUT[:, :, :]).then_inc(out_stored, 16)

            @block.tensor
            def _(pe):
                turn_rows_tensor(nc, k, pe, bank[0:4], rows_done, turned, taken)
                pe.wait_ge(taken, NT)
                pe.wait_ge(small_in, 96)
                for t in range(NT):
                    for c in range(DC):
                        last = nc.tensor.matmul(bank[6][0:TP, t * GE:(t + 1) * GE], k.XT[:, c, t * TP:(t + 1) * TP], GW[:, c, :],
                                                start=c == 0, stop=c == DC - 1)
                last.then_inc(logit_mm, 1)
                pe.wait_ge(wex_in, 16 * DC)
                for t in range(NT):
                    if t == 1:
                        D2.tensor(nc, pe, k, bank[6], bank[7])
                    for h in range(HALF):
                        m = HALF * t + h
                        if m >= 3:
                            pe.wait_ge(ex_done, m - 2)
                        for s in range(2):
                            for c in range(DC):
                                last = nc.tensor.matmul(bank[2 * (m % 3) + s][0:TP, :], k.XT[:, c, t * TP:(t + 1) * TP],
                                                        WEX[:, c, H2 * s + 512 * h:H2 * s + 512 * (h + 1)], start=c == 0, stop=c == DC - 1)
                            last.then_inc(ex_mm, 1)
                pe.wait_ge(ex_done, HALF * NT)
                pe.wait_ge(zero_done, 1)
                m = 0
                for j in range(HC):
                    pe.wait_ge(win_in[j % 2], 32 * (j // 2 + 1))
                    for c0, w in SPANS:
                        if m >= 2:
                            pe.wait_ge(hid_done, m - 1)
                        for s in range(2):
                            for c in range(DC):
                                last = nc.tensor.matmul(bank[2 * (m % 2) + s][:, 0:w], WIN[j % 2][:, s, c, :], k.XT[:, c, c0:c0 + w],
                                                        start=c == 0, stop=c == DC - 1)
                            last.then_inc(in_mm, 1)
                        m += 1
                pe.wait_ge(wout_in[0], 16)
                pe.wait_ge(hid_done, 3 * HC)
                for g, (t0, n) in enumerate(GROUPS):
                    for t in range(n):
                        last = nc.tensor.transpose(bank[g][0:R2, t * TP:(t + 1) * TP], D2.SEL[:, t0 + t, :], k.IDENT[0:TP, 0:TP])
                    last.then_inc(cnt_turned, 1)
                pe.wait_ge(cnt_copied, 3)
                for t in range(NT):
                    if t >= 4:
                        pe.wait_ge(shared_added, t - 3)
                    for j in range(HC):
                        nc.tensor.matmul(bank[4 + t % 4][0:TP, :], HID[:, j, t * TP:(t + 1) * TP], WOUT[0][:, j, :], start=j == 0, stop=False)
                    nc.tensor.matmul(bank[4 + t % 4][0:TP, :], CT[:, t * TP:(t + 1) * TP], EB[:, :], start=False, stop=True).then_inc(shared_mm, 1)
                for s in range(SB):
                    pe.sem_inc(slots_turned[s], 1)
                pe.sem_inc(y_mm, SB)
                pe.wait_ge(shared_added, NT)
                pe.wait_ge(D2.table_done, 1)

                def turn_slots(g, s):
                    pe.wait_ge(slots_in[s], 16 * g + 16)
                    for c in range(HC):
                        last = nc.tensor.transpose(bank[2 * s + c // 4][:, (c % 4) * 128:(c % 4 + 1) * 128], SLOTS[:, s, c * 128:(c + 1) * 128],
                                                   k.IDENT[:, :])
                    last.then_inc(slots_turned[s], 1)

                for s in range(SB):
                    turn_slots(0, s)
                with pe.Fori(0, R2 // 2) as u:
                    for p in range(2):
                        groups, base = D2.groups(pe, 2 * u + p), D2.base(pe, 2 * u + p)
                        with pe.Fori(base, base + groups) as g:
                            pe.wait_ge(wout_in[1 - p], 16 * u + 16 * (p + 1))
                            for s in range(SB):
                                pe.wait_ge(slots_copied[s], g + 1)
                                pe.wait_ge(y_copied, SB * g + s + 1)
                                for j in range(HC):
                                    last = nc.tensor.matmul(bank[4 + s][:, :], SLOTST[:, j, s * 128:(s + 1) * 128], WOUT[1 - p][:, j, :],
                                                            start=j == 0, stop=j == HC - 1)
                                last.then_inc(y_mm, 1)
                                turn_slots(g + 1, s)


def finish_stage(nc, k, d):
    with nc.semaphore("stored") as stored, nc.Block() as block:
        @block.sync
        def _(sp):
            sp.dma_start(d["out"].rearrange("(t p) c -> p t c", p=TP), k.X[:, :, :]).then_inc(stored, 16)
            sp.wait_ge(stored, 16)


def program(nc, d):
    with ExitStack() as ctx:
        sb = lambda n, s, t: ctx.enter_context(nc.sbuf_tensor(n, s, t))
        k = OnChip()
        k.X = sb("X", [TP, NT, D], F32)
        k.XN = sb("XN", [TP, NT, D], F32)
        k.XT = sb("XT", [128, DC, N], F32)
        k.IDENT = sb("IDENT", [128, 128], F32)
        k.ONES = sb("ONES", [128, 128], F32)
        k.EPSC = sb("EPSC", [128, 1], F32)
        k.STATS = sb("STATS", [TP, NT, 6], F32)
        k.MV = sb("MV", [TP, NT, 2], F32)
        k.STD = sb("STD", [TP, NT], F32)
        k.RSTD = sb("RSTD", [TP, NT], F32)
        k.x_in = ctx.enter_context(nc.semaphore("x_in"))
        k.gnn_w_in = ctx.enter_context(nc.semaphore("gnn_w_in"))
        stop = d.get("stop", 4)
        with ExitStack() as graph:
            k.A16 = graph.enter_context(nc.sbuf_tensor("A16", [TP, NT, N], U16))
            k.M = graph.enter_context(nc.sbuf_tensor("M", [TP, NT, N], BF16))
            with ExitStack() as gnn:
                k.AT = gnn.enter_context(nc.sbuf_tensor("AT", [TP, NT, N], F32))
                k.WT = gnn.enter_context(nc.sbuf_tensor("WT", [128, DC, D], F32))
                k.ROWS = gnn.enter_context(nc.sbuf_tensor("ROWS", [TP, 3, D], F32))
                before = nc.snapshot_sems()
                adjacency_stage(nc, k, d)
                graph_stage(nc, k, d)
                nc.clear_and_free_semaphores(nc.allocated_since(before))
                nc.all_engine_barrier()
            if stop == 1:
                return finish_stage(nc, k, d)
            mixture_stage(nc, k, d)
            if stop == 2:
                return finish_stage(nc, k, d)
            attention_stage(nc, k, d)
            if stop == 3:
                return finish_stage(nc, k, d)
        feedforward_stage(nc, k, d)


def layout(nc, inputs):
    arrays = {
        "x": inputs["x"], "src": inputs["src"], "dst": inputs["dst"],
        "gnn_w": inputs["L0_gnn_W"].T, "gnn_b": inputs["L0_gnn_b"],
        "gnn_gamma": inputs["L0_gnn_gamma"], "gnn_beta": inputs["L0_gnn_beta"],
        "router_w": inputs["L0_ffn_router_w"], "router_b": inputs["L0_ffn_router_b"],
        "w1": inputs["L0_ffn_w1"], "b1": inputs["L0_ffn_b1"].reshape(R1, H1 // 128, 128).transpose(0, 2, 1).reshape(R1, H1),
        "w2": inputs["L0_ffn_w2"], "b2": inputs["L0_ffn_b2"],
    }
    bqkv = inputs["L1_gnn_b_qkv"].reshape(3, HEADS // 2, 128)
    arrays |= {
        "qkv_w": inputs["L1_gnn_W_qkv"].T, "ff_w": inputs["L1_gnn_W_ff"].T, "ff_b": inputs["L1_gnn_b_ff"],
        "qk_b": bqkv[0:2].transpose(1, 2, 0).reshape(HEADS // 2, 256), "v_b": bqkv[2],
    }
    rows = lambda w: w.T[None]
    arrays |= {
        "in_w": np.concatenate([rows(inputs["L1_ffn_shared_in_w"]), rows(inputs["L1_ffn_expert_in_w"])]),
        "out_w": np.concatenate([rows(inputs["L1_ffn_shared_out_w"]), inputs["L1_ffn_expert_out_weight"].transpose(0, 2, 1)]),
        "gate_w": np.concatenate([inputs["L1_ffn_group_gate_w"], inputs["L1_ffn_expert_gate_w"]]).T,
        "gate_b": np.concatenate([inputs["L1_ffn_group_bias"], inputs["L1_ffn_expert_bias"]]),
        "shared_out_b": inputs["L1_ffn_shared_out_b"], "expert_out_b": inputs["L1_ffn_expert_out_bias"],
        "ln_scale": inputs["L1_ffn_ln_scale"], "ln_bias": inputs["L1_ffn_ln_bias"],
    }
    d = {}
    for name, a in arrays.items():
        arrays[name] = a = np.ascontiguousarray(a)
        d[name] = nc.dram_tensor(name, a.shape, mybir.dt.from_np(a.dtype), kind="ExternalInput").ap()
    d["out"] = nc.dram_tensor("out", (N, D), F32, kind="ExternalOutput").ap()
    return arrays, d


def kernel(**inputs):
    import numpy as _np
    import concourse.bacc as _bacc
    from concourse.bass_utils import run_bass_kernel_spmd as _run

    nc = _bacc.Bacc("TRN2", target_bir_lowering=False, num_devices=1)
    arrays, d = layout(nc, {name: _np.asarray(a) for name, a in inputs.items()})
    program(nc, d)
    r = _run(nc, [arrays], core_ids=[0])
    return r.results[0]["out"]
```

```python
import numpy as np
import concourse.bass as bass
from concourse import mybir
from contextlib import ExitStack

F32 = mybir.dt.float32
F32R = mybir.dt.float32r
BF16 = mybir.dt.bfloat16
F16 = mybir.dt.float16
U16 = mybir.dt.uint16
I32 = mybir.dt.int32
ALU = mybir.AluOpType
ACT = mybir.ActivationFunctionType
AX = mybir.AxisListType

N = 1250
D = 512
E = 20000
TP = 125
NT = N // TP
ET = E // TP
DC = D // 128
SPANS = [(0, 500), (500, 500), (1000, 250)]
GROUPS = [(0, 4), (4, 4), (8, 2)]
EPS = 1e-5
WHOLE = 1.5 * 2.0 ** 23
NEG = -1.0e30

R1, H1 = 16, 256
TOP1 = 4
HEADS, DK = 8, 64
H2 = 1024
G2, EG2 = 2, 4
R2 = G2 * EG2
TOP2 = 2


class OnChip:
    pass


def blocks5(ap):
    return ap.rearrange("p (a b) -> p a b", b=256)[:, :, 0:250]


def five(ap):
    return ap.rearrange("p (a b) -> p a b", b=250)


def adjacency_stage(nc, k, d):
    ctx = ExitStack()
    sb = lambda n, s, t: ctx.enter_context(nc.sbuf_tensor(n, s, t))
    pb = lambda n, s, t: ctx.enter_context(nc.psum_tensor(n, s, t))
    sem = lambda n: nc.alloc_semaphore(name=n)
    HALF = ET // 2
    with ctx:
        edges_i = sb("edges_i", [HALF, 2, 2, TP], I32)
        edges_f = sb("edges_f", [HALF, 2, 2, TP], F32)
        bounds_q = sb("bounds_q", [HALF, 2, 2], F32)
        spread = sb("spread", [HALF, 2, 2, HALF], F32)
        RING = 6
        src_e = sb("src_e", [TP, ET + 2 * RING], F32)
        dst_e = sb("dst_e", [TP, ET + 2 * RING], F32)
        nodes = sb("nodes", [TP, N], F16)
        tile_up_i = sb("tile_up_i", [NT, ET], I32)
        tile_up = sb("tile_up", [NT, ET], F32)
        tile_down = sb("tile_down", [NT, ET], F32)
        first_i = sb("first_i", [NT, 1], I32)
        first = sb("first", [NT, 2], F32)
        ones_q = sb("ones_q", [HALF, NT], F32)
        before = sb("before", [NT, NT], F32)
        touch = sb("touch", [NT, 3, ET], F32)
        reach = sb("reach", [NT, 8], F32)
        table_i = sb("table_i", [NT, 5], I32)
        table = sb("table", [1, 5 * NT], I32)
        hot_src = sb("hot_src", [TP, RING * N], BF16)
        hot_dst = sb("hot_dst", [TP, RING * TP], BF16)
        zeros = sb("zeros", [TP, 500], BF16)
        nodes_i = k.M[:, 4:6, :].rearrange("p t c -> p (t c)").bitcast(I32)
        counts = [k.M[:, 2 * p:2 * p + 2, :].rearrange("p t c -> p (t c)").bitcast(F32) for p in range(2)]
        pA = [pb(f"pA{p}", [128, 1536], F32) for p in range(2)]
        pT = [pb(f"pT{p}", [128, 512], F32) for p in range(2)]

        edges_in = sem("edges_in")
        table_in = sem("table_in")
        iota_done = sem("iota_done")
        consts_done = sem("consts_done")
        cast_done = sem("cast_done")
        ident_done = sem("ident_done")
        edges_turned = sem("edges_turned")
        edges_copied = sem("edges_copied")
        step = sem("step")
        spread_done = sem("spread_done")
        bounds_mm = sem("bounds_mm")
        reach_done = sem("reach_done")
        prefix_mm = sem("prefix_mm")
        table_done = sem("table_done")
        hot_ready = sem("hot_ready")
        hot_used = sem("hot_used")
        block_mm = sem("block_mm")
        counts_copied = sem("counts_copied")
        block_taken = sem("block_taken")
        turned = sem("turned")
        turned_copied = sem("turned_copied")
        norm = norm_semaphores(sem, "g")

        with nc.Block() as block:
            @block.sync
            def _(sp):
                for j, e in enumerate((d["src"], d["dst"])):
                    sp.dma_start(edges_i[:, j, :, :], e.rearrange("(r q e) -> q r e", r=2, e=TP)).then_inc(edges_in, 16)
                sp.dma_start(k.X[:, :, :], d["x"].rearrange("(t p) c -> p t c", p=TP)).then_inc(k.x_in, 16)
                sp.dma_start(k.WT[:, :, :], d["gnn_w"].rearrange("(c p) f -> p c f", p=128)).then_inc(k.gnn_w_in, 16)
                for j, row in enumerate((d["gnn_b"], d["gnn_gamma"], d["gnn_beta"])):
                    sp.dma_start(k.ROWS[:, j, :], row.rearrange("(a n) -> a n", a=1).to_broadcast([TP, D])).then_inc(k.gnn_w_in, 16)
                sp.dma_start(k.RW[:, :, :], d["router_w"].rearrange("(c p) e -> p c e", p=128)).then_inc(k.router_in, 16)
                sp.dma_start(k.RB[:, :], d["router_b"].rearrange("(a n) -> a n", a=1).to_broadcast([TP, R1])).then_inc(k.router_in, 16)
                sp.dma_start(k.B2[:, :], d["b2"]).then_inc(k.router_in, 16)
                sp.wait_ge(table_done, 1)
                sp.dma_start(table[0:1, :], table_i[:, :]).then_inc(table_in, 16)

            @block.gpsimd
            def _(pool):
                pool.iota(nodes_i, pattern=[[1, N]], base=0, channel_multiplier=0).then_inc(iota_done, 1)
                pool.iota(tile_up_i[:, :], pattern=[[1, ET]], base=1, channel_multiplier=0).then_inc(iota_done, 1)
                pool.iota(first_i[:, :], pattern=[[0, 1]], base=0, channel_multiplier=TP).then_inc(iota_done, 1)
                pool.memset(k.IDENT[:, :], 0.0).then_inc(consts_done, 1)
                pool.memset(before[:, :], 1.0).then_inc(consts_done, 1)
                pool.memset(ones_q[:, :], 1.0).then_inc(consts_done, 1)
                pool.memset(zeros[:, :], 0.0).then_inc(consts_done, 1)
                pool.memset(k.ONES[:, :], 1.0).then_inc(consts_done, 1)
                pool.memset(k.EPSC[:, :], EPS).then_inc(consts_done, 1)
                pool.memset(src_e[:, ET:ET + 2 * RING], -1.0).then_inc(consts_done, 1)
                pool.memset(dst_e[:, ET:ET + 2 * RING], -1.0).then_inc(consts_done, 1)
                pool.wait_ge(consts_done, 8)
                pool.affine_select(out=k.IDENT[:, :], in_=k.IDENT[:, :], compare_op=ALU.not_equal, fill=1.0,
                                   base=0, pattern=[[-1, 128]], channel_multiplier=1).then_inc(ident_done, 1)
                pool.affine_select(out=before[:, :], in_=before[:, :], compare_op=ALU.is_gt, fill=0.0,
                                   base=0, pattern=[[1, NT]], channel_multiplier=-1).then_inc(ident_done, 1)

            @block.vector
            def _(dve):
                dve.wait_ge(edges_in, 32)
                nc.vector.tensor_copy(edges_f[:, :, :, :], edges_i[:, :, :, :]).then_inc(cast_done, 1)
                dve.wait_ge(iota_done, 3)
                nc.vector.tensor_copy(nodes[:, :], nodes_i).then_inc(cast_done, 1)
                nc.vector.tensor_copy(tile_up[:, :], tile_up_i[:, :]).then_inc(step, 1)
                nc.vector.tensor_copy(first[:, 0:1], first_i[:, :]).then_inc(step, 1)
                dve.wait_ge(cast_done, 1)
                nc.vector.tensor_reduce(bounds_q[:, 0, :], edges_f[:, 1, :, :], AX.X, ALU.min).then_inc(step, 1)
                nc.vector.tensor_reduce(bounds_q[:, 1, :], edges_f[:, 1, :, :], AX.X, ALU.max).then_inc(step, 1)
                dve.wait_ge(step, 4)
                nc.vector.tensor_scalar(tile_down[:, :], tile_up[:, :], -1.0, float(ET + 1), ALU.mult, ALU.add).then_inc(step, 1)
                nc.vector.tensor_scalar(first[:, 1:2], first[:, 0:1], float(TP - 1), None, ALU.add).then_inc(step, 1)
                dve.wait_ge(ident_done, 1)
                for m in range(2):
                    for r in range(2):
                        nc.vector.tensor_scalar(spread[:, m, r, :], k.IDENT[0:HALF, 0:HALF], bounds_q[:, m, r:r + 1], None,
                                                ALU.mult).then_inc(spread_done, 1)
                dve.wait_ge(edges_turned, 1)
                nc.vector.tensor_copy(src_e[:, 0:ET], pT[0][0:TP, 0:ET]).then_inc(edges_copied, 1)
                nc.vector.tensor_copy(dst_e[:, 0:ET], pT[0][0:TP, 256:256 + ET]).then_inc(edges_copied, 1)
                dve.wait_ge(bounds_mm, 1)
                dve.wait_ge(step, 6)
                nc.vector.tensor_scalar(touch[:, 0, :], pT[1][0:NT, 0:ET], first[:, 1:2], None, ALU.is_le).then_inc(step, 1)
                nc.vector.tensor_scalar(touch[:, 1, :], pT[1][0:NT, 256:256 + ET], first[:, 0:1], None, ALU.is_ge).then_inc(step, 1)
                dve.wait_ge(step, 8)
                nc.vector.tensor_tensor(touch[:, 2, :], touch[:, 0, :], touch[:, 1, :], ALU.mult).then_inc(step, 1)
                dve.wait_ge(step, 9)
                nc.vector.tensor_tensor(touch[:, 0, :], touch[:, 2, :], tile_down[:, :], ALU.mult).then_inc(step, 1)
                nc.vector.tensor_tensor(touch[:, 1, :], touch[:, 2, :], tile_up[:, :], ALU.mult).then_inc(step, 1)
                dve.wait_ge(step, 11)
                nc.vector.tensor_reduce(reach[:, 0:2], touch[:, 0:2, :], AX.X, ALU.max).then_inc(step, 1)
                dve.wait_ge(step, 12)
                nc.vector.tensor_scalar(reach[:, 2:3], reach[:, 0:1], -1.0, float(ET), ALU.mult, ALU.add).then_inc(step, 1)
                dve.wait_ge(step, 13)
                nc.vector.tensor_scalar(reach[:, 2:3], reach[:, 2:3], float(ET - 1), None, ALU.min).then_inc(step, 1)
                dve.wait_ge(step, 14)
                nc.vector.tensor_tensor(reach[:, 3:4], reach[:, 1:2], reach[:, 2:3], ALU.subtract).then_inc(step, 1)
                dve.wait_ge(step, 15)
                nc.vector.tensor_scalar(reach[:, 3:4], reach[:, 3:4], 1.0, 1.0 / RING, ALU.max, ALU.mult).then_inc(step, 1)
                dve.wait_ge(step, 16)
                nc.vector.tensor_scalar(reach[:, 3:4], reach[:, 3:4], (RING - 1) / (2.0 * RING), WHOLE, ALU.add, ALU.add).then_inc(step, 1)
                dve.wait_ge(step, 17)
                nc.vector.tensor_scalar(reach[:, 3:4], reach[:, 3:4], WHOLE, float(RING), ALU.subtract, ALU.mult).then_inc(reach_done, 1)
                dve.wait_ge(reach_done, 1)
                nc.vector.tensor_tensor(reach[:, 4:5], reach[:, 2:3], reach[:, 3:4], ALU.add).then_inc(step, 1)
                dve.wait_ge(prefix_mm, 1)
                nc.vector.tensor_scalar(reach[:, 6:7], pT[0][0:NT, 510:511], float(ET), None, ALU.add).then_inc(step, 1)
                dve.wait_ge(step, 19)
                nc.vector.tensor_tensor(reach[:, 5:6], reach[:, 6:7], reach[:, 2:3], ALU.subtract).then_inc(step, 1)
                nc.vector.tensor_tensor(reach[:, 7:8], reach[:, 6:7], reach[:, 3:4], ALU.add).then_inc(step, 1)
                nc.vector.tensor_copy(table_i[:, 0:1], reach[:, 2:3]).then_inc(step, 1)
                nc.vector.tensor_copy(table_i[:, 1:2], reach[:, 4:5]).then_inc(step, 1)
                dve.wait_ge(step, 23)
                nc.vector.tensor_copy(table_i[:, 2:5], reach[:, 5:8]).then_inc(table_done, 1)
                dve.wait_ge(edges_copied, 2)
                dve.wait_ge(cast_done, 2)
                dve.wait_ge(table_in, 16)
                dve.sem_inc(hot_ready, ET)
                with dve.Fori(0, NT) as b:
                    lo = dve.value_load(table[0:1, bass.ds(5 * b, 1)], min_val=0, max_val=ET - 1)
                    hi = dve.value_load(table[0:1, bass.ds(5 * b + 1, 1)], min_val=1, max_val=ET + RING)
                    off = dve.value_load(table[0:1, bass.ds(5 * b + 2, 1)], min_val=1, max_val=(NT + 1) * (ET + RING))
                    with dve.Fori(lo, hi, RING) as t:
                        for s in range(RING):
                            dve.wait_ge(hot_used, off + t + s + 1)
                            nc.vector.tensor_scalar(hot_dst[:, s * TP:(s + 1) * TP], nodes[:, bass.ds(b * TP, TP)],
                                                    dst_e[:, bass.ds(t + s, 1)], None, ALU.is_equal)
                            nc.vector.tensor_scalar(hot_src[:, s * N:(s + 1) * N], nodes[:, :],
                                                    src_e[:, bass.ds(t + s, 1)], None, ALU.is_equal).then_inc(hot_ready, 1)
                dve.wait_ge(k.x_in, 16)
                normalise_rows_vector(nc, k, dve, k.X, k.XN, norm, step)
                dve.wait_ge(turned_copied, 3 * NT + 2)
                for t in range(NT):
                    nc.vector.tensor_tensor(k.AT[:, t, t * TP:(t + 1) * TP], k.AT[:, t, t * TP:(t + 1) * TP],
                                            k.IDENT[0:TP, 0:TP], ALU.add).then_inc(step, 1)

            @block.tensor
            def _(pe):
                pe.wait_ge(ident_done, 2)
                pe.wait_ge(cast_done, 1)
                for j in range(2):
                    for r in range(2):
                        last = nc.tensor.transpose(pT[0][0:TP, 256 * j + HALF * r:256 * j + HALF * (r + 1)],
                                                   edges_f[:, j, r, :], k.IDENT[0:HALF, 0:HALF])
                last.then_inc(edges_turned, 1)
                pe.wait_ge(spread_done, 4)
                for m in range(2):
                    last = nc.tensor.matmul(pT[1][0:NT, 256 * m:256 * m + ET], ones_q[:, :],
                                            spread[:, m, :, :].rearrange("p r q -> p (r q)"), start=True, stop=True)
                last.then_inc(bounds_mm, 1)
                pe.wait_ge(reach_done, 1)
                pe.wait_ge(edges_copied, 2)
                nc.tensor.matmul(pT[0][0:NT, 510:511], before[:, :], reach[:, 3:4], start=True, stop=True).then_inc(prefix_mm, 1)
                pe.wait_ge(table_in, 16)
                pe.sem_inc(hot_used, ET + RING)

                def count_block(b, p):
                    first = pe.value_load(table[0:1, bass.ds(5 * b + 3, 1)], min_val=1, max_val=(NT + 1) * (ET + RING))
                    end = pe.value_load(table[0:1, bass.ds(5 * b + 4, 1)], min_val=1, max_val=(NT + 1) * (ET + RING))
                    pe.wait_ge(block_taken, b + 1)
                    for c0, w in SPANS:
                        out = pA[p][0:TP, c0 * 256 // 250:c0 * 256 // 250 + w * 256 // 250]
                        nc.tensor.matmul(blocks5(out), zeros[:, 0:TP], five(zeros[:, 0:w]), start=True, stop=False, skip_group_check=True)
                    with pe.Fori(first, end, RING) as n:
                        for s in range(RING):
                            pe.wait_ge(hot_ready, n + s + 1)
                            for c0, w in SPANS:
                                out = pA[p][0:TP, c0 * 256 // 250:c0 * 256 // 250 + w * 256 // 250]
                                last = nc.tensor.matmul(blocks5(out), hot_dst[:, s * TP:(s + 1) * TP],
                                                        five(hot_src[:, s * N + c0:s * N + c0 + w]),
                                                        start=False, stop=False, skip_group_check=True)
                            last.then_inc(hot_used, 1)
                    for c0, w in SPANS:
                        out = pA[p][0:TP, c0 * 256 // 250:c0 * 256 // 250 + w * 256 // 250]
                        last = nc.tensor.matmul(blocks5(out), zeros[:, 0:TP], five(zeros[:, 0:w]), start=False, stop=True,
                                                skip_group_check=True)
                    last.then_inc(block_mm, 1)

                def turn_block(b, p):
                    pe.wait_ge(counts_copied, b + 1)
                    for g, (t0, n) in enumerate(GROUPS):
                        q = (3 * p + g) % 2
                        pe.wait_ge(turned_copied, 3 * b + g + 1)
                        for t in range(n):
                            last = nc.tensor.transpose(pT[q][0:TP, t * TP:(t + 1) * TP],
                                                       counts[p][:, (t0 + t) * TP:(t0 + t + 1) * TP], k.IDENT[0:TP, 0:TP])
                        last.then_inc(turned, 1)

                count_block(0, 0)
                with pe.Fori(0, NT // 2 - 1) as u:
                    for p in range(2):
                        count_block(2 * u + p + 1, 1 - p)
                        turn_block(2 * u + p, p)
                count_block(NT - 1, 1)
                turn_block(NT - 2, 0)
                turn_block(NT - 1, 1)

            @block.scalar
            def _(act):
                act.sem_inc(block_taken, 2)
                act.wait_ge(table_in, 16)
                act.sem_inc(turned_copied, 2)

                def copy_counts(b, p):
                    act.wait_ge(block_mm, b + 1)
                    nc.scalar.activation(five(counts[p]), blocks5(pA[p][0:TP, 0:1280]), ACT.Copy).then_inc(counts_copied, 1)
                    nc.scalar.activation(k.A16[:, bass.ds(b, 1), :].rearrange("p o (a b) -> p (o a) b", b=250),
                                         blocks5(pA[p][0:TP, 0:1280]), ACT.Copy).then_inc(block_taken, 1)

                def copy_turned(b, p):
                    for g, (t0, n) in enumerate(GROUPS):
                        q = (3 * p + g) % 2
                        act.wait_ge(turned, 3 * b + g + 1)
                        nc.scalar.activation(k.AT[:, t0:t0 + n, bass.ds(b * TP, TP)],
                                             pT[q][0:TP, 0:n * TP].rearrange("p (t n) -> p t n", n=TP),
                                             ACT.Copy).then_inc(turned_copied, 1)

                copy_counts(0, 0)
                with act.Fori(0, NT // 2 - 1) as u:
                    for p in range(2):
                        copy_turned(2 * u + p, p)
                        copy_counts(2 * u + p + 1, 1 - p)
                copy_turned(NT - 2, 0)
                copy_counts(NT - 1, 1)
                copy_turned(NT - 1, 1)
                normalise_rows_scalar(nc, k, act, norm)


def normalise_rows_vector(nc, k, dve, src, dst, s, done):
    for t in range(NT):
        nc.vector.bn_stats(k.STATS[:, t, :], src[:, t, :]).then_inc(s.stats, 1)
    for t in range(NT):
        dve.wait_ge(s.stats, t + 1)
        nc.vector.bn_aggr(k.MV[:, t, :], k.STATS[:, t, :]).then_inc(s.moments, 1)
    dve.wait_ge(s.std, 1)
    nc.vector.reciprocal(k.RSTD[:, :], k.STD[:, :]).then_inc(s.rstd, 1)
    dve.wait_ge(s.rstd, 1)
    for t in range(NT):
        nc.vector.tensor_scalar(dst[:, t, :], src[:, t, :], k.MV[:, t, 0:1], k.RSTD[:, t:t + 1],
                                ALU.subtract, ALU.mult).then_inc(done, 1)


def normalise_rows_scalar(nc, k, act, s):
    act.wait_ge(s.moments, NT)
    nc.scalar.activation(k.STD[:, :], k.MV[:, :, 1], ACT.Sqrt, bias=k.EPSC[0:TP, 0:1]).then_inc(s.std, 1)


def norm_semaphores(sem, name):
    s = OnChip()
    s.stats, s.moments, s.std, s.rstd = sem(name + "_stats"), sem(name + "_moments"), sem(name + "_std"), sem(name + "_rstd")
    return s


class NextNorm:

    def __init__(self, sem, name, banks):
        self.banks = banks
        self.stats, self.moments, self.std, self.rstd = sem(name + "_stats"), sem(name + "_moments"), sem(name + "_std"), sem(name + "_rstd")
        self.rows, self.turned, self.taken = sem(name + "_rows"), sem(name + "_turned"), sem(name + "_taken")

    def vector(self, nc, k, dve, t):
        if t < NT:
            nc.vector.bn_stats(k.STATS[:, t, :], k.X[:, t, :]).then_inc(self.stats, 1)
            dve.wait_ge(self.stats, t + 1)
            nc.vector.bn_aggr(k.MV[:, t, :], k.STATS[:, t, :]).then_inc(self.moments, 1)
        if t > 0:
            dve.wait_ge(self.std, t)
            nc.vector.reciprocal(k.RSTD[:, t - 1:t], k.STD[:, t - 1:t]).then_inc(self.rstd, 1)
            dve.wait_ge(self.rstd, t)
            nc.vector.tensor_scalar(k.XN[:, t - 1, :], k.X[:, t - 1, :], k.MV[:, t - 1, 0:1], k.RSTD[:, t - 1:t],
                                    ALU.subtract, ALU.mult).then_inc(self.rows, 1)

    def scalar(self, nc, k, act):
        for t in range(NT + 2):
            if t < NT:
                act.wait_ge(self.moments, t + 1)
                nc.scalar.activation(k.STD[:, t:t + 1], k.MV[:, t, 1:2], ACT.Sqrt, bias=k.EPSC[0:TP, 0:1]).then_inc(self.std, 1)
            if t >= 2:
                act.wait_ge(self.turned, t - 1)
                nc.scalar.activation(k.XT[:, :, (t - 2) * TP:(t - 1) * TP],
                                     self.banks[(t - 2) % len(self.banks)][:, 0:DC * TP].rearrange("p (c n) -> p c n", n=TP),
                                     ACT.Copy).then_inc(self.taken, 1)

    def tensor(self, nc, k, pe, behind=None):
        for t in range(NT + 1):
            if t < NT:
                pe.wait_ge(self.rows, t + 1)
                if t >= len(self.banks):
                    pe.wait_ge(self.taken, t - len(self.banks) + 1)
                for c in range(DC):
                    last = nc.tensor.transpose(self.banks[t % len(self.banks)][:, c * TP:(c + 1) * TP],
                                               k.XN[:, t, c * 128:(c + 1) * 128], k.IDENT[0:TP, 0:TP])
                last.then_inc(self.turned, 1)
            if behind and t:
                behind(t - 1)


def graph_stage(nc, k, d):
    ctx = ExitStack()
    pb = lambda n, s, t: ctx.enter_context(nc.psum_tensor(n, s, t))
    sem = lambda n: nc.alloc_semaphore(name=n)
    with ctx:
        bank = [pb(f"gbank{i}", [128, 512], F32) for i in range(6)]
        column_mean = pb("column_mean", [128, 512], F32)
        column_var = pb("column_var", [128, 512], F32)
        SQ = ctx.enter_context(nc.sbuf_tensor("SQ", [TP, 2, D], F32))
        GAIN = ctx.enter_context(nc.sbuf_tensor("GAIN", [TP, D], F32))
        MEAN = ctx.enter_context(nc.sbuf_tensor("MEAN", [TP, D], F32))
        logit_mm, masked_out, agg_mm, agg_taken = sem("logit_mm"), sem("masked_out"), sem("agg_mm"), sem("agg_taken")
        z_mm, z_done, mean_mm, mean_done = sem("z_mm"), sem("z_done"), sem("mean_mm"), sem("mean_done")
        centred, squared, var_mm = sem("centred"), sem("squared"), sem("var_mm")
        std_done, gain, beta_added, scaled, first_scaled, added = sem("std_done"), sem("gain"), sem("beta_added"), sem("scaled"), sem("first_scaled"), sem("added")
        nextnorm = NextNorm(sem, "m", bank[0:4])
        Z = k.XN
        with nc.Block() as block:
            @block.vector
            def _(dve):
                for t in range(NT):
                    nc.vector.tensor_scalar(k.M[:, t, :], k.A16[:, t, :], 0.0, NEG, ALU.is_equal, ALU.mult).then_inc(masked_out, 1)
                dve.wait_ge(k.gnn_w_in, 64)
                dve.wait_ge(agg_taken, 3 * DC)
                for t in range(NT):
                    dve.wait_ge(z_mm, t + 1)
                    nc.vector.tensor_tensor(Z[:, t, :], bank[t % 6][0:TP, :], k.ROWS[:, 0, :], ALU.add).then_inc(z_done, 1)
                dve.wait_ge(mean_mm, 1)
                nc.vector.tensor_scalar(MEAN[:, :], column_mean[0:TP, :], 1.0 / N, None, ALU.mult).then_inc(mean_done, 1)
                dve.wait_ge(z_done, NT)
                dve.wait_ge(mean_done, 1)
                for t in range(NT):
                    nc.vector.tensor_tensor(Z[:, t, :], Z[:, t, :], MEAN[:, :], ALU.subtract).then_inc(centred, 1)
                dve.wait_ge(std_done, 1)
                nc.vector.reciprocal(MEAN[:, :], GAIN[:, :]).then_inc(gain, 1)
                dve.wait_ge(gain, 1)
                nc.vector.tensor_tensor(MEAN[:, :], MEAN[:, :], k.ROWS[:, 1, :], ALU.mult).then_inc(gain, 1)
                dve.wait_ge(gain, 2)
                dve.wait_ge(centred, NT)
                dve.wait_ge(squared, NT)
                nc.vector.tensor_tensor(Z[:, 0, :], Z[:, 0, :], MEAN[:, :], ALU.mult).then_inc(first_scaled, 1)
                dve.wait_ge(beta_added, NT)
                for t in range(NT + 1):
                    if t < NT:
                        if t:
                            dve.wait_ge(scaled, t)
                        else:
                            dve.wait_ge(first_scaled, 1)
                        nc.vector.tensor_tensor(k.X[:, t, :], k.X[:, t, :], Z[:, t, :], ALU.add).then_inc(added, 1)
                        dve.wait_ge(added, t + 1)
                    nextnorm.vector(nc, k, dve, t)
                dve.wait_ge(k.router_in, 48)
                dve.wait_ge(logit_mm, NT)
                nc.vector.tensor_tensor(k.LG[:, :, :], bank[5][0:TP, 0:NT * R1].rearrange("p (t e) -> p t e", e=R1),
                                        k.RB[:, :].unsqueeze(1).to_broadcast([TP, NT, R1]), ALU.add).then_inc(added, 1)

            @block.scalar
            def _(act):
                g = 0
                for c in range(DC):
                    for c0, w in SPANS:
                        act.wait_ge(agg_mm, g + 1)
                        nc.scalar.activation(k.XT[:, c, c0:c0 + w], bank[g % 6][:, 0:w], ACT.Copy).then_inc(agg_taken, 1)
                        g += 1
                for t in range(NT):
                    act.wait_ge(centred, t + 1)
                    if t >= 2:
                        act.wait_ge(var_mm, t - 1)
                    nc.scalar.activation(SQ[:, t % 2, :], Z[:, t, :], ACT.Square).then_inc(squared, 1)
                act.wait_ge(var_mm, NT)
                nc.scalar.activation(GAIN[:, :], column_var[0:TP, :], ACT.Sqrt, bias=k.EPSC[0:TP, 0:1],
                                     scale=1.0 / N).then_inc(std_done, 1)
                nextnorm.scalar(nc, k, act)

            @block.gpsimd
            def _(pool):
                pool.wait_ge(k.gnn_w_in, 64)
                for t in range(NT):
                    pool.tensor_tensor(k.X[:, t, :], k.X[:, t, :], k.ROWS[:, 2, :], ALU.add).then_inc(beta_added, 1)
                pool.wait_ge(gain, 2)
                pool.wait_ge(squared, NT)
                for t in range(1, NT):
                    pool.tensor_tensor(Z[:, t, :], Z[:, t, :], MEAN[:, :], ALU.mult).then_inc(scaled, 1)

            @block.tensor
            def _(pe):
                g = 0
                for c in range(DC):
                    for c0, w in SPANS:
                        if g >= 6:
                            pe.wait_ge(agg_taken, g - 5)
                        for s in range(NT):
                            last = nc.tensor.matmul(bank[g % 6][:, 0:w], k.XN[:, s, c * 128:(c + 1) * 128],
                                                    k.AT[:, s, c0:c0 + w], start=s == 0, stop=s == NT - 1)
                        last.then_inc(agg_mm, 1)
                        g += 1
                pe.wait_ge(agg_taken, 3 * DC)
                pe.wait_ge(k.gnn_w_in, 64)

                def add_mean(t):
                    pe.wait_ge(z_done, t + 1)
                    last = nc.tensor.matmul(column_mean[0:TP, :], k.ONES[0:TP, 0:TP], Z[:, t, :], start=t == 0, stop=t == NT - 1)
                    if t == NT - 1:
                        last.then_inc(mean_mm, 1)

                for t in range(NT):
                    if t >= 6:
                        pe.wait_ge(z_done, t - 5)
                    for c in range(DC):
                        last = nc.tensor.matmul(bank[t % 6][0:TP, :], k.XT[:, c, t * TP:(t + 1) * TP], k.WT[:, c, :],
                                                start=c == 0, stop=c == DC - 1)
                    last.then_inc(z_mm, 1)
                    if t >= 2:
                        add_mean(t - 2)
                add_mean(NT - 2)
                add_mean(NT - 1)
                for t in range(NT):
                    pe.wait_ge(squared, t + 1)
                    nc.tensor.matmul(column_var[0:TP, :], k.ONES[0:TP, 0:TP], SQ[:, t % 2, :], start=t == 0,
                                     stop=t == NT - 1).then_inc(var_mm, 1)

                def route(t):
                    pe.wait_ge(nextnorm.taken, t + 1)
                    for c in range(DC):
                        last = nc.tensor.matmul(bank[5][0:TP, t * R1:(t + 1) * R1], k.XT[:, c, t * TP:(t + 1) * TP], k.RW[:, c, :],
                                                start=c == 0, stop=c == DC - 1)
                    last.then_inc(logit_mm, 1)

                pe.wait_ge(k.router_in, 48)
                nextnorm.tensor(nc, k, pe, route)


GROUP = 256


def groups_max(experts, top):
    return N * top // GROUP + experts


class Dispatch:

    def __init__(self, nc, k, ctx, name, experts, top):
        sb = lambda n, s, t: ctx.enter_context(nc.sbuf_tensor(name + n, s, t))
        sem = lambda n: nc.alloc_semaphore(name=name + n)
        self.R, self.K = experts, top
        self.LOWER = sb("LOWER", [TP, experts, experts], F32)
        self.EARLIER = sb("EARLIER", [TP, TP], BF16)
        self.ONE = sb("ONE", [TP, TP], BF16)
        self.SEL16 = sb("SEL16", [TP, NT, experts], BF16)
        self.RANK = sb("RANK", [TP, NT, experts], F32)
        self.SEL = sb("SEL", [TP, NT, experts], F32)
        self.GATE = sb("GATE", [TP, NT, experts], F32)
        self.SLOT = sb("SLOT", [TP, NT, experts], F32)
        self.PICK = sb("PICK", [TP, top, NT, experts], F32)
        self.WORK = sb("WORK", [TP, top, NT, experts], F32)
        self.PAIR = sb("PAIR", [TP, experts, experts], F32)
        self.OVER = sb("OVER", [TP, experts, 4], F32)
        self.TOTAL = sb("TOTAL", [TP, experts], F32)
        self.TAB = sb("TAB", [TP, 3, experts], F32)
        self.TABI = sb("TABI", [1, 3, experts], I32)
        self.AT = sb("AT", [TP, top, NT], F32)
        self.INDEX = sb("INDEX", [TP, top, NT], I32)
        self.WEIGHT = sb("WEIGHT", [TP, top, NT], F32)
        self.lower_done, self.selected, self.counted = sem("lower_done"), sem("selected"), sem("counted")
        self.selected16, self.weighed = sem("selected16"), sem("weighed")
        self.step, self.table_done, self.index_done = sem("step"), sem("table_done"), sem("index_done")

    def gpsimd(self, nc, pool):
        pool.memset(self.LOWER[:, :, :], 1.0).then_inc(self.lower_done, 1)
        pool.memset(self.EARLIER[:, :], 1.0).then_inc(self.lower_done, 1)
        pool.memset(self.ONE[:, :], 1.0).then_inc(self.lower_done, 1)
        pool.wait_ge(self.lower_done, 3)
        pool.affine_select(out=self.LOWER[:, :, :], in_=self.LOWER[:, :, :], compare_op=ALU.is_gt, fill=0.0, base=0,
                           pattern=[[1, self.R], [-1, self.R]], channel_multiplier=0).then_inc(self.lower_done, 1)
        pool.affine_select(out=self.EARLIER[:, :], in_=self.EARLIER[:, :], compare_op=ALU.is_gt, fill=0.0, base=0,
                           pattern=[[1, TP]], channel_multiplier=-1).then_inc(self.lower_done, 1)

    def tensor(self, nc, pe, k, places, totals):
        R = self.R
        pe.wait_ge(self.lower_done, 5)
        pe.wait_ge(self.selected16, 1)
        flat = self.SEL16[:, :, :].rearrange("p t e -> p (t e)")
        nc.tensor.matmul(places[0:TP, 0:NT * R], self.EARLIER[:, :], flat, start=True, stop=False)
        for s in range(1, NT):
            nc.tensor.matmul(places[0:TP, s * R:NT * R], self.ONE[:, :], flat[:, 0:(NT - s) * R], start=False, stop=s == NT - 1)
        for t in range(NT):
            last = nc.tensor.matmul(totals[0:TP, 0:R], self.ONE[:, :], self.SEL16[:, t, :], start=t == 0, stop=t == NT - 1)
        last.then_inc(self.counted, 1)

    def vector(self, nc, dve, places, totals):
        R, K = self.R, self.K
        n = [0]

        def chain(instruction):
            n[0] += 1
            instruction.then_inc(self.step, 1)
            dve.wait_ge(self.step, n[0])

        for r in range(K):
            chain(nc.vector.tensor_scalar(self.PICK[:, r, :, :], self.RANK[:, :, :], float(r), None, ALU.is_equal))
        dve.wait_ge(self.lower_done, 5)
        dve.wait_ge(self.counted, 1)
        chain(nc.vector.tensor_copy(self.TOTAL[:, :], totals[0:TP, 0:R]))
        over_totals = self.TOTAL[:, :].unsqueeze(1).to_broadcast([TP, R, R])
        chain(nc.vector.tensor_tensor(self.PAIR[:, :, :], over_totals, self.LOWER[:, :, :], ALU.mult))
        chain(nc.vector.tensor_reduce(self.TAB[:, 0, :], self.PAIR[:, :, :], AX.X, ALU.add))
        for j in range(4):
            chain(nc.vector.tensor_scalar(self.OVER[:, :, j], self.TOTAL[:, :], GROUP * (j + 1) + 0.5, None, ALU.is_gt))
        chain(nc.vector.tensor_reduce(self.TAB[:, 1, :], self.OVER[:, :, :], AX.X, ALU.add))
        chain(nc.vector.tensor_scalar(self.TAB[:, 1, :], self.TAB[:, 1, :], 1.0, None, ALU.add))
        chain(nc.vector.tensor_tensor(self.PAIR[:, :, :], self.TAB[:, 1, :].unsqueeze(1).to_broadcast([TP, R, R]), self.LOWER[:, :, :], ALU.mult))
        chain(nc.vector.tensor_reduce(self.TAB[:, 2, :], self.PAIR[:, :, :], AX.X, ALU.add))
        nc.vector.tensor_copy(self.TABI[:, :, :], self.TAB[0:1, :, :]).then_inc(self.table_done, 1)
        chain(nc.vector.tensor_tensor(self.SLOT[:, :, :], places[0:TP, 0:NT * R].rearrange("p (t e) -> p t e", e=R),
                                      self.TAB[:, 0, :].unsqueeze(1).to_broadcast([TP, NT, R]), ALU.add))
        work = self.WORK[:, :, :, :].rearrange("p k t e -> p k (t e)")
        pick = self.PICK[:, :, :, :].rearrange("p k t e -> p k (t e)")
        slot = self.SLOT[:, :, :].rearrange("p t e -> p (t e)").unsqueeze(1).to_broadcast([TP, K, NT * R])
        chain(nc.vector.tensor_tensor(work, pick, slot, ALU.mult))
        chain(nc.vector.tensor_reduce(self.AT[:, :, :], self.WORK[:, :, :, :], AX.X, ALU.add))
        nc.vector.tensor_copy(self.INDEX[:, :, :], self.AT[:, :, :]).then_inc(self.index_done, 1)

    def weigh(self, nc, dve):
        work = self.WORK[:, :, :, :].rearrange("p k t e -> p k (t e)")
        pick = self.PICK[:, :, :, :].rearrange("p k t e -> p k (t e)")
        K, R = self.K, self.R
        gate = self.GATE[:, :, :].rearrange("p t e -> p (t e)").unsqueeze(1).to_broadcast([TP, K, NT * R])
        nc.vector.tensor_tensor(work, pick, gate, ALU.mult).then_inc(self.weighed, 1)
        dve.wait_ge(self.weighed, 1)
        nc.vector.tensor_reduce(self.WEIGHT[:, :, :], self.WORK[:, :, :, :], AX.X, ALU.add).then_inc(self.weighed, 1)
        dve.wait_ge(self.weighed, 2)

    def row(self, engine, e):
        return engine.value_load(self.TABI[0:1, 0, bass.ds(e, 1)], min_val=0, max_val=N * self.K)

    def groups(self, engine, e):
        return engine.value_load(self.TABI[0:1, 1, bass.ds(e, 1)], min_val=1, max_val=(N + GROUP - 1) // GROUP)

    def base(self, engine, e):
        return engine.value_load(self.TABI[0:1, 2, bass.ds(e, 1)], min_val=0, max_val=groups_max(self.R, self.K) - 1)


def mixture_stage(nc, k, d):
    ctx = ExitStack()
    sb = lambda n, s, t: ctx.enter_context(nc.sbuf_tensor(n, s, t))
    pb = lambda n, s, t: ctx.enter_context(nc.psum_tensor(n, s, t))
    sem = lambda n: nc.alloc_semaphore(name=n)
    HC = H1 // 128
    SB = GROUP // 128
    BACK = 8
    rows_in = nc.dram_tensor("m_rows_in", (N * TOP1 + 5 * GROUP, D), F32, kind="Internal").ap()
    rows_out = nc.dram_tensor("m_rows_out", (N * TOP1 + 5 * GROUP, D), F32, kind="Internal").ap()
    with ctx:
        W1 = [sb(f"W1_{p}", [128, DC, H1], F32) for p in range(2)]
        W2 = [sb(f"W2_{p}", [128, HC, D], F32) for p in range(2)]
        B1 = [sb(f"B1_{p}", [128, HC], F32) for p in range(2)]
        SLOTS = sb("SLOTS", [128, SB, D], F32)
        SLOTST = sb("SLOTST", [128, DC, GROUP], F32)
        HID = sb("HID", [128, HC, GROUP], F32)
        OUT = sb("OUT", [128, SB, D], F32)
        RES = sb("RES", [TP, BACK, D], F32)
        ZERO = sb("ZERO", [128, D], F32)
        LG = k.LG
        GT = sb("GT", [R1, N], F32)
        COL = sb("COL", [TP, 3, NT], F32)
        BEAT = sb("BEAT", [TP, NT, R1, R1], F32)
        D1 = Dispatch(nc, k, ctx, "m_", R1, TOP1)
        bank = [pb(f"mbank{i}", [128, 512], F32) for i in range(8)]
        ybank, tbank, hbank = bank[0:4], bank[4:6], bank[6:8]
        nextnorm = NextNorm(sem, "a", bank[0:4])
        w_ready = [sem(f"w_ready{p}") for p in range(2)]
        zero_done, pad_in = sem("zero_done"), sem("pad_in")
        vstep, shifted, exped, gates = sem("m_vstep"), sem("shifted"), sem("exped"), sem("gates")
        gates_turned, gates_copied, bias_mm, bias_added = sem("gates_turned"), sem("gates_copied"), sem("bias_mm"), sem("bias_added")
        sent, slots_in = sem("m_sent"), sem("slots_in")
        slots_turned, slots_copied, hid_mm, hid_done = sem("slots_turned"), sem("slots_copied"), sem("hid_mm"), sem("hid_done")
        y_mm, y_copied, out_stored, pool_passed = sem("y_mm"), sem("y_copied"), sem("out_stored"), sem("m_pool_passed")
        passed, compared = sem("m_passed"), sem("m_compared")
        back_in = [sem(f"back_in{i}") for i in range(BACK)]
        back_added = sem("back_added")
        w1v = d["w1"].rearrange("e (c p) h -> e p c h", p=128)
        w2v = d["w2"].rearrange("e (c p) f -> e p c f", p=128)

        with nc.Block() as block:
            @block.sync
            def _(sp):
                load_qkv(sp, k, d, 0)
                sp.wait_ge(zero_done, 1)
                for s in range(SB):
                    sp.dma_start(rows_in[N * TOP1 + 128 * s:N * TOP1 + 128 * (s + 1), :], ZERO[:, :]).then_inc(pad_in, 16)
                sp.wait_ge(pad_in, 16 * SB)

                sp.wait_ge(D1.table_done, 1)
                sp.wait_ge(sent, 16 * TOP1 * NT)
                with sp.Fori(0, R1) as e:
                    row, groups, base = D1.row(sp, e), D1.groups(sp, e), D1.base(sp, e)
                    with sp.Fori(0, groups) as j:
                        sp.wait_ge(slots_turned, base + j + 1)
                        sp.dma_start(SLOTS[:, :, :], rows_in[bass.ds(row + GROUP * j, GROUP), :].rearrange("(s p) c -> p s c", p=128)).then_inc(slots_in, 16)
                last_base, last_groups = D1.base(sp, R1 - 1), D1.groups(sp, R1 - 1)
                sp.wait_ge(slots_turned, last_base + last_groups + 1)
                sp.dma_start(SLOTS[:, :, :], rows_in[0:GROUP, :].rearrange("(s p) c -> p s c", p=128)).then_inc(slots_in, 16)
                sp.wait_ge(slots_turned, last_base + last_groups + 2)
                sp.sem_inc(passed, 1)

            @block.gpsimd
            def _(pool):
                pool.memset(ZERO[:, :], 0.0).then_inc(zero_done, 1)

                def load_weights(e, p):
                    pool.dma_start(B1[p][:, :], d["b1"][bass.ds(e, 1)].rearrange("o (p c) -> p (o c)", p=128)).then_inc(w_ready[p], 16)
                    pool.dma_start(W1[p][:, :, :], w1v[bass.ds(e, 1)].rearrange("o p c h -> p (o c) h")).then_inc(w_ready[p], 16)
                    pool.dma_start(W2[p][:, :, :], w2v[bass.ds(e, 1)].rearrange("o p c f -> p (o c) f")).then_inc(w_ready[p], 16)

                load_weights(0, 0)
                load_weights(1, 1)
                D1.gpsimd(nc, pool)
                pool.wait_ge(D1.index_done, 1)
                for t in range(NT):
                    for r in range(TOP1):
                        pool.indirect_dma_start(rows_in[0:N * TOP1, :], bass.IndirectOffsetOnAxis(D1.INDEX[:, r, t:t + 1], 0),
                                                k.XN[:, t, :], None).then_inc(sent, 16)
                with pool.Fori(1, R1 // 2) as u:
                    for p in range(2):
                        done = D1.base(pool, 2 * u + p - 1)
                        pool.wait_ge(y_mm, SB * done + SB)
                        pool.sem_inc(pool_passed, 1)
                        load_weights(2 * u + p, p)
                last_base, last_groups = D1.base(pool, R1 - 1), D1.groups(pool, R1 - 1)
                pool.wait_ge(out_stored, 16 * (last_base + last_groups) + 16)
                pool.sem_inc(pool_passed, 1)
                for n in range(NT * TOP1):
                    t, r = divmod(n, TOP1)
                    if n >= BACK:
                        pool.wait_ge(back_added, n - BACK + 1)
                    pool.indirect_dma_start(RES[:, n % BACK, :], None, rows_out[0:N * TOP1, :],
                                            bass.IndirectOffsetOnAxis(D1.INDEX[:, r, t:t + 1], 0)).then_inc(back_in[n % BACK], 16)

            @block.vector
            def _(dve):
                dve.sem_inc(vstep, 5)
                for e in range(R1):
                    if e:
                        nc.vector.tensor_tensor(BEAT[:, :, e, 0:e], LG[:, :, 0:e], LG[:, :, e:e + 1].to_broadcast([TP, NT, e]),
                                                ALU.is_ge).then_inc(compared, 1)
                    nc.vector.tensor_tensor(BEAT[:, :, e, e:R1], LG[:, :, e:R1], LG[:, :, e:e + 1].to_broadcast([TP, NT, R1 - e]),
                                            ALU.is_gt).then_inc(compared, 1)
                dve.wait_ge(compared, 2 * R1 - 1)
                nc.vector.tensor_reduce(D1.RANK[:, :, :], BEAT[:, :, :, :], AX.X, ALU.add).then_inc(vstep, 1)
                dve.wait_ge(vstep, 6)
                nc.vector.tensor_scalar(D1.SEL16[:, :, :], D1.RANK[:, :, :], TOP1 - 0.5, None, ALU.is_lt).then_inc(D1.selected16, 1)
                nc.vector.tensor_scalar(D1.SEL[:, :, :], D1.RANK[:, :, :], TOP1 - 0.5, None, ALU.is_lt).then_inc(D1.selected, 1)
                nc.vector.tensor_reduce(COL[:, 0, :], LG[:, :, :], AX.X, ALU.max).then_inc(vstep, 1)
                dve.wait_ge(vstep, 7)
                nc.vector.tensor_tensor(LG[:, :, :], LG[:, :, :], COL[:, 0, :].unsqueeze(2).to_broadcast([TP, NT, R1]),
                                        ALU.subtract).then_inc(shifted, 1)
                D1.vector(nc, dve, tbank[0], tbank[1])
                dve.wait_ge(exped, 1)
                dve.wait_ge(D1.selected, 1)
                nc.vector.tensor_tensor(D1.GATE[:, :, :], D1.GATE[:, :, :], D1.SEL[:, :, :], ALU.mult).then_inc(vstep, 1)
                dve.wait_ge(vstep, 8)
                nc.vector.tensor_reduce(COL[:, 1, :], D1.GATE[:, :, :], AX.X, ALU.add).then_inc(vstep, 1)
                dve.wait_ge(vstep, 9)
                nc.vector.reciprocal(COL[:, 2, :], COL[:, 1, :]).then_inc(vstep, 1)
                dve.wait_ge(vstep, 10)
                nc.vector.tensor_tensor(D1.GATE[:, :, :], D1.GATE[:, :, :], COL[:, 2, :].unsqueeze(2).to_broadcast([TP, NT, R1]),
                                        ALU.mult).then_inc(gates, 1)
                dve.wait_ge(gates, 1)
                D1.weigh(nc, dve)
                for t in range(NT):
                    dve.wait_ge(bias_mm, t + 1)
                    nc.vector.tensor_tensor(k.X[:, t, :], k.X[:, t, :], ybank[t % 4][0:TP, :], ALU.add).then_inc(bias_added, 1)
                dve.wait_ge(bias_added, NT)
                dve.sem_inc(y_copied, SB)
                with dve.Fori(0, R1) as e:
                    groups, base = D1.groups(dve, e), D1.base(dve, e)
                    with dve.Fori(base, base + groups) as g:
                        dve.wait_ge(out_stored, 16 * g + 16)
                        for s in range(SB):
                            dve.wait_ge(y_mm, SB * g + SB + s + 1)
                            nc.vector.tensor_copy(OUT[:, s, :], ybank[s][:, :]).then_inc(y_copied, 1)
                for n in range(NT * TOP1):
                    t, r = divmod(n, TOP1)
                    dve.wait_ge(back_in[n % BACK], 16 * (n // BACK + 1))
                    if n:
                        dve.wait_ge(back_added, n)
                    nc.vector.scalar_tensor_tensor(out=k.X[:, t, :], in0=RES[:, n % BACK, :], scalar=D1.WEIGHT[:, r, t:t + 1],
                                                   in1=k.X[:, t, :], op0=ALU.mult, op1=ALU.add).then_inc(back_added, 1)
                    if r == TOP1 - 1:
                        dve.wait_ge(back_added, n + 1)
                        nextnorm.vector(nc, k, dve, t)
                nextnorm.vector(nc, k, dve, NT)

            @block.scalar
            def _(act):
                act.wait_ge(shifted, 1)
                nc.scalar.activation(D1.GATE[:, :, :], LG[:, :, :], ACT.Exp).then_inc(exped, 1)
                for g, (t0, n) in enumerate(GROUPS):
                    act.wait_ge(gates_turned, g + 1)
                    nc.scalar.activation(GT[:, t0 * TP:(t0 + n) * TP], (hbank + ybank[3:4])[g][0:R1, 0:n * TP], ACT.Copy).then_inc(gates_copied, 1)
                act.wait_ge(D1.table_done, 1)

                def copy_slots(g):
                    act.wait_ge(slots_turned, g + 2)
                    for s in range(SB):
                        nc.scalar.activation(SLOTST[:, :, s * 128:(s + 1) * 128], tbank[s][:, :].rearrange("p (c n) -> p c n", n=128),
                                             ACT.Copy).then_inc(slots_copied, 1)

                act.sem_inc(out_stored, 16)
                copy_slots(0)
                with act.Fori(0, R1 // 2) as u:
                    for p in range(2):
                        row, groups, base = D1.row(act, 2 * u + p), D1.groups(act, 2 * u + p), D1.base(act, 2 * u + p)
                        act.wait_ge(w_ready[p], 48 * u + 48)
                        with act.Fori(0, groups) as j:
                            g = base + j
                            for h in range(HC):
                                act.wait_ge(hid_mm, HC * g + h + 1)
                                nc.scalar.activation(HID[:, h, :], hbank[h][:, 0:GROUP], ACT.Relu, bias=B1[p][:, h:h + 1]).then_inc(hid_done, 1)
                            copy_slots(g + 1)
                            act.wait_ge(y_copied, SB * g + 2 * SB)
                            act.dma_start(rows_out[bass.ds(row + GROUP * j, GROUP), :].rearrange("(s p) c -> p s c", p=128), OUT[:, :, :]).then_inc(out_stored, 16)
                nextnorm.scalar(nc, k, act)

            @block.tensor
            def _(pe):
                D1.tensor(nc, pe, k, tbank[0], tbank[1])
                pe.wait_ge(gates, 1)
                for g, (t0, n) in enumerate(GROUPS):
                    for t in range(n):
                        last = nc.tensor.transpose((hbank + ybank[3:4])[g][0:R1, t * TP:(t + 1) * TP], D1.GATE[:, t0 + t, :], k.IDENT[0:TP, 0:TP])
                    last.then_inc(gates_turned, 1)
                pe.wait_ge(gates_copied, 3)
                for t in range(NT):
                    if t >= 4:
                        pe.wait_ge(bias_added, t - 3)
                    nc.tensor.matmul(ybank[t % 4][0:TP, :], GT[:, t * TP:(t + 1) * TP], k.B2[:, :], start=True, stop=True).then_inc(bias_mm, 1)
                pe.wait_ge(bias_added, NT)
                pe.wait_ge(D1.table_done, 1)
                pe.sem_inc(slots_turned, 1)
                pe.sem_inc(y_mm, SB)

                def turn_slots(g):
                    pe.wait_ge(slots_in, 16 * g + 16)
                    for s in range(SB):
                        for c in range(DC):
                            last = nc.tensor.transpose(tbank[s][:, c * 128:(c + 1) * 128], SLOTS[:, s, c * 128:(c + 1) * 128], k.IDENT[:, :])
                    last.then_inc(slots_turned, 1)

                turn_slots(0)
                with pe.Fori(0, R1 // 2) as u:
                    for p in range(2):
                        groups, base = D1.groups(pe, 2 * u + p), D1.base(pe, 2 * u + p)
                        with pe.Fori(base, base + groups) as g:
                            pe.wait_ge(w_ready[p], 48 * u + 48)
                            pe.wait_ge(slots_copied, SB * g + SB)
                            for h in range(HC):
                                for c in range(DC):
                                    last = nc.tensor.matmul(hbank[h][:, 0:GROUP], W1[p][:, c, h * 128:(h + 1) * 128], SLOTST[:, c, :],
                                                            start=c == 0, stop=c == DC - 1)
                                last.then_inc(hid_mm, 1)
                            turn_slots(g + 1)
                            pe.wait_ge(hid_done, HC * g + HC)
                            for s in range(SB):
                                pe.wait_ge(y_copied, SB * g + s + 1)
                                for h in range(HC):
                                    last = nc.tensor.matmul(ybank[s][:, :], HID[:, h, s * 128:(s + 1) * 128], W2[p][:, h, :],
                                                            start=h == 0, stop=h == HC - 1)
                                last.then_inc(y_mm, 1)
                nextnorm.tensor(nc, k, pe)


def load_qkv(sp, k, d, i):
    for j in range(3):
        sp.dma_start(k.WQKV[:, j, :, :], d["qkv_w"].rearrange("(c p) f -> p c f", p=128)[:, :, bass.ds(128 * i + D * j, 128)]).then_inc(k.wqkv_in, 16)


def attention_stage(nc, k, d):
    ctx = ExitStack()
    sb = lambda n, s, t: ctx.enter_context(nc.sbuf_tensor(n, s, t))
    pb = lambda n, s, t: ctx.enter_context(nc.psum_tensor(n, s, t))
    sem = lambda n: nc.alloc_semaphore(name=n)
    PAIRS = HEADS // 2
    UNITS = 2 * NT
    SCALE = 1.0 / float(np.sqrt(DK))
    WIDE = 96
    with ctx:
        WFF = sb("WFF", [128, D], F32)
        BQK = sb("BQK", [128, 2], F32)
        BV = sb("BV", [TP, 128], F32)
        BFF = sb("BFF", [TP, D], F32)
        Q = [sb(f"Q{h}", [128, N], F32R) for h in range(2)]
        KHIGH = [sb(f"KHIGH{h}", [128, N], F32R) for h in range(2)]
        KLOW = [sb(f"KLOW{h}", [128, N], F32R) for h in range(2)]
        own = [slice(0, DK), slice(DK, 2 * DK)]
        other = [slice(DK, 2 * DK), slice(0, DK)]
        V = sb("V", [TP, NT, 128], F32)
        MASKED = [sb(f"MASKED{p}", [TP, N], F32) for p in range(2)]
        PROB = [sb(f"PROB{p}", [TP, N], F32) for p in range(3)]
        PROBT = [sb(f"PROBT{p}", [TP, NT, TP], F32) for p in range(2)]
        MSG = sb("MSG", [TP, NT, 2, DK], F32)
        MSGT = sb("MSGT", [128, N], F32)
        TOP = sb("TOP", [TP, UNITS], F32)
        SHIFT = sb("SHIFT", [TP, UNITS], F32)
        DEN = sb("DEN", [TP, 2, NT], F32)
        score = pb("score", [128, 1536], F32)
        turn = pb("turn", [128, 3, 512], F32)
        out_bank = [pb(f"out_bank{p}", [128, 512], F32) for p in range(2)]
        wff_in, bff_in, bff_added = sem("wff_in"), sem("bff_in"), sem("bff_added")
        proj_mm, v_done = sem("proj_mm"), sem("v_done")
        q_high, q_low, k_high, k_low = sem("q_high"), sem("q_low"), sem("k_high"), sem("k_low")
        scores_seen = sem("scores_seen")
        score_mm, masked, shift_done, exp_done, weighted = sem("score_mm"), sem("masked"), sem("shift_done"), sem("exp_done"), sem("weighted")
        prob_turned, prob_copied, msg_mm, msg_copied = sem("prob_turned"), sem("prob_copied"), sem("msg_mm"), sem("msg_copied")
        den_floored, den_inverted, msg_turned, msgt_copied = sem("den_floored"), sem("den_inverted"), sem("msg_turned"), sem("msgt_copied")
        ff_mm, ff_added = sem("ff_mm"), sem("ff_added")
        bank = lambda i: score[:, 512 * i:512 * (i + 1)] if i < 3 else turn[:, i - 3, :]

        with nc.Block() as block:
            @block.sync
            def _(sp):
                def load_rest(i):
                    sp.dma_start(BQK[:, :], d["qk_b"][bass.ds(i, 1)].rearrange("o (p j) -> p (o j)", p=128)).then_inc(wff_in, 16)
                    sp.dma_start(BV[:, :], d["v_b"][bass.ds(i, 1)].to_broadcast([TP, 128])).then_inc(wff_in, 16)
                    sp.dma_start(WFF[:, :], d["ff_w"][bass.ds(128 * i, 128), :]).then_inc(wff_in, 16)

                load_rest(0)
                sp.dma_start(BFF[:, :], d["ff_b"].rearrange("(a n) -> a n", a=1).to_broadcast([TP, D])).then_inc(bff_in, 16)
                with sp.Fori(1, PAIRS) as i:
                    sp.wait_ge(proj_mm, 9 * i + 9)
                    load_qkv(sp, k, d, i)
                    sp.wait_ge(ff_mm, NT * i + NT)
                    load_rest(i)

            @block.gpsimd
            def _(pool):
                pool.wait_ge(bff_in, 16)
                for t in range(NT):
                    pool.tensor_tensor(k.X[:, t, :], k.X[:, t, :], BFF[:, :], ALU.add).then_inc(bff_added, 1)

            @block.vector
            def _(dve):
                dve.sem_inc(ff_added, 3)
                with dve.Fori(0, PAIRS) as i:
                    dve.wait_ge(wff_in, 48 * i + 48)
                    for g, (c0, w) in enumerate(SPANS):
                        for h in range(2):
                            dve.wait_ge(q_high, 6 * i + 2 * g + h + 1)
                            nc.vector.scalar_tensor_tensor(out=Q[h][other[h], c0:c0 + w], in0=bank(g)[own[h], 0:w], scalar=BQK[own[h], 0:1],
                                                           in1=Q[h][own[h], c0:c0 + w], op0=ALU.add, op1=ALU.subtract).then_inc(q_low, 1)
                    for g, (c0, w) in enumerate(SPANS):
                        for h in range(2):
                            dve.wait_ge(k_high, 12 * i + 4 * g + h + 3)
                            for half in (own[h], other[h]):
                                nc.vector.scalar_tensor_tensor(out=KLOW[h][half, c0:c0 + w], in0=bank(3 + g)[own[h], 0:w], scalar=BQK[own[h], 1:2],
                                                               in1=KHIGH[h][own[h], c0:c0 + w], op0=ALU.add, op1=ALU.subtract).then_inc(k_low, 1)

                    def add_v_bias(g):
                        t0, n = GROUPS[g]
                        dve.wait_ge(proj_mm, 9 * i + 9 + 6 + g + 1)
                        nc.vector.tensor_tensor(V[:, t0:t0 + n, :], out_bank[g % 2][0:TP, 0:128 * n].rearrange("p (t c) -> p t c", c=128),
                                                BV[:, :].unsqueeze(1).to_broadcast([TP, n, 128]), ALU.add).then_inc(v_done, 1)

                    add_v_bias(0)
                    for s in range(UNITS + 4):
                        if s < UNITS:
                            u, t = s, s % NT
                            dve.wait_ge(score_mm, UNITS * i + u + 1)
                            if u >= 2:
                                dve.wait_ge(exp_done, UNITS * i + u - 1)
                            dve.sem_inc(scores_seen, 1)
                            nc.vector.tensor_tensor_reduce(out=five(MASKED[u % 2][:, :]), in0=blocks5(score[0:TP, 0:1280]),
                                                           in1=five(k.M[:, t, :]), scale=1.0, scalar=3.0 * NEG, op0=ALU.add, op1=ALU.max,
                                                           accum_out=TOP[:, u:u + 1]).then_inc(masked, 1)
                            dve.wait_ge(masked, UNITS * i + u + 1)
                            nc.vector.tensor_scalar(SHIFT[:, u:u + 1], TOP[:, u:u + 1], -SCALE, None, ALU.mult).then_inc(shift_done, 1)
                        if s < 2:
                            add_v_bias(s + 1)
                        if 1 <= s <= UNITS:
                            u = s - 1
                            h, t = divmod(u, NT)
                            dve.wait_ge(exp_done, UNITS * i + u + 1)
                            nc.vector.tensor_tensor_reduce(out=PROB[u % 3][:, :], in0=PROB[u % 3][:, :], in1=k.A16[:, t, :], scale=1.0,
                                                           scalar=0.0, op0=ALU.mult, op1=ALU.add,
                                                           accum_out=DEN[:, h, t:t + 1]).then_inc(weighted, 1)
                        if 2 <= s < UNITS + 2:
                            u = s - 2
                            h, t = divmod(u, NT)
                            dve.wait_ge(weighted, UNITS * i + u + 1)
                            nc.vector.tensor_scalar(DEN[:, h, t:t + 1], DEN[:, h, t:t + 1], 1e-30, None, ALU.max).then_inc(den_floored, 1)
                        if 3 <= s < UNITS + 3:
                            u = s - 3
                            h, t = divmod(u, NT)
                            dve.wait_ge(den_floored, UNITS * i + u + 1)
                            nc.vector.reciprocal(DEN[:, h, t:t + 1], DEN[:, h, t:t + 1]).then_inc(den_inverted, 1)
                        if s >= 4:
                            u = s - 4
                            h, t = divmod(u, NT)
                            dve.wait_ge(den_inverted, UNITS * i + u + 1)
                            dve.wait_ge(msg_mm, UNITS * i + u + 1)
                            nc.vector.tensor_scalar(MSG[:, t, h, :], out_bank[u % 2][0:TP, (WIDE - DK) * h:(WIDE - DK) * h + DK],
                                                    DEN[:, h, t:t + 1], None, ALU.mult).then_inc(msg_copied, 1)
                    dve.wait_ge(bff_added, NT)
                    for t in range(NT):
                        dve.wait_ge(ff_mm, NT * i + NT + t + 1)
                        nc.vector.tensor_tensor(k.X[:, t, :], k.X[:, t, :], bank(t % 3)[0:TP, :], ALU.add).then_inc(ff_added, 1)
                    dve.wait_ge(ff_added, NT * i + NT + 3)

            @block.scalar
            def _(act):
                with act.Fori(0, PAIRS) as i:
                    act.wait_ge(wff_in, 48 * i + 48)
                    for g, (c0, w) in enumerate(SPANS):
                        act.wait_ge(proj_mm, 9 * i + 9 + g + 1)
                        for h in range(2):
                            nc.scalar.activation(Q[h][own[h], c0:c0 + w], bank(g)[own[h], 0:w], ACT.Identity,
                                                 bias=BQK[own[h], 0:1]).then_inc(q_high, 1)
                    for g, (c0, w) in enumerate(SPANS):
                        act.wait_ge(proj_mm, 9 * i + 9 + 3 + g + 1)
                        for half in (own, other):
                            for h in range(2):
                                nc.scalar.activation(KHIGH[h][half[h], c0:c0 + w], bank(3 + g)[own[h], 0:w], ACT.Identity,
                                                     bias=BQK[own[h], 1:2]).then_inc(k_high, 1)
                    for s in range(UNITS + 2):
                        if s < UNITS:
                            u = s
                            act.wait_ge(shift_done, UNITS * i + u + 1)
                            if u >= 3:
                                act.wait_ge(prob_turned, 3 * (UNITS * i + u - 2))
                            nc.scalar.activation(PROB[u % 3][:, :], MASKED[u % 2][:, :], ACT.Exp, bias=SHIFT[:, u:u + 1],
                                                 scale=SCALE).then_inc(exp_done, 1)
                        if s >= 2:
                            u = s - 2
                            if u >= 2:
                                act.wait_ge(msg_mm, UNITS * i + u - 1)
                            for g, (t0, n) in enumerate(GROUPS):
                                act.wait_ge(prob_turned, 3 * (UNITS * i + u) + g + 1)
                                nc.scalar.activation(PROBT[u % 2][:, t0:t0 + n, :], turn[0:TP, g, 0:n * TP].rearrange("p (t n) -> p t n", n=TP),
                                                     ACT.Copy).then_inc(prob_copied, 1)
                    for g, (t0, n) in enumerate(GROUPS):
                        act.wait_ge(msg_turned, 3 * i + g + 1)
                        nc.scalar.activation(MSGT[:, t0 * TP:(t0 + n) * TP], turn[:, g, 0:n * TP], ACT.Copy).then_inc(msgt_copied, 1)

            @block.tensor
            def _(pe):
                pe.sem_inc(proj_mm, 9)
                pe.sem_inc(ff_mm, NT)
                with pe.Fori(0, PAIRS) as i:
                    pe.wait_ge(k.wqkv_in, 48 * i + 48)
                    pe.wait_ge(ff_added, NT * i + 3)
                    for j in range(2):
                        for g, (c0, w) in enumerate(SPANS):
                            for c in range(DC):
                                last = nc.tensor.matmul(bank(3 * j + g)[:, 0:w], k.WQKV[:, j, c, :], k.XT[:, c, c0:c0 + w],
                                                        start=c == 0, stop=c == DC - 1)
                            last.then_inc(proj_mm, 1)

                    def project_v(g):
                        t0, n = GROUPS[g]
                        if g == 2:
                            pe.wait_ge(v_done, 3 * i + 1)
                        for t in range(n):
                            for c in range(DC):
                                last = nc.tensor.matmul(out_bank[g % 2][0:TP, 128 * t:128 * (t + 1)], k.XT[:, c, (t0 + t) * TP:(t0 + t + 1) * TP],
                                                        k.WQKV[:, 2, c, :], start=c == 0, stop=c == DC - 1)
                        last.then_inc(proj_mm, 1)

                    project_v(0)
                    for s in range(UNITS + 3):
                        if s < UNITS:
                            u = s
                            h, t = divmod(u, NT)
                            if u == 0:
                                pe.wait_ge(k_high, 12 * i + 12)
                                pe.wait_ge(k_low, 12 * i + 12)
                            else:
                                pe.wait_ge(masked, UNITS * i + u)
                            for c0, w in SPANS:
                                col = c0 * 256 // 250
                                for part, K in enumerate((KHIGH, KLOW)):
                                    last = nc.tensor.matmul(blocks5(score[0:TP, col:col + w * 256 // 250]), Q[h][:, t * TP:(t + 1) * TP],
                                                            five(K[h][:, c0:c0 + w]), start=part == 0, stop=part == 1)
                            last.then_inc(score_mm, 1)
                        if s < 2:
                            project_v(s + 1)
                        if 2 <= s < UNITS + 2:
                            u = s - 2
                            pe.wait_ge(weighted, UNITS * i + u + 1)
                            for g, (t0, n) in enumerate(GROUPS):
                                if u:
                                    pe.wait_ge(prob_copied, 3 * (UNITS * i + u - 1) + g + 1)
                                for t in range(n):
                                    last = nc.tensor.transpose(turn[0:TP, g, t * TP:(t + 1) * TP],
                                                               PROB[u % 3][:, (t0 + t) * TP:(t0 + t + 1) * TP], k.IDENT[0:TP, 0:TP])
                                last.then_inc(prob_turned, 1)
                        if s >= 3:
                            u = s - 3
                            h, t = divmod(u, NT)
                            pe.wait_ge(prob_copied, 3 * (UNITS * i + u) + 3)
                            if u >= 2:
                                pe.wait_ge(msg_copied, UNITS * i + u - 1)
                            if u == 0:
                                pe.wait_ge(v_done, 3 * i + 3)
                            for q in range(NT):
                                last = nc.tensor.matmul(out_bank[u % 2][0:TP, 0:WIDE], PROBT[u % 2][:, q, :],
                                                        V[:, q, (128 - WIDE) * h:(128 - WIDE) * h + WIDE], start=q == 0, stop=q == NT - 1)
                            last.then_inc(msg_mm, 1)
                    for g, (t0, n) in enumerate(GROUPS):
                        pe.wait_ge(msg_copied, UNITS * i + NT + t0 + n)
                        for t in range(n):
                            last = nc.tensor.transpose(turn[:, g, t * TP:(t + 1) * TP],
                                                       MSG[:, t0 + t, :, :].rearrange("p h c -> p (h c)"), k.IDENT[0:TP, 0:TP])
                        last.then_inc(msg_turned, 1)
                    pe.wait_ge(wff_in, 48 * i + 48)
                    for t in range(NT):
                        if t % 4 == 0:
                            pe.wait_ge(msgt_copied, 3 * i + t // 4 + 1)
                        if t >= 3:
                            pe.wait_ge(ff_added, NT * i + t - 2 + 3)
                        nc.tensor.matmul(bank(t % 3)[0:TP, :], MSGT[:, t * TP:(t + 1) * TP], WFF[:, :], start=True, stop=True).then_inc(ff_mm, 1)
                pe.wait_ge(ff_added, NT * PAIRS + 3)


def feedforward_stage(nc, k, d):
    ctx = ExitStack()
    sb = lambda n, s, t: ctx.enter_context(nc.sbuf_tensor(n, s, t))
    pb = lambda n, s, t: ctx.enter_context(nc.psum_tensor(n, s, t))
    sem = lambda n: nc.alloc_semaphore(name=n)
    HC = H2 // 128
    HALF = H2 // 512
    GE = G2 + R2
    SB = GROUP // 128
    BACK = 8
    RING = 3
    rows_in = nc.dram_tensor("f_rows_in", (N * TOP2 + 5 * GROUP, H2), F32, kind="Internal").ap()
    rows_out = nc.dram_tensor("f_rows_out", (N * TOP2 + 5 * GROUP, D), F32, kind="Internal").ap()
    with ctx:
        with ExitStack() as first:
            fsb = lambda n, s, t: first.enter_context(nc.sbuf_tensor(n, s, t))
            XT = fsb("XT2", [128, DC, N], F32)
            XHIGH = fsb("XHIGH", [128, DC, N], F32R)
            HID = fsb("HID2", [128, HC, N], F32)
            WSHARED = fsb("WSHARED", [128, HC, D], F32)
            WIN = [fsb(f"WIN{p}", [128, 2, DC, 128], F32) for p in range(2)]
        XN = HID[0:TP, :, :].rearrange("p c n -> p (c n)")[:, 0:NT * D].rearrange("p (t c) -> p t c", c=D)
        with ExitStack() as low:
            XLOW = low.enter_context(nc.sbuf_tensor("XLOW", [128, DC, N], F32R))
        with ExitStack() as second:
            ssb = lambda n, s, t: second.enter_context(nc.sbuf_tensor(n, s, t))
            WHIGH, WLOW = [None, None], [None, None]
            WHIGH[0], WLOW[0] = ssb("WHIGH0", [128, HC, D], F32R), ssb("WLOW0", [128, HC, D], F32R)
            SHIGH = ssb("SHIGH", [128, HC, GROUP], F32R)
            WHIGH[1], WLOW[1] = ssb("WHIGH1", [128, HC, D], F32R), ssb("WLOW1", [128, HC, D], F32R)
            SLOW = ssb("SLOW", [128, HC, GROUP], F32R)
        ctx.enter_context(nc.sbuf_tensor("both", [128, 2 * NT * D + HC * N + HC * D + 16 * 128], F32))
        WRAW = sb("WRAW", [128, HC, D], F32)
        HIDN = sb("HIDN", [TP, RING, H2], F32)
        SILU = [sb(f"SILU{p}", [128, 512], F32) for p in range(2)]
        with ExitStack() as chunk:
            WINHIGH = [chunk.enter_context(nc.sbuf_tensor(f"WINHIGH{p}", [128, 2, DC, 128], F32R)) for p in range(2)]
            WINLOW = [chunk.enter_context(nc.sbuf_tensor(f"WINLOW{p}", [128, 2, DC, 128], F32R)) for p in range(2)]
        LATE = sb("LATE", [128, 9216], F32)
        WEX = LATE[:, 0:2 * H2 * DC].rearrange("p (c f) -> p c f", c=DC)
        SLOTS = LATE[:, 0:SB * H2].rearrange("p (s f) -> p s f", s=SB)
        OUT = LATE[:, 4096:4096 + SB * D].rearrange("p (s f) -> p s f", s=SB)
        RES = LATE[0:TP, 5120:5120 + BACK * D].rearrange("p (b f) -> p b f", b=BACK)
        ROW = sb("ROW2", [TP, 3, D], F32)
        GW = sb("GW", [128, DC, GE], F32)
        GB = sb("GB", [TP, GE], F32)
        EB = sb("EB", [R2, D], F32)
        LG = sb("LG2", [TP, NT, GE], F32)
        BEST = sb("BEST", [TP, 2, NT], F32)
        P4 = sb("P4", [TP, 4, NT, EG2], F32)
        COL = sb("COL2", [TP, 3, NT], F32)
        RANK = sb("RANK2", [TP, NT, EG2], F32)
        BEAT = sb("BEAT2", [TP, 2, NT, EG2 * EG2], F32)
        LOWER = sb("LOWER2", [TP, EG2, EG2], F32)
        CT = LATE[0:R2, 5120:5120 + N]
        D2 = Dispatch(nc, k, ctx, "f_", R2, TOP2)
        bank = [pb(f"fbank{i}", [128, 512], F32) for i in range(8)]
        norm, norm2 = norm_semaphores(sem, "f"), norm_semaphores(sem, "f2")
        rows1, scaled_rows, rows_done = sem("f_rows1"), sem("f_scaled"), sem("f_rows_done")
        turned, taken = sem("f_turned"), sem("f_taken")
        small_in, lower_done, compared, logit_mm, zero_done, pad_in = sem("f_small_in"), sem("f_lower"), sem("f_compared"), sem("f_logit_mm"), sem("f_zero"), sem("f_pad_in")
        win_in = [sem(f"win_in{p}") for p in range(2)]
        shared_in, w_high, w_low = sem("shared_in"), sem("w_high"), sem("w_low")
        raw_in = [sem(f"raw_in{h}") for h in range(2)]
        wex_in = [sem(f"wex_in{h}") for h in range(HALF)]
        vs, exped, shared_bias = sem("f_vs"), sem("f_exped"), sem("shared_bias")
        cnt_turned, cnt_copied = sem("cnt_turned"), sem("cnt_copied")
        ex_mm, ex_silu, ex_done = sem("ex_mm"), sem("ex_silu"), sem("ex_done")
        sent = [sem(f"f_sent{i}") for i in range(RING)]
        x_high, x_low, win_high, win_low = sem("x_high"), sem("x_low"), sem("win_high"), sem("win_low")
        in_mm, silu_done, hid_done, shared_mm, shared_added = sem("in_mm"), sem("silu_done"), sem("f_hid_done"), sem("shared_mm"), sem("shared_added")
        slots_in = [sem(f"f_slots_in{s}") for s in range(SB)]
        slots_turned = [sem(f"f_slots_turned{s}") for s in range(SB)]
        slots_high, slots_low = [sem(f"f_slots_high{s}") for s in range(SB)], [sem(f"f_slots_low{s}") for s in range(SB)]
        y_mm, y_copied, out_stored, passed = sem("f_y_mm"), sem("f_y_copied"), sem("f_out_stored"), sem("f_passed")
        back_in = [sem(f"f_back_in{i}") for i in range(BACK)]
        back_added, stored = sem("f_back_added"), sem("stored")
        half = lambda h: slice(HC // 2 * h, HC // 2 * (h + 1))
        winv = d["in_w"].rearrange("w (c p) (s j q) -> w j p s c q", p=128, s=2, q=128)
        woutv = d["out_w"].rearrange("e (j p) f -> e p j f", p=128)

        with nc.Block() as block:
            @block.sync
            def _(sp):
                for j, row in enumerate((d["ln_scale"], d["ln_bias"], d["shared_out_b"])):
                    sp.dma_start(ROW[:, j, :], row.rearrange("(a n) -> a n", a=1).to_broadcast([TP, D])).then_inc(small_in, 16)
                sp.dma_start(GW[:, :, :], d["gate_w"].rearrange("(c p) e -> p c e", p=128)).then_inc(small_in, 16)
                sp.dma_start(GB[:, :], d["gate_b"].rearrange("(a n) -> a n", a=1).to_broadcast([TP, GE])).then_inc(small_in, 16)
                sp.dma_start(EB[:, :], d["expert_out_b"]).then_inc(small_in, 16)
                for h in range(HALF):
                    for q in range(2):
                        c0 = H2 * q + 512 * h
                        sp.dma_start(WEX[:, :, c0:c0 + 512], d["in_w"][1, :, c0:c0 + 512].rearrange("(c p) f -> p c f", p=128)).then_inc(wex_in[h], 16)
                sp.wait_ge(zero_done, 1)
                for s in range(SB):
                    sp.dma_start(rows_in[N * TOP2 + 128 * s:N * TOP2 + 128 * (s + 1), :], HID[:, HC - 1, 0:H2]).then_inc(pad_in, 16)
                for j in range(HC):
                    if j >= 2:
                        sp.wait_ge(win_high, j - 1)
                        sp.wait_ge(win_low, j - 1)
                    for s in range(2):
                        sp.dma_start(WIN[j % 2][:, s, :, :], winv[0, j, :, s]).then_inc(win_in[j % 2], 16)
                sp.wait_ge(pad_in, 16 * SB)
                sp.wait_ge(D2.table_done, 1)
                for i in range(RING):
                    sp.wait_ge(sent[i], 16 * TOP2 * len(range(i, NT, RING)))
                sp.wait_ge(in_mm, 6 * HC)
                with sp.Fori(0, R2) as e:
                    row, groups, base = D2.row(sp, e), D2.groups(sp, e), D2.base(sp, e)
                    with sp.Fori(0, groups) as j:
                        for s in range(SB):
                            sp.wait_ge(slots_turned[s], base + j + 1)
                            sp.dma_start(SLOTS[:, s, :], rows_in[bass.ds(row + GROUP * j + 128 * s, 128), :]).then_inc(slots_in[s], 16)
                last_base, last_groups = D2.base(sp, R2 - 1), D2.groups(sp, R2 - 1)
                for s in range(SB):
                    sp.wait_ge(slots_turned[s], last_base + last_groups + 1)
                    sp.dma_start(SLOTS[:, s, :], rows_in[0:128, :]).then_inc(slots_in[s], 16)
                sp.wait_ge(slots_turned[SB - 1], last_base + last_groups + 2)
                sp.sem_inc(passed, 1)
                for t in range(NT):
                    sp.wait_ge(back_added, TOP2 * (t + 1))
                    sp.dma_start(d["out"][t * TP:(t + 1) * TP, :], k.X[:, t, :]).then_inc(stored, 16)
                sp.wait_ge(stored, 16 * NT)

            @block.gpsimd
            def _(pool):
                pool.memset(HID[:, HC - 1, 0:H2], 0.0).then_inc(zero_done, 1)
                pool.memset(LOWER[:, :, :], 1.0).then_inc(lower_done, 1)
                pool.wait_ge(lower_done, 1)
                pool.affine_select(out=LOWER[:, :, :], in_=LOWER[:, :, :], compare_op=ALU.is_gt, fill=0.0, base=0,
                                   pattern=[[1, EG2], [-1, EG2]], channel_multiplier=0).then_inc(lower_done, 1)
                D2.gpsimd(nc, pool)
                pool.wait_ge(small_in, 96)
                for t in range(NT):
                    pool.wait_ge(rows1, t + 1)
                    pool.tensor_tensor(k.X[:, t, :], k.X[:, t, :], ROW[:, 2, :], ALU.add).then_inc(shared_bias, 1)
                for h in range(HALF):
                    pool.wait_ge(wex_in[h], 32)
                pool.dma_start(WSHARED[:, :, :], woutv[0]).then_inc(shared_in, 16)
                for h in range(2):
                    pool.dma_start(WRAW[:, half(h), :], woutv[1][:, half(h), :]).then_inc(raw_in[h], 16)
                pool.wait_ge(D2.index_done, 1)
                for t in range(NT):
                    pool.wait_ge(ex_done, HALF * (t + 1))
                    for r in range(TOP2):
                        pool.indirect_dma_start(rows_in[0:N * TOP2, :], bass.IndirectOffsetOnAxis(D2.INDEX[:, r, t:t + 1], 0),
                                                HIDN[:, t % RING, :], None).then_inc(sent[t % RING], 16)
                with pool.Fori(1, R2) as e:
                    for h in range(2):
                        pool.wait_ge(w_low, 2 * e - 1 + h)
                        pool.sem_inc(passed, 1)
                        pool.dma_start(WRAW[:, half(h), :], woutv[bass.ds(e + 1, 1), :, half(h), :].rearrange("o p j f -> p (o j) f")).then_inc(raw_in[h], 16)
                for h in range(2):
                    pool.wait_ge(w_low, 2 * R2 - 1 + h)
                    pool.dma_start(WRAW[:, half(h), :], woutv[R2][:, half(h), :]).then_inc(raw_in[h], 16)
                last_base, last_groups = D2.base(pool, R2 - 1), D2.groups(pool, R2 - 1)
                pool.wait_ge(out_stored, 16 * (last_base + last_groups) + 16)
                pool.sem_inc(passed, 1)
                for n in range(NT * TOP2):
                    t, r = divmod(n, TOP2)
                    if n >= BACK:
                        pool.wait_ge(back_added, n - BACK + 1)
                    pool.indirect_dma_start(RES[:, n % BACK, :], None, rows_out[0:N * TOP2, :],
                                            bass.IndirectOffsetOnAxis(D2.INDEX[:, r, t:t + 1], 0)).then_inc(back_in[n % BACK], 16)

            @block.vector
            def _(dve):
                def expert_rows(m):
                    t, h = divmod(m, HALF)
                    if t >= RING and h == 0:
                        dve.wait_ge(sent[t % RING], 16 * TOP2 * (t // RING))
                    dve.wait_ge(ex_silu, m + 1)
                    dve.wait_ge(ex_mm, 2 * m + 2)
                    nc.vector.tensor_tensor(HIDN[:, t % RING, 512 * h:512 * (h + 1)], SILU[m % 2][0:TP, :], bank[2 * (m % 3) + 1][0:TP, :],
                                            ALU.mult).then_inc(ex_done, 1)
                    if h == HALF - 1:
                        dve.wait_ge(x_high, t + 1)
                        nc.vector.tensor_tensor(XLOW[:, :, t * TP:(t + 1) * TP], XT[:, :, t * TP:(t + 1) * TP],
                                                XHIGH[:, :, t * TP:(t + 1) * TP], ALU.subtract).then_inc(x_low, 1)

                for s in range(NT + 2):
                    if s < NT:
                        t = s
                        nc.vector.bn_stats(k.STATS[:, t, :], k.X[:, t, :]).then_inc(norm.stats, 1)
                        dve.wait_ge(norm.stats, t + 1)
                        nc.vector.bn_aggr(k.MV[:, t, :], k.STATS[:, t, :]).then_inc(norm.moments, 1)
                    if 1 <= s <= NT:
                        t = s - 1
                        dve.wait_ge(norm.std, t + 1)
                        nc.vector.reciprocal(k.RSTD[:, t:t + 1], k.STD[:, t:t + 1]).then_inc(norm.rstd, 1)
                        dve.wait_ge(norm.rstd, t + 1)
                        nc.vector.tensor_scalar(XN[:, t, :], k.X[:, t, :], k.MV[:, t, 0:1], k.RSTD[:, t:t + 1],
                                                ALU.subtract, ALU.mult).then_inc(rows1, 1)
                        dve.wait_ge(rows1, t + 1)
                        nc.vector.bn_stats(k.STATS[:, t, :], XN[:, t, :]).then_inc(norm2.stats, 1)
                        dve.wait_ge(norm2.stats, t + 1)
                        nc.vector.bn_aggr(k.MV[:, t, :], k.STATS[:, t, :]).then_inc(norm2.moments, 1)
                    if s >= 2:
                        t = s - 2
                        if t == 0:
                            dve.wait_ge(small_in, 96)
                        dve.wait_ge(norm2.std, t + 1)
                        nc.vector.reciprocal(k.RSTD[:, t:t + 1], k.STD[:, t:t + 1]).then_inc(norm2.rstd, 1)
                        nc.vector.scalar_tensor_tensor(out=XN[:, t, :], in0=XN[:, t, :], scalar=k.MV[:, t, 0:1], in1=ROW[:, 0, :],
                                                       op0=ALU.subtract, op1=ALU.mult).then_inc(scaled_rows, 1)
                        dve.wait_ge(norm2.rstd, t + 1)
                        dve.wait_ge(scaled_rows, t + 1)
                        nc.vector.scalar_tensor_tensor(out=XN[:, t, :], in0=XN[:, t, :], scalar=k.RSTD[:, t:t + 1], in1=ROW[:, 1, :],
                                                       op0=ALU.mult, op1=ALU.add).then_inc(rows_done, 1)
                for m in range(3):
                    expert_rows(m)
                n = [0]

                def chain(instruction):
                    n[0] += 1
                    instruction.then_inc(vs, 1)
                    dve.wait_ge(vs, n[0])

                dve.wait_ge(logit_mm, NT)
                chain(nc.vector.tensor_tensor(LG[:, :, :], bank[7][0:TP, 0:NT * GE].rearrange("p (t e) -> p t e", e=GE),
                                              GB[:, :].unsqueeze(1).to_broadcast([TP, NT, GE]), ALU.add))
                chain(nc.vector.tensor_tensor(BEST[:, 1, :], LG[:, :, 1], LG[:, :, 0], ALU.is_gt))
                chain(nc.vector.tensor_scalar(BEST[:, 0, :], BEST[:, 1, :], -1.0, 1.0, ALU.mult, ALU.add))
                for g in range(2):
                    chain(nc.vector.tensor_tensor(P4[:, g, :, :], LG[:, :, G2 + EG2 * g:G2 + EG2 * (g + 1)],
                                                  BEST[:, g, :].unsqueeze(2).to_broadcast([TP, NT, EG2]), ALU.mult))
                chain(nc.vector.tensor_tensor(P4[:, 2, :, :], P4[:, 0, :, :], P4[:, 1, :, :], ALU.add))
                chain(nc.vector.tensor_reduce(COL[:, 0, :], P4[:, 2, :, :], AX.X, ALU.max))
                chain(nc.vector.tensor_tensor(P4[:, 0, :, :], P4[:, 2, :, :], COL[:, 0, :].unsqueeze(2).to_broadcast([TP, NT, EG2]), ALU.subtract))
                dve.wait_ge(exped, 1)
                chain(nc.vector.tensor_reduce(COL[:, 0, :], P4[:, 1, :, :], AX.X, ALU.add))
                chain(nc.vector.reciprocal(COL[:, 1, :], COL[:, 0, :]))
                chain(nc.vector.tensor_tensor(P4[:, 2, :, :], P4[:, 1, :, :], COL[:, 1, :].unsqueeze(2).to_broadcast([TP, NT, EG2]), ALU.mult))
                dve.wait_ge(lower_done, 2)
                mine = P4[:, 2, :, :].unsqueeze(3).to_broadcast([TP, NT, EG2, EG2])
                other = P4[:, 2, :, :].unsqueeze(2).to_broadcast([TP, NT, EG2, EG2])
                nc.vector.tensor_tensor(BEAT[:, 0, :, :].rearrange("p t (i j) -> p t i j", j=EG2), other, mine, ALU.is_gt).then_inc(compared, 1)
                nc.vector.tensor_tensor(BEAT[:, 1, :, :].rearrange("p t (i j) -> p t i j", j=EG2), other, mine, ALU.is_equal).then_inc(compared, 1)
                dve.wait_ge(compared, 2)
                chain(nc.vector.tensor_tensor(BEAT[:, 1, :, :], BEAT[:, 1, :, :],
                                              LOWER[:, :, :].rearrange("p i j -> p (i j)").unsqueeze(1).to_broadcast([TP, NT, EG2 * EG2]), ALU.mult))
                chain(nc.vector.tensor_tensor(BEAT[:, 0, :, :], BEAT[:, 0, :, :], BEAT[:, 1, :, :], ALU.add))
                chain(nc.vector.tensor_reduce(RANK[:, :, :], BEAT[:, 0, :, :].rearrange("p t (i j) -> p t i j", j=EG2), AX.X, ALU.add))
                chain(nc.vector.tensor_scalar(COL[:, 0:2, :], BEST[:, :, :], float(-EG2), float(EG2), ALU.mult, ALU.add))
                for g in range(2):
                    chain(nc.vector.tensor_tensor(D2.RANK[:, :, EG2 * g:EG2 * (g + 1)], RANK[:, :, :],
                                                  COL[:, g, :].unsqueeze(2).to_broadcast([TP, NT, EG2]), ALU.add))
                nc.vector.tensor_scalar(D2.SEL16[:, :, :], D2.RANK[:, :, :], TOP2 - 0.5, None, ALU.is_lt).then_inc(D2.selected16, 1)
                nc.vector.tensor_scalar(D2.SEL[:, :, :], D2.RANK[:, :, :], TOP2 - 0.5, None, ALU.is_lt).then_inc(D2.selected, 1)
                chain(nc.vector.tensor_scalar(RANK[:, :, :], RANK[:, :, :], TOP2 - 0.5, None, ALU.is_lt))
                chain(nc.vector.tensor_tensor(P4[:, 0, :, :], P4[:, 2, :, :], RANK[:, :, :], ALU.mult))
                chain(nc.vector.tensor_reduce(COL[:, 0, :], P4[:, 0, :, :], AX.X, ALU.add))
                chain(nc.vector.tensor_scalar(COL[:, 1, :], COL[:, 0, :], 1e-8, None, ALU.add))
                chain(nc.vector.reciprocal(COL[:, 2, :], COL[:, 1, :]))
                chain(nc.vector.tensor_tensor(P4[:, 3, :, :], P4[:, 0, :, :], COL[:, 2, :].unsqueeze(2).to_broadcast([TP, NT, EG2]), ALU.mult))
                for g in range(2):
                    chain(nc.vector.tensor_tensor(D2.GATE[:, :, EG2 * g:EG2 * (g + 1)], P4[:, 3, :, :],
                                                  BEST[:, g, :].unsqueeze(2).to_broadcast([TP, NT, EG2]), ALU.mult))

                D2.vector(nc, dve, bank[6], bank[7])
                D2.weigh(nc, dve)
                for m in range(3, HALF * NT):
                    expert_rows(m)
                def chunk_low(j):
                    dve.wait_ge(win_high, j + 1)
                    nc.vector.tensor_tensor(WINLOW[j % 2][:, :, :, :], WIN[j % 2][:, :, :, :], WINHIGH[j % 2][:, :, :, :],
                                            ALU.subtract).then_inc(win_low, 1)

                chunk_low(0)
                m = 0
                for j in range(HC):
                    for c0, w in SPANS:
                        dve.wait_ge(silu_done, m + 1)
                        dve.wait_ge(in_mm, 2 * m + 2)
                        nc.vector.tensor_tensor(HID[:, j, c0:c0 + w], SILU[m % 2][:, 0:w], bank[2 * (m % 2) + 1][:, 0:w], ALU.mult).then_inc(hid_done, 1)
                        m += 1
                        if c0 == 0 and j + 1 < HC:
                            chunk_low(j + 1)
                def weights_low(p, done):
                    for h in range(2):
                        dve.wait_ge(w_high, 2 * done - 1 + h)
                        nc.vector.tensor_tensor(WLOW[p][:, half(h), :], WRAW[:, half(h), :], WHIGH[p][:, half(h), :], ALU.subtract).then_inc(w_low, 1)

                def slots_low_part(g, s):
                    dve.wait_ge(slots_high[s], g + 2)
                    for q in range(2):
                        last = nc.vector.tensor_tensor(SLOW[:, 4 * q:4 * q + 4, s * 128:(s + 1) * 128], bank[2 * s + q][:, :].rearrange("p (c n) -> p c n", n=128),
                                                       SHIGH[:, 4 * q:4 * q + 4, s * 128:(s + 1) * 128], ALU.subtract)
                    last.then_inc(slots_low[s], 1)

                weights_low(0, 1)
                dve.wait_ge(shared_bias, NT)
                for t in range(NT):
                    dve.wait_ge(shared_mm, t + 1)
                    nc.vector.tensor_tensor(k.X[:, t, :], k.X[:, t, :], bank[4 + t % 4][0:TP, :], ALU.add).then_inc(shared_added, 1)
                for s in range(SB):
                    slots_low_part(0, s)
                dve.sem_inc(y_copied, SB)
                with dve.Fori(0, R2 // 2) as u:
                    for p in range(2):
                        groups, base = D2.groups(dve, 2 * u + p), D2.base(dve, 2 * u + p)
                        weights_low(1 - p, 2 * u + p + 2)
                        with dve.Fori(base, base + groups) as g:
                            dve.wait_ge(out_stored, 16 * g + 16)
                            for s in range(SB):
                                dve.wait_ge(y_mm, SB * g + SB + s + 1)
                                nc.vector.tensor_copy(OUT[:, s, :], bank[4 + s][:, :]).then_inc(y_copied, 1)
                                slots_low_part(g + 1, s)
                dve.wait_ge(shared_added, NT)
                for n in range(NT * TOP2):
                    t, r = divmod(n, TOP2)
                    dve.wait_ge(back_in[n % BACK], 16 * (n // BACK + 1))
                    if n:
                        dve.wait_ge(back_added, n)
                    nc.vector.scalar_tensor_tensor(out=k.X[:, t, :], in0=RES[:, n % BACK, :], scalar=D2.WEIGHT[:, r, t:t + 1],
                                                   in1=k.X[:, t, :], op0=ALU.mult, op1=ALU.add).then_inc(back_added, 1)

            @block.scalar
            def _(act):
                for s in range(NT + 3):
                    if s < NT:
                        act.wait_ge(norm.moments, s + 1)
                        nc.scalar.activation(k.STD[:, s:s + 1], k.MV[:, s, 1:2], ACT.Sqrt, bias=k.EPSC[0:TP, 0:1]).then_inc(norm.std, 1)
                    if 1 <= s <= NT:
                        act.wait_ge(norm2.moments, s)
                        nc.scalar.activation(k.STD[:, s - 1:s], k.MV[:, s - 1, 1:2], ACT.Sqrt, bias=k.EPSC[0:TP, 0:1]).then_inc(norm2.std, 1)
                    if s >= 3:
                        t = s - 3
                        act.wait_ge(turned, t + 1)
                        nc.scalar.activation(XT[:, :, t * TP:(t + 1) * TP],
                                             bank[6][:, 0:DC * TP].rearrange("p (c n) -> p c n", n=TP), ACT.Copy).then_inc(taken, 1)
                for m in range(HALF * NT):
                    if m == 3:
                        act.wait_ge(vs, 8)
                        nc.scalar.activation(P4[:, 1, :, :], P4[:, 0, :, :], ACT.Exp).then_inc(exped, 1)
                    act.wait_ge(ex_mm, 2 * m + 1)
                    if m >= 2:
                        act.wait_ge(ex_done, m - 1)
                    nc.scalar.activation(SILU[m % 2][0:TP, :], bank[2 * (m % 3)][0:TP, :], ACT.Silu).then_inc(ex_silu, 1)
                    if m % HALF == HALF - 1:
                        t = m // HALF
                        act.wait_ge(ex_mm, 2 * m + 2)
                        nc.scalar.activation(XHIGH[:, :, t * TP:(t + 1) * TP], XT[:, :, t * TP:(t + 1) * TP], ACT.Copy).then_inc(x_high, 1)
                def chunk_high(j):
                    act.wait_ge(win_in[j % 2], 32 * (j // 2 + 1))
                    nc.scalar.activation(WINHIGH[j % 2][:, :, :, :], WIN[j % 2][:, :, :, :], ACT.Copy).then_inc(win_high, 1)

                act.wait_ge(ex_mm, 2 * HALF * NT)
                chunk_high(0)
                for m in range(3 * HC):
                    w = SPANS[m % 3][1]
                    act.wait_ge(in_mm, 2 * m + 1)
                    if m >= 2:
                        act.wait_ge(hid_done, m - 1)
                    else:
                        act.wait_ge(ex_done, HALF * NT)
                    nc.scalar.activation(SILU[m % 2][:, 0:w], bank[2 * (m % 2)][:, 0:w], ACT.Silu).then_inc(silu_done, 1)
                    if m % 3 == 0 and m // 3 + 1 < HC:
                        chunk_high(m // 3 + 1)
                for g, (t0, n) in enumerate(GROUPS):
                    act.wait_ge(cnt_turned, g + 1)
                    nc.scalar.activation(CT[:, t0 * TP:(t0 + n) * TP], bank[g][0:R2, 0:n * TP], ACT.Copy).then_inc(cnt_copied, 1)

                def weights_high(p, loaded):
                    for h in range(2):
                        act.wait_ge(raw_in[h], 16 * loaded)
                        nc.scalar.activation(WHIGH[p][:, half(h), :], WRAW[:, half(h), :], ACT.Copy).then_inc(w_high, 1)

                def slots_high_part(g, s):
                    act.wait_ge(slots_turned[s], g + 2)
                    for q in range(2):
                        last = nc.scalar.activation(SHIGH[:, 4 * q:4 * q + 4, s * 128:(s + 1) * 128],
                                                    bank[2 * s + q][:, :].rearrange("p (c n) -> p c n", n=128), ACT.Copy)
                    last.then_inc(slots_high[s], 1)

                weights_high(0, 1)
                act.sem_inc(out_stored, 16)
                for s in range(SB):
                    act.sem_inc(slots_high[s], 1)
                    slots_high_part(0, s)
                with act.Fori(0, R2 // 2) as u:
                    for p in range(2):
                        row, groups, base = D2.row(act, 2 * u + p), D2.groups(act, 2 * u + p), D2.base(act, 2 * u + p)
                        act.wait_ge(y_mm, SB * base + SB)
                        weights_high(1 - p, 2 * u + p + 2)
                        with act.Fori(0, groups) as j:
                            g = base + j
                            for s in range(SB):
                                slots_high_part(g + 1, s)
                            act.wait_ge(y_copied, SB * g + 2 * SB)
                            act.dma_start(rows_out[bass.ds(row + GROUP * j, GROUP), :].rearrange("(s p) c -> p s c", p=128), OUT[:, :, :]).then_inc(out_stored, 16)

            @block.tensor
            def _(pe):
                def turn(t):
                    pe.wait_ge(rows_done, t + 1)
                    if t:
                        pe.wait_ge(taken, t)
                    for c in range(DC):
                        last = nc.tensor.transpose(bank[6][:, c * TP:(c + 1) * TP], XN[:, t, c * 128:(c + 1) * 128], k.IDENT[0:TP, 0:TP])
                    last.then_inc(turned, 1)

                def expert_rows(m):
                    t, h = divmod(m, HALF)
                    pe.wait_ge(taken, t + 1)
                    pe.wait_ge(wex_in[h], 32)
                    if m >= 3:
                        pe.wait_ge(ex_done, m - 2)
                    for s in range(2):
                        for c in range(DC):
                            last = nc.tensor.matmul(bank[2 * (m % 3) + s][0:TP, :], XT[:, c, t * TP:(t + 1) * TP],
                                                    WEX[:, c, H2 * s + 512 * h:H2 * s + 512 * (h + 1)], start=c == 0, stop=c == DC - 1)
                        last.then_inc(ex_mm, 1)

                def gate(t):
                    pe.wait_ge(taken, t + 1)
                    for c in range(DC):
                        last = nc.tensor.matmul(bank[7][0:TP, t * GE:(t + 1) * GE], XT[:, c, t * TP:(t + 1) * TP], GW[:, c, :],
                                                start=c == 0, stop=c == DC - 1)
                    last.then_inc(logit_mm, 1)

                pe.wait_ge(small_in, 96)
                turn(0)
                for m, tiles in enumerate((range(1, 3), range(3, 6), range(6, NT))):
                    expert_rows(m)
                    for t in tiles:
                        turn(t)
                        gate(t - 1)
                gate(NT - 1)
                for m in range(3, HALF * NT):
                    if m == 5:
                        D2.tensor(nc, pe, k, bank[6], bank[7])
                    expert_rows(m)
                pe.wait_ge(ex_done, HALF * NT)
                pe.wait_ge(zero_done, 1)
                m = 0
                for j in range(HC):
                    pe.wait_ge(win_high, j + 1)
                    pe.wait_ge(win_low, j + 1)
                    if j == 0:
                        pe.wait_ge(x_high, NT)
                        pe.wait_ge(x_low, NT)
                    for c0, w in SPANS:
                        if m >= 2:
                            pe.wait_ge(hid_done, m - 1)
                        for s in range(2):
                            for part, (W, T) in enumerate(((WINHIGH, XHIGH), (WINHIGH, XLOW), (WINLOW, XHIGH))):
                                for c in range(DC):
                                    last = nc.tensor.matmul(bank[2 * (m % 2) + s][:, 0:w], W[j % 2][:, s, c, :], T[:, c, c0:c0 + w],
                                                            start=part == 0 and c == 0, stop=part == 2 and c == DC - 1)
                            last.then_inc(in_mm, 1)
                        m += 1
                pe.wait_ge(shared_in, 16)
                pe.wait_ge(hid_done, 3 * HC)
                for g, (t0, n) in enumerate(GROUPS):
                    for t in range(n):
                        last = nc.tensor.transpose(bank[g][0:R2, t * TP:(t + 1) * TP], D2.SEL[:, t0 + t, :], k.IDENT[0:TP, 0:TP])
                    last.then_inc(cnt_turned, 1)
                pe.wait_ge(cnt_copied, 3)
                for t in range(NT):
                    if t >= 4:
                        pe.wait_ge(shared_added, t - 3)
                    for j in range(HC):
                        nc.tensor.matmul(bank[4 + t % 4][0:TP, :], HID[:, j, t * TP:(t + 1) * TP], WSHARED[:, j, :], start=j == 0, stop=False)
                    nc.tensor.matmul(bank[4 + t % 4][0:TP, :], CT[:, t * TP:(t + 1) * TP], EB[:, :], start=False, stop=True).then_inc(shared_mm, 1)
                for s in range(SB):
                    pe.sem_inc(slots_turned[s], 1)
                pe.sem_inc(y_mm, SB)
                pe.wait_ge(shared_added, NT)
                pe.wait_ge(D2.table_done, 1)

                def turn_slots(g, s):
                    pe.wait_ge(slots_in[s], 16 * g + 16)
                    for c in range(HC):
                        last = nc.tensor.transpose(bank[2 * s + c // 4][:, (c % 4) * 128:(c % 4 + 1) * 128], SLOTS[:, s, c * 128:(c + 1) * 128],
                                                   k.IDENT[:, :])
                    last.then_inc(slots_turned[s], 1)

                for s in range(SB):
                    turn_slots(0, s)
                with pe.Fori(0, R2 // 2) as u:
                    for p in range(2):
                        groups, base = D2.groups(pe, 2 * u + p), D2.base(pe, 2 * u + p)
                        with pe.Fori(base, base + groups) as g:
                            pe.wait_ge(w_high, 4 * u + 2 * p + 2)
                            pe.wait_ge(w_low, 4 * u + 2 * p + 2)
                            for s in range(SB):
                                pe.wait_ge(slots_high[s], g + 2)
                                pe.wait_ge(slots_low[s], g + 1)
                                pe.wait_ge(y_copied, SB * g + s + 1)
                                for part, (rows, weights) in enumerate(((SHIGH, WHIGH[p]), (SHIGH, WLOW[p]), (SLOW, WHIGH[p]))):
                                    for j in range(HC):
                                        last = nc.tensor.matmul(bank[4 + s][:, :], rows[:, j, s * 128:(s + 1) * 128], weights[:, j, :],
                                                                start=part == 0 and j == 0, stop=part == 2 and j == HC - 1)
                                last.then_inc(y_mm, 1)
                                turn_slots(g + 1, s)


def program(nc, d):
    with ExitStack() as ctx:
        sb = lambda n, s, t: ctx.enter_context(nc.sbuf_tensor(n, s, t))
        k = OnChip()
        k.X = sb("X", [TP, NT, D], F32)
        k.IDENT = sb("IDENT", [128, 128], F32)
        k.ONES = sb("ONES", [128, 128], F32)
        k.EPSC = sb("EPSC", [128, 1], F32)
        k.STATS = sb("STATS", [TP, NT, 6], F32)
        k.MV = sb("MV", [TP, NT, 2], F32)
        k.STD = sb("STD", [TP, NT], F32)
        k.RSTD = sb("RSTD", [TP, NT], F32)
        k.x_in = ctx.enter_context(nc.semaphore("x_in"))
        k.wqkv_in = ctx.enter_context(nc.semaphore("wqkv_in"))
        k.router_in = ctx.enter_context(nc.semaphore("router_in"))
        k.gnn_w_in = ctx.enter_context(nc.semaphore("gnn_w_in"))
        with ExitStack() as graph:
            k.XN = graph.enter_context(nc.sbuf_tensor("XN", [TP, NT, D], F32))
            k.XT = graph.enter_context(nc.sbuf_tensor("XT", [128, DC, N], F32))
            k.A16 = graph.enter_context(nc.sbuf_tensor("A16", [TP, NT, N], U16))
            k.M = graph.enter_context(nc.sbuf_tensor("M", [TP, NT, N], BF16))
            k.RW = graph.enter_context(nc.sbuf_tensor("RW", [128, DC, R1], F32))
            k.RB = graph.enter_context(nc.sbuf_tensor("RB", [TP, R1], F32))
            k.LG = graph.enter_context(nc.sbuf_tensor("LG", [TP, NT, R1], F32))
            k.B2 = graph.enter_context(nc.sbuf_tensor("B2", [R1, D], F32))
            with ExitStack() as gnn:
                k.AT = gnn.enter_context(nc.sbuf_tensor("AT", [TP, NT, N], F32))
                k.WT = gnn.enter_context(nc.sbuf_tensor("WT", [128, DC, D], F32))
                k.ROWS = gnn.enter_context(nc.sbuf_tensor("ROWS", [TP, 3, D], F32))
                before = nc.snapshot_sems()
                adjacency_stage(nc, k, d)
                graph_stage(nc, k, d)
                nc.clear_and_free_semaphores(nc.allocated_since(before))
                nc.all_engine_barrier()
            k.WQKV = graph.enter_context(nc.sbuf_tensor("WQKV", [128, 3, DC, 128], F32))
            mixture_stage(nc, k, d)
            attention_stage(nc, k, d)
        feedforward_stage(nc, k, d)


def layout(nc, inputs):
    arrays = {
        "x": inputs["x"], "src": inputs["src"], "dst": inputs["dst"],
        "gnn_w": inputs["L0_gnn_W"].T, "gnn_b": inputs["L0_gnn_b"],
        "gnn_gamma": inputs["L0_gnn_gamma"], "gnn_beta": inputs["L0_gnn_beta"],
        "router_w": inputs["L0_ffn_router_w"], "router_b": inputs["L0_ffn_router_b"],
        "w1": inputs["L0_ffn_w1"], "b1": inputs["L0_ffn_b1"].reshape(R1, H1 // 128, 128).transpose(0, 2, 1).reshape(R1, H1),
        "w2": inputs["L0_ffn_w2"], "b2": inputs["L0_ffn_b2"],
    }
    bqkv = inputs["L1_gnn_b_qkv"].reshape(3, HEADS // 2, 128)
    arrays |= {
        "qkv_w": inputs["L1_gnn_W_qkv"].T, "ff_w": inputs["L1_gnn_W_ff"].T, "ff_b": inputs["L1_gnn_b_ff"],
        "qk_b": bqkv[0:2].transpose(1, 2, 0).reshape(HEADS // 2, 256), "v_b": bqkv[2],
    }
    rows = lambda w: w.T[None]
    arrays |= {
        "in_w": np.concatenate([rows(inputs["L1_ffn_shared_in_w"]), rows(inputs["L1_ffn_expert_in_w"])]),
        "out_w": np.concatenate([rows(inputs["L1_ffn_shared_out_w"]), inputs["L1_ffn_expert_out_weight"].transpose(0, 2, 1)]),
        "gate_w": np.concatenate([inputs["L1_ffn_group_gate_w"], inputs["L1_ffn_expert_gate_w"]]).T,
        "gate_b": np.concatenate([inputs["L1_ffn_group_bias"], inputs["L1_ffn_expert_bias"]]),
        "shared_out_b": inputs["L1_ffn_shared_out_b"], "expert_out_b": inputs["L1_ffn_expert_out_bias"],
        "ln_scale": inputs["L1_ffn_ln_scale"], "ln_bias": inputs["L1_ffn_ln_bias"],
    }
    d = {}
    for name, a in arrays.items():
        arrays[name] = a = np.ascontiguousarray(a)
        d[name] = nc.dram_tensor(name, a.shape, mybir.dt.from_np(a.dtype), kind="ExternalInput").ap()
    d["out"] = nc.dram_tensor("out", (N, D), F32, kind="ExternalOutput").ap()
    return arrays, d


def kernel(**inputs):
    import numpy as _np
    import concourse.bacc as _bacc
    from concourse.bass_utils import run_bass_kernel_spmd as _run

    nc = _bacc.Bacc("TRN2", target_bir_lowering=False, num_devices=1)
    arrays, d = layout(nc, {name: _np.asarray(a) for name, a in inputs.items()})
    program(nc, d)
    r = _run(nc, [arrays], core_ids=[0])
    return r.results[0]["out"]
```
